# Optimizing a Trainium2 kernel written in Bass

```python
import numpy as np
import jax
import jax.numpy as jnp

def _softmax(x, axis=-1):
    return jax.nn.softmax(x, axis=axis)

def _gelu(x):
    return jax.nn.gelu(x, approximate=True)

def _silu(x):
    return jax.nn.silu(x)

def _sigmoid(x):
    return jax.nn.sigmoid(x)

def _layernorm(x, axis=-1, eps=1e-05):
    m = jnp.mean(x, axis=axis, keepdims=True)
    v = jnp.var(x, axis=axis, keepdims=True)
    return (x - m) / jnp.sqrt(v + eps)

def _scatter_add(tgt, idx, src, axis=0):
    return tgt.at[idx].add(src)

def _segment_sum(src, seg, n):
    return jax.ops.segment_sum(src, seg, n)
kernel_name = 'mk_xattn_ffn_d2_seqx_r4_1fb8e3'

def setup_inputs(seed: int=0):
    np.random.seed(seed)
    _w = jnp.asarray

    def _rec_inputs():
        import jax
        import jax.numpy as jnp
        _rk = jax.random.key(seed)
        x = 7.22e-05 + 1 * jax.random.normal(jax.random.fold_in(_rk, 1), (2, 1024, 256), jnp.float32)
        _lenS = 1024 - jax.random.randint(jax.random.fold_in(_rk, 7), (2,), 0, max(1, 1024 // 4) + 1, jnp.int32)
        _lenS2 = 64 - jax.random.randint(jax.random.fold_in(_rk, 8), (2,), 0, max(1, 64 // 4) + 1, jnp.int32)
        _ctx_1024P = jax.random.normal(jax.random.fold_in(_rk, 11), (2, 16, 256), jnp.float32)
        _ctx_1024c = jax.random.dirichlet(jax.random.fold_in(_rk, 511), 0.3 * jnp.ones((16,), jnp.float32), (2, 64))
        _ctx_1024t = jnp.einsum('bsk,bkd->bsd', _ctx_1024c, _ctx_1024P)
        _ctx_1024t = _ctx_1024t * jax.lax.rsqrt(jnp.mean(jnp.square(_ctx_1024t)) + 1e-12) * 0.953939
        ctx_1024 = 4.13588e-05 + 0.999923 * (_ctx_1024t + 0.3 * jax.random.normal(jax.random.fold_in(_rk, 611), (2, 64, 256), jnp.float32))
        return (x, ctx_1024)
    x, ctx_1024 = _rec_inputs()

    def _L0_xattn_setup():
        import jax, jax.numpy as jnp
        import numpy as np
        D_MODEL = 256
        NUM_HEADS = 16
        D_K = D_MODEL // NUM_HEADS
        B, S = (4, 512)
        key = jax.random.key(seed)
        ks = jax.random.split(key, 11)
        scale = 1.0 / np.sqrt(D_MODEL)
        inp = {'query': jax.random.normal(ks[0], (B, S, D_MODEL), dtype=jnp.float32), 'key': jax.random.normal(ks[1], (B, S, D_MODEL), dtype=jnp.float32), 'value': jax.random.normal(ks[2], (B, S, D_MODEL), dtype=jnp.float32), 'Wq': jax.random.normal(ks[3], (D_MODEL, D_MODEL), dtype=jnp.float32) * scale, 'bq': jnp.zeros((D_MODEL,), dtype=jnp.float32), 'Wk': jax.random.normal(ks[4], (D_MODEL, D_MODEL), dtype=jnp.float32) * scale, 'bk': jnp.zeros((D_MODEL,), dtype=jnp.float32), 'Wv': jax.random.normal(ks[5], (D_MODEL, D_MODEL), dtype=jnp.float32) * scale, 'bv': jnp.zeros((D_MODEL,), dtype=jnp.float32), 'Wo': jax.random.normal(ks[6], (D_MODEL, D_MODEL), dtype=jnp.float32) * scale, 'bo': jnp.zeros((D_MODEL,), dtype=jnp.float32)}
        return inp
    _L0_xattn_all = _L0_xattn_setup()
    _L0_xattn_in = {k: v for k, v in _L0_xattn_all.items() if k in ('Wq', 'bq', 'Wk', 'bk', 'Wv', 'bv', 'Wo', 'bo')}
    del _L0_xattn_all

    def _L0_ffn_setup():
        import jax, jax.numpy as jnp
        import numpy as np
        DIM, HEADS, FFN, E = (256, 16, 1024, 8)
        B, S = (2, 256)
        EPS = 1e-05

        def _ln(x, g, b):
            mu = jnp.mean(x, axis=-1, keepdims=True)
            var = jnp.mean((x - mu) ** 2, axis=-1, keepdims=True)
            return (x - mu) * jax.lax.rsqrt(var + EPS) * g + b
        key = jax.random.key(seed)
        ks = jax.random.split(key, 20)
        sd = 0.02
        d, f = (DIM, FFN)
        return {'x': jax.random.normal(ks[0], (B, S, d), jnp.float32), 'ln1_g': jnp.ones((d,), jnp.float32), 'ln1_b': jnp.zeros((d,), jnp.float32), 'Wqkv': jax.random.normal(ks[1], (d, 3 * d), jnp.float32) * sd, 'bqkv': jnp.zeros((3 * d,), jnp.float32), 'Wo': jax.random.normal(ks[2], (d, d), jnp.float32) * sd, 'bo': jnp.zeros((d,), jnp.float32), 'ln2_g': jnp.ones((d,), jnp.float32), 'ln2_b': jnp.zeros((d,), jnp.float32), 'gate_w': jax.random.normal(ks[3], (d, E), jnp.float32) * sd, 'W1': jax.random.normal(ks[4], (E, d, f), jnp.float32) * sd, 'b1': jnp.zeros((E, f), jnp.float32), 'W2': jax.random.normal(ks[5], (E, f, d), jnp.float32) * sd, 'b2': jnp.zeros((E, d), jnp.float32), 'rW1': jax.random.normal(ks[6], (d, f), jnp.float32) * sd, 'rb1': jnp.zeros((f,), jnp.float32), 'rW2': jax.random.normal(ks[7], (f, d), jnp.float32) * sd, 'rb2': jnp.zeros((d,), jnp.float32), 'coef_w': jax.random.normal(ks[8], (d, 2), jnp.float32) * sd, 'coef_b': jnp.zeros((2,), jnp.float32)}
    _L0_ffn_all = _L0_ffn_setup()
    _L0_ffn_in = {k: v for k, v in _L0_ffn_all.items() if k in ('ln1_g', 'ln1_b', 'Wqkv', 'bqkv', 'Wo', 'bo', 'ln2_g', 'ln2_b', 'gate_w', 'W1', 'b1', 'W2', 'b2', 'rW1', 'rb1', 'rW2', 'rb2', 'coef_w', 'coef_b')}
    del _L0_ffn_all

    def _L1_xattn_setup():
        import jax, jax.numpy as jnp
        import numpy as np
        D_MODEL = 256
        NUM_HEADS = 16
        HEAD_DIM = D_MODEL // NUM_HEADS
        key = jax.random.key(seed)
        ks = jax.random.split(key, 10)
        B, SQ, SKV = (4, 512, 512)
        s = 1.0 / np.sqrt(D_MODEL)
        return {'query': jax.random.normal(ks[0], (B, SQ, D_MODEL), jnp.float32), 'key_value': jax.random.normal(ks[1], (B, SKV, D_MODEL), jnp.float32), 'Wq': jax.random.normal(ks[2], (D_MODEL, D_MODEL), jnp.float32) * s, 'bq': jnp.zeros((D_MODEL,), jnp.float32), 'Wk': jax.random.normal(ks[3], (D_MODEL, D_MODEL), jnp.float32) * s, 'bk': jnp.zeros((D_MODEL,), jnp.float32), 'Wv': jax.random.normal(ks[4], (D_MODEL, D_MODEL), jnp.float32) * s, 'bv': jnp.zeros((D_MODEL,), jnp.float32), 'Wo': jax.random.normal(ks[5], (D_MODEL, D_MODEL), jnp.float32) * s, 'bo': jnp.zeros((D_MODEL,), jnp.float32)}
    _L1_xattn_all = _L1_xattn_setup()
    _L1_xattn_in = {k: v for k, v in _L1_xattn_all.items() if k in ('Wq', 'bq', 'Wk', 'bk', 'Wv', 'bv', 'Wo', 'bo')}
    del _L1_xattn_all

    def _L1_ffn_setup():
        import jax, jax.numpy as jnp
        import numpy as np
        B, S, D, F, E = (4, 512, 256, 1024, 4)
        key = jax.random.key(seed)
        ks = jax.random.split(key, 8)
        sd = 1.0 / np.sqrt(D)
        sf = 1.0 / np.sqrt(F)
        return {'x': jax.random.normal(ks[0], (B, S, D), dtype=jnp.float32), 'W1': jax.random.uniform(ks[1], (E, D, F), jnp.float32, -sd, sd), 'b1': jax.random.uniform(ks[2], (E, F), jnp.float32, -sd, sd), 'W2': jax.random.uniform(ks[3], (E, F, D), jnp.float32, -sf, sf), 'b2': jax.random.uniform(ks[4], (E, D), jnp.float32, -sf, sf), 'Wu': jax.random.uniform(ks[5], (D, 1), jnp.float32, -sd, sd), 'bu': jax.random.uniform(ks[6], (1,), jnp.float32, -sd, sd)}
    _L1_ffn_all = _L1_ffn_setup()
    _L1_ffn_in = {k: v for k, v in _L1_ffn_all.items() if k in ('W1', 'b1', 'W2', 'b2', 'Wu', 'bu')}
    del _L1_ffn_all
    return {'x': x, 'ctx_1024': ctx_1024, 'L0_xattn_Wq': _L0_xattn_in['Wq'], 'L0_xattn_bq': _L0_xattn_in['bq'], 'L0_xattn_Wk': _L0_xattn_in['Wk'], 'L0_xattn_bk': _L0_xattn_in['bk'], 'L0_xattn_Wv': _L0_xattn_in['Wv'], 'L0_xattn_bv': _L0_xattn_in['bv'], 'L0_xattn_Wo': _L0_xattn_in['Wo'], 'L0_xattn_bo': _L0_xattn_in['bo'], 'L0_ffn_ln1_g': _L0_ffn_in['ln1_g'], 'L0_ffn_ln1_b': _L0_ffn_in['ln1_b'], 'L0_ffn_Wqkv': _L0_ffn_in['Wqkv'], 'L0_ffn_bqkv': _L0_ffn_in['bqkv'], 'L0_ffn_Wo': _L0_ffn_in['Wo'], 'L0_ffn_bo': _L0_ffn_in['bo'], 'L0_ffn_ln2_g': _L0_ffn_in['ln2_g'], 'L0_ffn_ln2_b': _L0_ffn_in['ln2_b'], 'L0_ffn_gate_w': _L0_ffn_in['gate_w'], 'L0_ffn_W1': _L0_ffn_in['W1'], 'L0_ffn_b1': _L0_ffn_in['b1'], 'L0_ffn_W2': _L0_ffn_in['W2'], 'L0_ffn_b2': _L0_ffn_in['b2'], 'L0_ffn_rW1': _L0_ffn_in['rW1'], 'L0_ffn_rb1': _L0_ffn_in['rb1'], 'L0_ffn_rW2': _L0_ffn_in['rW2'], 'L0_ffn_rb2': _L0_ffn_in['rb2'], 'L0_ffn_coef_w': _L0_ffn_in['coef_w'], 'L0_ffn_coef_b': _L0_ffn_in['coef_b'], 'L1_xattn_Wq': _L1_xattn_in['Wq'], 'L1_xattn_bq': _L1_xattn_in['bq'], 'L1_xattn_Wk': _L1_xattn_in['Wk'], 'L1_xattn_bk': _L1_xattn_in['bk'], 'L1_xattn_Wv': _L1_xattn_in['Wv'], 'L1_xattn_bv': _L1_xattn_in['bv'], 'L1_xattn_Wo': _L1_xattn_in['Wo'], 'L1_xattn_bo': _L1_xattn_in['bo'], 'L1_ffn_W1': _L1_ffn_in['W1'], 'L1_ffn_b1': _L1_ffn_in['b1'], 'L1_ffn_W2': _L1_ffn_in['W2'], 'L1_ffn_b2': _L1_ffn_in['b2'], 'L1_ffn_Wu': _L1_ffn_in['Wu'], 'L1_ffn_bu': _L1_ffn_in['bu']}

def reference(x, ctx_1024, L0_xattn_Wq, L0_xattn_bq, L0_xattn_Wk, L0_xattn_bk, L0_xattn_Wv, L0_xattn_bv, L0_xattn_Wo, L0_xattn_bo, L0_ffn_ln1_g, L0_ffn_ln1_b, L0_ffn_Wqkv, L0_ffn_bqkv, L0_ffn_Wo, L0_ffn_bo, L0_ffn_ln2_g, L0_ffn_ln2_b, L0_ffn_gate_w, L0_ffn_W1, L0_ffn_b1, L0_ffn_W2, L0_ffn_b2, L0_ffn_rW1, L0_ffn_rb1, L0_ffn_rW2, L0_ffn_rb2, L0_ffn_coef_w, L0_ffn_coef_b, L1_xattn_Wq, L1_xattn_bq, L1_xattn_Wk, L1_xattn_bk, L1_xattn_Wv, L1_xattn_bv, L1_xattn_Wo, L1_xattn_bo, L1_ffn_W1, L1_ffn_b1, L1_ffn_W2, L1_ffn_b2, L1_ffn_Wu, L1_ffn_bu):
    import jax
    import jax.numpy as jnp

    def _L0_xattn_ref(query, key, value, Wq, bq, Wk, bk, Wv, bv, Wo, bo):
        import jax, jax.numpy as jnp
        import numpy as np
        D_MODEL = 256
        NUM_HEADS = 16
        D_K = D_MODEL // NUM_HEADS
        B, S = (4, 512)
        b, sq, _ = query.shape
        sk = key.shape[1]
        Q = query @ Wq + bq
        K = key @ Wk + bk
        V = value @ Wv + bv
        Q = Q.reshape(b, sq, NUM_HEADS, D_K).transpose(0, 2, 1, 3)
        K = K.reshape(b, sk, NUM_HEADS, D_K).transpose(0, 2, 1, 3)
        V = V.reshape(b, sk, NUM_HEADS, D_K).transpose(0, 2, 1, 3)
        scores = jnp.einsum('bhqd,bhkd->bhqk', Q, K) / jnp.sqrt(jnp.float32(D_K))
        attn = jax.nn.softmax(scores, axis=-1)
        out = jnp.einsum('bhqk,bhkd->bhqd', attn, V)
        out = out.transpose(0, 2, 1, 3).reshape(b, sq, D_MODEL)
        return out @ Wo + bo

    def _L0_ffn_ref(x, ln1_g, ln1_b, Wqkv, bqkv, Wo, bo, ln2_g, ln2_b, gate_w, W1, b1, W2, b2, rW1, rb1, rW2, rb2, coef_w, coef_b):
        import jax, jax.numpy as jnp
        import numpy as np
        DIM, HEADS, FFN, E = (256, 16, 1024, 8)
        B, S = (2, 256)
        EPS = 1e-05

        def _ln(x, g, b):
            mu = jnp.mean(x, axis=-1, keepdims=True)
            var = jnp.mean((x - mu) ** 2, axis=-1, keepdims=True)
            return (x - mu) * jax.lax.rsqrt(var + EPS) * g + b
        b, s, d = x.shape
        h, dh = (HEADS, d // HEADS)
        xn = _ln(x, ln1_g, ln1_b)
        qkv = xn @ Wqkv + bqkv
        q, k, v = jnp.split(qkv, 3, axis=-1)
        q = q.reshape(b, s, h, dh)
        k = k.reshape(b, s, h, dh)
        v = v.reshape(b, s, h, dh)
        scores = jnp.einsum('bqhd,bkhd->bhqk', q, k) / jnp.sqrt(jnp.float32(dh))
        attn = jax.nn.softmax(scores, axis=-1)
        ctx = jnp.einsum('bhqk,bkhd->bqhd', attn, v).reshape(b, s, d)
        x = x + ctx @ Wo + bo
        xn2 = _ln(x, ln2_g, ln2_b)
        xt = xn2.reshape(b * s, d)
        probs = jax.nn.softmax(xt @ gate_w, axis=-1)
        gate_val = jnp.max(probs, axis=-1, keepdims=True)
        expert_idx = jnp.argmax(probs, axis=-1)
        oh = jax.nn.one_hot(expert_idx, E, dtype=xt.dtype)
        xe = jnp.einsum('te,td->etd', oh, xt)
        he = jax.nn.gelu(jnp.einsum('etd,edf->etf', xe, W1) + b1[:, None, :], approximate=False)
        ye = jnp.einsum('etf,efd->etd', he, W2) + b2[:, None, :]
        moe_out = jnp.einsum('te,etd->td', oh, ye) * gate_val
        rm = jax.nn.gelu(xt @ rW1 + rb1, approximate=False) @ rW2 + rb2
        coef = jax.nn.softmax(xt @ coef_w + coef_b, axis=-1)
        ff = moe_out * coef[:, 0:1] + rm * coef[:, 1:2]
        return x + ff.reshape(b, s, d)

    def _L1_xattn_ref(query, key_value, Wq, bq, Wk, bk, Wv, bv, Wo, bo):
        import jax, jax.numpy as jnp
        import numpy as np
        D_MODEL = 256
        NUM_HEADS = 16
        HEAD_DIM = D_MODEL // NUM_HEADS
        B, SQ, _ = query.shape
        SKV = key_value.shape[1]
        H, Dh = (NUM_HEADS, HEAD_DIM)
        Q = (query @ Wq.T + bq).reshape(B, SQ, H, Dh).transpose(0, 2, 1, 3)
        K = (key_value @ Wk.T + bk).reshape(B, SKV, H, Dh).transpose(0, 2, 1, 3)
        V = (key_value @ Wv.T + bv).reshape(B, SKV, H, Dh).transpose(0, 2, 1, 3)
        scale = jnp.asarray(np.sqrt(Dh), query.dtype)
        scores = jnp.einsum('bhqd,bhkd->bhqk', Q, K) / scale
        weights = jax.nn.softmax(scores, axis=-1)
        attn = jnp.einsum('bhqk,bhkd->bhqd', weights, V)
        attn = attn.transpose(0, 2, 1, 3).reshape(B, SQ, H * Dh)
        return attn @ Wo.T + bo

    def _L1_ffn_ref(x, W1, b1, W2, b2, Wu, bu):
        import jax, jax.numpy as jnp
        import numpy as np
        B, S, D, F, E = (4, 512, 256, 1024, 4)
        n_exp = W1.shape[0]
        seq = x.shape[1]
        u = jax.nn.sigmoid(jnp.einsum('bsd,do->bso', x, Wu) + bu)[..., 0]
        k = jnp.clip(jnp.ceil(u * n_exp), 1, n_exp).astype(jnp.int32)
        h = jax.nn.relu(jnp.einsum('bsd,edf->bsef', x, W1) + b1)
        y = jnp.einsum('bsef,efd->bsed', h, W2) + b2
        s_idx = jnp.arange(seq)
        out = jnp.zeros_like(x)
        for i in range(1, n_exp + 1):
            e_idx = (s_idx + i - 1) % n_exp
            y_i = jnp.take_along_axis(y, e_idx[None, :, None, None], axis=2)[:, :, 0, :]
            w = jnp.where(k >= i, u / i, 0.0)
            out = out + w[..., None] * y_i
        return out
    x = x + _L0_xattn_ref(_layernorm(x, axis=-1), ctx_1024, ctx_1024, L0_xattn_Wq, L0_xattn_bq, L0_xattn_Wk, L0_xattn_bk, L0_xattn_Wv, L0_xattn_bv, L0_xattn_Wo, L0_xattn_bo)
    x = x + _L0_ffn_ref(_layernorm(x, axis=-1), L0_ffn_ln1_g, L0_ffn_ln1_b, L0_ffn_Wqkv, L0_ffn_bqkv, L0_ffn_Wo, L0_ffn_bo, L0_ffn_ln2_g, L0_ffn_ln2_b, L0_ffn_gate_w, L0_ffn_W1, L0_ffn_b1, L0_ffn_W2, L0_ffn_b2, L0_ffn_rW1, L0_ffn_rb1, L0_ffn_rW2, L0_ffn_rb2, L0_ffn_coef_w, L0_ffn_coef_b)
    x = x + _L1_xattn_ref(_layernorm(x, axis=-1), ctx_1024, L1_xattn_Wq, L1_xattn_bq, L1_xattn_Wk, L1_xattn_bk, L1_xattn_Wv, L1_xattn_bv, L1_xattn_Wo, L1_xattn_bo)
    x = x + _L1_ffn_ref(_layernorm(x, axis=-1), L1_ffn_W1, L1_ffn_b1, L1_ffn_W2, L1_ffn_b2, L1_ffn_Wu, L1_ffn_bu)
    return x

_drawn_inputs = setup_inputs


def setup_inputs(seed=0):
    import zlib

    import numpy as np

    out = dict(_drawn_inputs(seed))
    spreads = {'L0_xattn_bq': (0.0, 0.393),
     'L0_xattn_bk': (0.0, 2.0),
     'L0_xattn_bv': (0.0, 0.1),
     'L0_xattn_bo': (0.0, 0.1),
     'L0_ffn_ln1_g': (1.0, 0.6),
     'L0_ffn_ln1_b': (0.0, 0.8),
     'L0_ffn_bqkv': (0.0, 0.502),
     'L0_ffn_bo': (0.0, 0.1),
     'L0_ffn_ln2_g': (1.0, 0.6),
     'L0_ffn_ln2_b': (0.0, 0.8),
     'L0_ffn_b1': (0.0, 0.8),
     'L0_ffn_b2': (0.0, 0.8),
     'L0_ffn_rb1': (0.0, 2.0),
     'L0_ffn_rb2': (0.0, 2.0),
     'L0_ffn_coef_b': (0.0, 0.8),
     'L1_xattn_bq': (0.0, 2.0),
     'L1_xattn_bk': (0.0, 2.0),
     'L1_xattn_bv': (0.0, 0.8),
     'L1_xattn_bo': (0.0, 0.8)}
    factors = {'L0_ffn_Wqkv': 2.856,
     'L0_ffn_gate_w': 8.0,
     'L0_ffn_W1': 8.0,
     'L0_ffn_W2': 8.0,
     'L0_ffn_coef_w': 7.351,
     'L1_ffn_b1': 64.0,
     'L1_ffn_b2': 54.524,
     'L0_ffn_rW1': 6.674,
     'L0_ffn_rW2': 3.714,
     'L1_ffn_W1': 4.705,
     'L1_ffn_W2': 3.556,
     'L1_ffn_Wu': 8.0}
    for name, (base, spread) in spreads.items():
        noise = np.random.default_rng([zlib.crc32(name.encode()), seed]).standard_normal(out[name].shape)
        drawn = base * np.exp(spread * noise) if base else spread * noise
        out[name] = jnp.asarray(drawn.astype(out[name].dtype))
    for name, factor in factors.items():
        out[name] = (out[name] * factor).astype(out[name].dtype)
    return out
```

```python
from collections import namedtuple
from contextlib import ExitStack

import concourse.bass as bass
from concourse import mybir

ALU = mybir.AluOpType
ACT = mybir.ActivationFunctionType
F32 = mybir.dt.float32
BF16 = mybir.dt.bfloat16
AX_X = mybir.AxisListType.X

P = 128
B, S, D = 2, 1024, 256
T = B * S
NT = T // P
NBLK = T // 512
KD = D // P
H, DH = 16, 16
CTX = 64
FF = 1024
KF = FF // P
E0, E0R, E1 = 8, 9, 4
EPS = 1e-5
SCALE = 0.25
NG = H // 4
NU = B * NG
QT = S // P
NSTK = 3
ARENA = 35456
PAR_O = 20
H_FREE = 4
QPART = (0, 0, 1, 0, 2, 1)
KPART = (0, 1, 0, 2, 0, 1)
KS = 16 * len(QPART)
KM = KS + 3


LN_SEMS = ("stats", "mean_var", "std", "rstd", "normed", "turned", "xt_ready")
LNSems = namedtuple("LNSems", LN_SEMS)
X_SEMS = ("k_psum", "k_ready", "kbd_ready", "v_psum", "v_biased", "vbd_ready", "q_psum", "q_ready", "s_ready",
          "max_ready", "s_shifted", "p_ready", "pt_psum", "pt_act", "pt_dve", "av_ready", "recip_ready", "at_ready",
          "wo_ready", "x_biased", "x_done")
XSems = namedtuple("XSems", X_SEMS)
F_SEMS = ("weights0", "weights1", "h_psum", "h_done", "o_psum", "o_free", "ct_psum", "ct_ready", "b2_psum",
          "b2_done")
FSems = namedtuple("FSems", F_SEMS)


def block_kernel(nc, A, out):
    ctx = ExitStack()
    with ctx:
        def sb(name, shape, dt=F32):
            return ctx.enter_context(nc.sbuf_tensor(name, shape, dt))

        def sem(name):
            return ctx.enter_context(nc.semaphore(name))

        x = sb("x", [P, NT, D])
        xT = sb("xT", [P, KD, T])
        attn = xT[:, :, :].rearrange("p k t -> p (k t)").rearrange("p (t d) -> p t d", d=D)
        ident = sb("ident", [P, P])
        head_mask = sb("head_mask", [P, 8])
        pair_mask = sb("pair_mask", [P, 32])
        w_qkv = sb("w_qkv", [P, KD, 3 * D])
        w_self_o = sb("w_self_o", [P, KD, D])
        w_route = sb("w_route", [P, KD, E0 + 2])
        w_u = sb("w_u", [P, KD, 1])
        cols = sb("cols", [P, 12, KD])
        BQ0, BK0, BQS, BKS, BQ1, BK1, G1, B1, G2, B2 = range(10)
        rows = sb("rows", [P, 6, D])
        BV0, BO0, BVS, BOS, BV1, BO1 = range(6)
        coef_b = sb("coef_b", [P, 2])
        bu = sb("bu", [P, 1])
        b1_0 = sb("b1_0", [P, E0R, KF])
        b1_1 = sb("b1_1", [P, E1, KF])
        b2_0 = sb("b2_0", [E0R, D])
        b2_1 = sb("b2_1", [E1, D])
        step_inv = sb("step_inv", [P, E1])
        step_thr = sb("step_thr", [P, E1])
        first8 = sb("first8", [P, E0])
        stats = sb("stats", [P, NT, 6])
        mv = sb("mv", [P, NT, 2])
        std = sb("std", [P, NT])
        rstd = sb("rstd", [P, NT])
        rstd2 = sb("rstd2", [P, NT])
        vtmp = sb("vtmp", [P, NT])
        eps = sb("eps", [P, 1])
        credit = sb("credit", [P, 6])
        ctxm = sb("ctxm", [P, D])
        ctxT = sb("ctxT", [P, KD, P])
        ctxT2 = sb("ctxT2", [P, KD, B, 2, CTX])
        c0 = sb("c0", [P, NT, E0R])
        c1 = sb("c1", [P, NT, E1])
        AR = sb("arena", [P, ARENA])
        off = [0]

        def at(n, dt=F32):
            v = AR[:, off[0]:off[0] + n]
            off[0] += n
            assert off[0] <= ARENA, off[0]
            return v.bitcast(dt) if dt != F32 else v

        off[0] = 0
        qT = at(KD * T).rearrange("p (k t) -> p k t", k=KD)
        kT = at(KD * P).rearrange("p (k c) -> p k c", k=KD)
        kbd = at(B * KD * 512).rearrange("p (b k c) -> p b k c", b=B, k=KD)
        vb = at(B * D).rearrange("p (b d) -> p b d", b=B)
        vbd = at(B * 8 * 32).rearrange("p (b h c) -> p b h c", b=B, h=8)
        mx = at(3 * H).rearrange("p (n h) -> p n h", n=3)
        pbuf = at(3 * 1024).rearrange("p (n c) -> p n c", n=3)
        pT = at(2 * 8 * 512).rearrange("p (n h q) -> p n h q", n=2, h=8)
        rden = at(2 * 512).rearrange("p (n q) -> p n q", n=2)
        aT = at(2 * KD * 512).rearrange("p (n k q) -> p n k q", n=2, k=KD)
        cross_end = off[0]
        off[0] = ARENA - 8 * D - 4 * D
        wq, wk, wv, wo = (at(KD * D).rearrange("p (k d) -> p k d", k=KD) for _ in range(4))
        xn = at(4 * D).rearrange("p (n d) -> p n d", n=4)
        assert cross_end <= ARENA - 12 * D
        off[0] = 0
        split = [at(3 * KD * T // 2, BF16).rearrange("p (a k t) -> p a k t", a=3, k=KD) for _ in range(2)]
        stk = [at(4 * S // 2, BF16).rearrange("p (h t) -> p h t", h=4) for _ in range(2 * NSTK)]
        qstk, kstk = stk[:NSTK], stk[NSTK:]
        vones = at(NT * H // 2 * 48).rearrange("p (t h c) -> p t h c", t=NT, c=48)
        ptb = at(2 * S).rearrange("p (n q) -> p n q", n=2)
        oT = at(S)
        mpart = at(64).rearrange("p (a h) -> p a h", h=2)
        mrow = at(32)
        rres = at(2 * 512).rearrange("p (n q) -> p n q", n=2)
        mres = at(P)
        msplit = at(3 * P // 2, BF16).rearrange("p (a q) -> p a q", a=3)
        rsum = at(2 * 16).rearrange("p (n a) -> p n a", n=2)
        off[0] = 0
        x2 = at(NT * D).rearrange("p (t d) -> p t d", t=NT)
        aTs = at(4 * KD * P).rearrange("p (n k q) -> p n k q", n=4, k=KD)
        w1 = at(2 * KD * FF).rearrange("p (n k f) -> p n k f", n=2, k=KD)
        w2 = at(2 * KF * D).rearrange("p (n k d) -> p n k d", n=2, k=KF)
        hT = at(2 * KF * 512).rearrange("p (n k t) -> p n k t", n=2, k=KF)
        cT = at(T)
        rt = [at(NT * E0) for _ in range(8)]
        assert off[0] <= ARENA - 12 * D

        def v_and_ones(t, h):
            return vones[:, t, h // 2, 16 * (h % 2):16 * (h % 2) + 32]

        PS = ctx.enter_context(nc.psum_tensor("PS", [P, 8, 512], F32))

        load = sem("load")
        load2 = sem("load2")
        wload = sem("wload")
        const = sem("const")
        ctx_turned = sem("ctx_turned")
        ctx_ready = sem("ctx_ready")
        LN = [LNSems(*[sem(f"ln{n}_{name}") for name in LN_SEMS]) for n in range(5)]
        X = [XSems(*[sem(f"x{n}_{name}") for name in X_SEMS]) for n in range(2)]
        F = [FSems(*[sem(f"f{n}_{name}") for name in F_SEMS]) for n in range(2)]
        qk_psum = sem("qk_psum")
        high_ready = sem("high_ready")
        rest_ready = sem("rest_ready")
        mid_ready = sem("mid_ready")
        low_ready = sem("low_ready")
        vs_psum = sem("vs_psum")
        vs_ready = sem("vs_ready")
        ones_ready = sem("ones_ready")
        stacked = [sem(f"stacked{n}") for n in range(NSTK)]
        ring_full = sem("ring_full")
        ring_free = sem("ring_free")
        max_joined = sem("max_joined")
        msplit_ready = sem("msplit_ready")
        msplit_tmp = sem("msplit_tmp")
        mrow_landed = sem("mrow_landed")
        st_full = sem("st_full")
        exp_done = sem("exp_done")
        av_done = sem("av_done")
        o_full = sem("o_full")
        o_copied = sem("o_copied")
        rsum_ready = sem("rsum_ready")
        y_biased = sem("y_biased")
        a_turned = sem("a_turned")
        a_ready = sem("a_ready")
        so_psum = sem("so_psum")
        y_ready = sem("y_ready")
        x2_ready = sem("x2_ready")
        x_joined = sem("x_joined")
        r_psum = sem("r_psum")
        r_step = sem("r_step")
        r_exp = sem("r_exp")
        r_step1 = sem("r_step1")
        r_exp1 = sem("r_exp1")
        c_ready = [sem("c_ready0"), sem("c_ready1")]
        out_stored = sem("out_stored")

        NLOAD = [0]

        def jobs_after(u):
            return 65 * (min(u, NU - 2) + 2) + 2 * (u + 1)

        JOBS = jobs_after(NU - 1)
        block = ctx.enter_context(nc.Block())

        def w_of(name):
            return A[name].rearrange("(k p) f -> p k f", p=P)

        @block.sync
        def _(sp):
            def ld(dst, src):
                sp.dma_start(dst, src).then_inc(load, 16)
                NLOAD[0] += 16

            ld(x[:, :, :], A["x"].rearrange("(t p) d -> p t d", p=P))
            ld(ident[:, :], A["ident"])
            ld(ctxm[:, :], A["ctx"])
            ld(cols[:, 0:10, :], A["cols"])
            ld(rows[:, :, :], A["rows"].unsqueeze(0).broadcast_to([P, 6, D]))
            ld(head_mask[:, :], A["head_mask"])
            ld(pair_mask[:, :], A["pair_mask"])
            for tile, name in ((wq, "Wq0"), (wk, "Wk0"), (wv, "Wv0"), (wo, "Wo0")):
                ld(tile, w_of(name))
            assert NLOAD[0] == 16 * 11
            n2 = 0
            for tile, name in ((w_qkv, "Wqkv"), (w_self_o, "WoS"), (w_route, "w_route")):
                sp.dma_start(tile[:, :, :], w_of(name)).then_inc(load2, 16)
                n2 += 16
            for dst, src in ((w_u[:, :, 0], A["w_u"]), (coef_b[:, :], A["coef_b"].unsqueeze(0).broadcast_to([P, 2])),
                             (bu[:, :], A["bu"].unsqueeze(0).broadcast_to([P, 1])),
                             (b1_0[:, :, :], A["b1_0"]), (b1_1[:, :, :], A["b1_1"]),
                             (b2_0[:, :], A["b2_0"]), (b2_1[:, :], A["b2_1"]),
                             (step_inv[:, :], A["step_inv"]), (step_thr[:, :], A["step_thr"]),
                             (first8[:, :], A["first8"])):
                sp.dma_start(dst, src).then_inc(load2, 16)
                n2 += 16
            assert n2 == 16 * 13

            def stack_unit(u):
                b, g = divmod(u, NG)
                if u >= NSTK:
                    sp.wait_ge(av_done, 32 * (u - NSTK + 1))
                for parts, which, dst in ((QPART, 0, qstk), (KPART, 1, kstk)):
                    for i, part in enumerate(parts):
                        for j in range(4):
                            row = (g % 2) * 64 + 16 * j
                            sp.dma_start(dst[u % NSTK][16 * i:16 * i + 16, j, :],
                                         split[which][row:row + 16, part, g // 2, b * S:(b + 1) * S])\
                                .then_inc(stacked[u % NSTK], 16)

            sp.wait_ge(high_ready, 2 * KD * NBLK)
            sp.wait_ge(mid_ready, 2 * KD * NBLK)
            sp.wait_ge(low_ready, 2 * KD * NBLK)
            for u in range(NSTK - 1):
                stack_unit(u)
            for u in range(NU):
                sp.wait_ge(msplit_ready, u + 1)
                for i in range(3):
                    sp.dma_start(qstk[u % NSTK][KS + i:KS + i + 1, :, :].rearrange("p h t -> p (h t)"),
                                 msplit[0:32, i, :]).then_inc(mrow_landed, 16)
                if u + NSTK - 1 < NU:
                    stack_unit(u + NSTK - 1)

            def experts(n, a1, a2, count):
                f = F[n]

                def one(e, par):
                    sp.wait_ge(f.o_psum, PAR_O + NT * (e - 1))
                    sp.dma_start(w1[:, par, :, :], a1[bass.ds(e, 1)].rearrange("a (k p) f -> p (a k) f", p=P))\
                        .then_inc((f.weights0, f.weights1)[par], 16)
                    sp.dma_start(w2[:, par, :, :], a2[bass.ds(e, 1)].rearrange("a (k p) f -> p (a k) f", p=P))\
                        .then_inc((f.weights0, f.weights1)[par], 16)

                with sp.Fori(0, count // 2) as pair:
                    one(pair * 2, 0)
                    one(pair * 2 + 1, 1)
                if count % 2:
                    one(count - 1, 0)

            sp.wait_ge(ring_free, JOBS)
            experts(0, A["W1_0"], A["W2_0"], E0R)

            sp.wait_ge(F[0].o_free, PAR_O + NT * E0R)
            for tile, name in ((wq, "Wq1"), (wk, "Wk1"), (wv, "Wv1"), (wo, "Wo1")):
                sp.dma_start(tile, w_of(name)).then_inc(wload, 16)
            sp.wait_ge(X[1].x_done, NT)
            experts(1, A["W1_1"], A["W2_1"], E1)

            sp.wait_ge(F[1].o_free, PAR_O + NT * E1)
            sp.dma_start(out.rearrange("(t p) d -> p t d", p=P), x[:, :, :]).then_inc(out_stored, 16)
            sp.wait_ge(out_stored, 16)

        @block.tensor
        def _(pe):
            mm = nc.tensor.matmul

            def turn_norm(n):
                s = LN[n]
                for t in range(NT):
                    pe.wait_ge(s.normed, t + 1)
                    if t >= 4:
                        pe.wait_ge(s.xt_ready, t - 3)
                    for k in range(KD):
                        last = nc.tensor.transpose(PS[:, t % 4, k * P:(k + 1) * P],
                                                   xn[:, t % 4, k * P:(k + 1) * P], ident[:, :])
                    last.then_inc(s.turned, 1)

            def cross(n):
                s = X[n]
                ln = (LN[0], LN[3])[n]
                if n == 1:
                    pe.wait_ge(wload, 16 * 4)
                    pe.wait_ge(F[0].o_free, PAR_O + NT * E0R)
                for m in range(KD):
                    for k in range(KD):
                        last = mm(PS[:, 4, m * P:(m + 1) * P], wk[:, k, m * P:(m + 1) * P], ctxT[:, k, :],
                                  start=(k == 0), stop=(k == KD - 1))
                last.then_inc(s.k_psum, 1)
                for b in range(B):
                    for k in range(KD):
                        last = mm(PS[:, 5, b * D:(b + 1) * D],
                                  ctxT2[:, k, b, :, :].rearrange("p a c -> p (a c)"), wv[:, k, :],
                                  start=(k == 0), stop=(k == KD - 1))
                last.then_inc(s.v_psum, 1)
                for m in range(KD):
                    for blk in range(NBLK):
                        i = m * NBLK + blk
                        if m == 0:
                            pe.wait_ge(ln.xt_ready, 4 * blk + 4)
                        if i >= 2:
                            pe.wait_ge(s.q_ready, i - 1)
                        for k in range(KD):
                            last = mm(PS[:, 6 + i % 2, :], wq[:, k, m * P:(m + 1) * P],
                                      xT[:, k, blk * 512:(blk + 1) * 512], start=(k == 0), stop=(k == KD - 1))
                        last.then_inc(s.q_psum, 1)
                pe.wait_ge(s.kbd_ready, B * KD)
                pe.wait_ge(s.vbd_ready, B)
                pe.wait_ge(s.q_ready, KD * NBLK)

                def scores(t):
                    b = t // QT
                    if t >= 2:
                        pe.wait_ge(s.s_shifted, t - 1)
                    for m in range(KD):
                        last = mm(PS[:, 2 * (t % 2) + m, :], qT[:, m, t * P:(t + 1) * P], kbd[:, b, m, :],
                                  start=True, stop=True)
                    last.then_inc(s.s_ready, 1)

                def turn_p(t):
                    pe.wait_ge(s.p_ready, t + 1)
                    if t >= 1:
                        pe.wait_ge(s.pt_act, t)
                        pe.wait_ge(s.pt_dve, t)
                    for h in range(8):
                        last = nc.tensor.transpose(PS[:, 4 + h // 4, (h % 4) * P:(h % 4 + 1) * P],
                                                   pbuf[:, t % 3, h * P:(h + 1) * P], ident[:, :])
                    last.then_inc(s.pt_psum, 1)

                def weigh(blk):
                    b = blk // (NBLK // B)
                    pe.wait_ge(s.pt_act, 4 * blk + 4)
                    pe.wait_ge(s.pt_dve, 4 * blk + 4)
                    for m in range(KD):
                        if m:
                            pe.wait_ge(s.at_ready, KD * blk + m)
                        elif blk:
                            pe.wait_ge(s.x_done, 4 * blk)
                        for j in range(4):
                            mm(PS[32 * j:32 * j + 32, 6, :], vbd[:, b, 4 * m + j, :], pT[:, blk % 2, 4 * m + j, :],
                               start=True, stop=True)
                        for j in range(4):
                            last = mm(PS[32 * j:32 * j + 32, 7, :], pair_mask[:, :], pT[:, blk % 2, 4 * m + j, :],
                                      start=True, stop=True)
                        last.then_inc(s.av_ready, 1)
                    pe.wait_ge(s.at_ready, KD * (blk + 1))
                    for sub in range(4):
                        for m in range(KD):
                            last = mm(PS[:, 6 + sub // 2, (sub % 2) * D:(sub % 2 + 1) * D],
                                      aT[:, blk % 2, m, sub * P:(sub + 1) * P], wo[:, m, :],
                                      start=(m == 0), stop=(m == KD - 1))
                        if sub % 2:
                            last.then_inc(s.wo_ready, 1)

                scores(0)
                for t in range(NT):
                    if t + 1 < NT:
                        scores(t + 1)
                    turn_p(t)
                    if t % 4 == 3:
                        weigh(t // 4)

            def self_attention():
                pe.wait_ge(load2, 16 * 13)
                pe.wait_ge(X[0].x_done, NT)
                for w in range(2):
                    for m in range(KD):
                        for blk in range(NBLK):
                            i = (w * KD + m) * NBLK + blk
                            if i < 4:
                                pe.wait_ge(LN[1].xt_ready, 4 * blk + 4)
                            if i >= 4:
                                pe.wait_ge(rest_ready, i - 3)
                            for k in range(KD):
                                last = mm(PS[:, 4 + i % 4, :], w_qkv[:, k, w * D + m * P:w * D + (m + 1) * P],
                                          xT[:, k, blk * 512:(blk + 1) * 512], start=(k == 0), stop=(k == KD - 1))
                            last.then_inc(qk_psum, 1)
                for t in range(NT):
                    if t >= 4:
                        pe.wait_ge(vs_ready, t - 3)
                    for k in range(KD):
                        last = mm(PS[:, t % 4, 0:D], xT[:, k, t * P:(t + 1) * P], w_qkv[:, k, 2 * D:3 * D],
                                  start=(k == 0), stop=(k == KD - 1))
                    last.then_inc(vs_psum, 1)
                pe.wait_ge(vs_ready, NT)
                pe.wait_ge(rest_ready, 2 * KD * NBLK)
                pe.wait_ge(ones_ready, 1 + NSTK)

                job = 0
                step = 0
                for u in range(-1, NU):
                    v = u + 1
                    if v < NU:
                        pe.wait_ge(stacked[v % NSTK], 16 * 48 * (v // NSTK + 1))
                    if u >= 0:
                        pe.wait_ge(mrow_landed, 48 * (u + 1))
                    b, g = divmod(max(u, 0), NG)

                    def weigh(n, kt, j):
                        pe.wait_ge(exp_done, n + 1)
                        if kt == 0 and j == 0 and u >= 1:
                            pe.wait_ge(o_copied, 2 * u)
                        for half in range(2):
                            last = mm(PS[32 * j:32 * j + 32, 6 + half, :], v_and_ones(b * QT + kt, 4 * g + j),
                                      ptb[:, n % 2, half * 512:(half + 1) * 512],
                                      start=(kt == 0), stop=(kt == QT - 1))
                        last.then_inc(av_done, 1)

                    for s in range(32):
                        kt, j = divmod(s, 4)
                        if u >= 0:
                            if step >= 2:
                                pe.wait_ge(exp_done, step - 1)
                            for half in range(2):
                                last = mm(PS[:, 2 * (step % 2) + half, :],
                                          kstk[u % NSTK][0:KM, j, kt * P:(kt + 1) * P],
                                          qstk[u % NSTK][0:KM, j, half * 512:(half + 1) * 512],
                                          start=True, stop=True)
                            last.then_inc(st_full, 1)
                        if v < NU:
                            jj, qt = divmod(s, QT)
                            for half in range(2):
                                if job >= 2:
                                    pe.wait_ge(ring_free, job - 1)
                                mm(PS[:, 4 + job % 2, :], qstk[v % NSTK][0:KS, jj, qt * P:(qt + 1) * P],
                                   kstk[v % NSTK][0:KS, jj, half * 512:(half + 1) * 512],
                                   start=True, stop=True).then_inc(ring_full, 1)
                                job += 1
                        if u >= 0:
                            if s >= 1:
                                weigh(step - 1, *divmod(s - 1, 4))
                            step += 1
                    if u >= 0:
                        weigh(step - 1, QT - 1, 3)
                    if v < NU:
                        pe.wait_ge(max_joined, v + 1)
                        pe.wait_ge(ring_free, job - 1)
                        nc.tensor.transpose(PS[0:32, 4 + job % 2, 0:P], mrow[:, :], ident[:, :]).then_inc(ring_full, 1)
                        job += 1
                    if u >= 0:
                        pe.wait_ge(o_copied, 2 * u + 2)
                        for half in range(2):
                            pe.wait_ge(ring_free, job - 1)
                            for c in range(4):
                                last = nc.tensor.transpose(PS[:, 4 + job % 2, c * P:(c + 1) * P],
                                                           oT[:, (half * 4 + c) * P:(half * 4 + c + 1) * P], ident[:, :])
                            last.then_inc(ring_full, 1)
                            job += 1

                for t in range(NT + 1):
                    if t < NT:
                        if t == 0:
                            pe.wait_ge(ring_free, JOBS)
                        if t >= 4:
                            pe.wait_ge(a_ready, t - 3)
                        for k in range(KD):
                            last = nc.tensor.transpose(PS[:, t % 4, k * P:(k + 1) * P],
                                                       attn[:, t, k * P:(k + 1) * P], ident[:, :])
                        last.then_inc(a_turned, 1)
                    if t >= 1:
                        n = t - 1
                        pe.wait_ge(a_ready, n + 1)
                        if n >= 4:
                            pe.wait_ge(x2_ready, n - 3)
                        for k in range(KD):
                            last = mm(PS[:, 4 + n % 4, 0:D], aTs[:, n % 4, k, :], w_self_o[:, k, :],
                                      start=(k == 0), stop=(k == KD - 1))
                        last.then_inc(so_psum, 1)

            def route(n):
                w, width = ((w_route, E0 + 2), (w_u, 1))[n]
                ln = (LN[2], LN[4])[n]
                pe.wait_ge(ln.xt_ready, NT)
                pe.wait_ge(load2, 16 * 13)
                if n == 0:
                    pe.wait_ge(x2_ready, NT)
                else:
                    pe.wait_ge(X[1].x_done, NT)
                for t in range(NT):
                    for k in range(KD):
                        last = mm(PS[:, 4, t * width:(t + 1) * width], xT[:, k, t * P:(t + 1) * P], w[:, k, :],
                                  start=(k == 0), stop=(k == KD - 1))
                last.then_inc(r_psum, 1)
                pe.wait_ge(c_ready[n], 1)
                e, c = ((E0R, c0), (E1, c1))[n]
                for t in range(NT):
                    last = nc.tensor.transpose(PS[0:e, t // 4, (t % 4) * P:(t % 4 + 1) * P], c[:, t, :], ident[:, :])
                last.then_inc(F[n].ct_psum, 1)
                pe.wait_ge(F[n].ct_ready, 1)
                b2 = (b2_0, b2_1)[n]
                for t in range(NT):
                    if t >= 4:
                        pe.wait_ge(F[n].b2_done, t - 3)
                    mm(PS[:, 4 + t % 4, 0:D], cT[0:e, t * P:(t + 1) * P], b2[:, :], start=True, stop=True)\
                        .then_inc(F[n].b2_psum, 1)
                pe.wait_ge(F[n].b2_done, NT)

            def experts(n, count):
                s = F[n]

                def one(e, par):
                    pe.wait_ge((s.weights0, s.weights1)[par], 32 + 16 * (e - par))
                    for tb in range(NBLK + 1):
                        if tb < NBLK:
                            for f in range(KF):
                                i = tb * KF + f
                                pe.wait_ge(s.h_done, 32 * e + i + 1)
                                for k in range(KD):
                                    last = mm(PS[:, i % 4, :], w1[:, par, k, f * P:(f + 1) * P],
                                              xT[:, k, tb * 512:(tb + 1) * 512], start=(k == 0), stop=(k == KD - 1))
                                last.then_inc(s.h_psum, 1)
                        if tb >= 1:
                            tp = tb - 1
                            pe.wait_ge(s.h_done, 32 * e + H_FREE + KF * (tp + 1))
                            for sub in range(4):
                                i = tp * 4 + sub
                                pe.wait_ge(s.o_free, 16 * e + PAR_O - 3 + i)
                                for f in range(KF):
                                    last = mm(PS[:, 4 + i % 4, 0:D], hT[:, tp % 2, f, sub * P:(sub + 1) * P],
                                              w2[:, par, f, :], start=(f == 0), stop=(f == KF - 1))
                                last.then_inc(s.o_psum, 1)

                with pe.Fori(0, count // 2) as pair:
                    one(pair * 2, 0)
                    one(pair * 2 + 1, 1)
                if count % 2:
                    one(count - 1, 0)

            pe.wait_ge(load, 16 * 11)
            for k in range(KD):
                last = nc.tensor.transpose(PS[:, 7, k * P:(k + 1) * P], ctxm[:, k * P:(k + 1) * P], ident[:, :])
            last.then_inc(ctx_turned, 1)
            turn_norm(0)
            pe.wait_ge(ctx_ready, 3)
            cross(0)
            turn_norm(1)
            self_attention()
            turn_norm(2)
            route(0)
            experts(0, E0R)
            turn_norm(3)
            cross(1)
            turn_norm(4)
            route(1)
            experts(1, E1)

        @block.scalar
        def _(act):
            run = nc.scalar.activation

            def evacuate_norm(n, gain=None, bias=None):
                s = LN[n]
                act.wait_ge(s.mean_var, NT)
                run(std[:, :], mv[:, :, 1], ACT.Sqrt, bias=eps[:, :]).then_inc(s.std, 1)
                if n == 1:
                    act.wait_ge(s.rstd, 3)
                    run(std[:, :], vtmp[:, :], ACT.Sqrt, bias=eps[:, :]).then_inc(s.std, 1)
                for t in range(NT):
                    act.wait_ge(s.turned, t + 1)
                    dst, src = xT[:, :, t * P:(t + 1) * P], PS[:, t % 4, 0:D].rearrange("p (k t) -> p k t", k=KD)
                    if gain is None:
                        run(dst, src, ACT.Copy).then_inc(s.xt_ready, 1)
                    else:
                        for k in range(KD):
                            last = run(dst[:, k, :], src[:, k, :], ACT.Identity, bias=cols[:, bias, k:k + 1],
                                       scale=cols[:, gain, k:k + 1])
                        last.then_inc(s.xt_ready, 1)

            def cross(n):
                s = X[n]
                bq, bk = ((BQ0, BK0), (BQ1, BK1))[n]
                act.wait_ge(s.k_psum, 1)
                for m in range(KD):
                    last = run(kT[:, m, :], PS[:, 4, m * P:(m + 1) * P], ACT.Identity, bias=cols[:, bk, m:m + 1])
                last.then_inc(s.k_ready, 1)
                for i in range(KD * NBLK):
                    m, blk = divmod(i, NBLK)
                    act.wait_ge(s.q_psum, i + 1)
                    run(qT[:, m, blk * 512:(blk + 1) * 512], PS[:, 6 + i % 2, :], ACT.Identity,
                        bias=cols[:, bq, m:m + 1]).then_inc(s.q_ready, 1)

                def expo(t):
                    act.wait_ge(s.s_shifted, t + 1)
                    run(pbuf[:, t % 3, :], pbuf[:, t % 3, :], ACT.Exp, scale=SCALE).then_inc(s.p_ready, 1)

                def evacuate(t):
                    blk, sub = divmod(t, 4)
                    act.wait_ge(s.pt_psum, t + 1)
                    if sub == 0 and blk >= 2:
                        act.wait_ge(s.av_ready, KD * (blk - 1))
                    run(pT[:, blk % 2, 0:4, sub * P:(sub + 1) * P],
                        PS[:, 4, :].rearrange("p (h q) -> p h q", h=4), ACT.Copy).then_inc(s.pt_act, 1)

                expo(0)
                for t in range(NT):
                    if t + 1 < NT:
                        expo(t + 1)
                    evacuate(t)

            def self_attention():
                def high(i):
                    w, m, blk = i // 8, i // 4 % 2, i % 4
                    act.wait_ge(qk_psum, i + 1)
                    run(split[w][:, 0, m, blk * 512:(blk + 1) * 512], PS[:, 4 + i % 4, :], ACT.Identity,
                        bias=cols[:, (BQS, BKS)[w], m:m + 1]).then_inc(high_ready, 1)

                def middle(i):
                    w, m, blk = i // 8, i // 4 % 2, i % 4
                    act.wait_ge(rest_ready, i + 1)
                    run(split[w][:, 1, m, blk * 512:(blk + 1) * 512], rres[:, i % 2, :], ACT.Copy)\
                        .then_inc(mid_ready, 1)

                n = 2 * KD * NBLK
                for i in range(n):
                    high(i)
                    if i >= 1:
                        middle(i - 1)
                middle(n - 1)
                for u in range(NU):
                    for s in range(32):
                        step = 32 * u + s
                        act.wait_ge(st_full, step + 1)
                        if step >= 2:
                            act.wait_ge(av_done, step - 1)
                        run(ptb[:, step % 2, :], PS[:, 2 * (step % 2):2 * (step % 2) + 2, :].rearrange("p a q -> p (a q)"),
                            ACT.Exp, scale=SCALE).then_inc(exp_done, 1)
                    act.wait_ge(av_done, 32 * (u + 1))
                    if u >= 1:
                        act.wait_ge(ring_free, jobs_after(u - 1))
                    run(oT[:, 512:1024], PS[:, 7, :], ACT.Copy).then_inc(o_copied, 1)
                for t in range(NT):
                    act.wait_ge(a_turned, t + 1)
                    if t >= 4:
                        act.wait_ge(so_psum, t - 3)
                    run(aTs[:, t % 4, :, :], PS[:, t % 4, 0:D].rearrange("p (k q) -> p k q", k=KD), ACT.Copy)\
                        .then_inc(a_ready, 1)

            def route(n):
                if n == 0:
                    act.wait_ge(r_step, 3)
                    run(rt[2], rt[1], ACT.Exp).then_inc(r_exp, 1)
                    act.wait_ge(r_step, 6)
                    run(rt[4][:, 0:2 * NT], rt[3][:, 0:2 * NT], ACT.Exp).then_inc(r_exp, 1)
                else:
                    act.wait_ge(r_step1, 1)
                    run(rt[1][:, 0:NT], rt[0][:, 0:NT], ACT.Exp, scale=-1.0).then_inc(r_exp1, 1)
                e = (E0R, E1)[n]
                act.wait_ge(F[n].ct_psum, 1)
                run(cT[0:e, :], PS[0:e, 0:4, :].rearrange("p a q -> p (a q)"), ACT.Copy).then_inc(F[n].ct_ready, 1)

            def experts(n, count):
                s = F[n]
                b1 = (b1_0, b1_1)[n]
                func = (ACT.Gelu, ACT.Relu)[n]

                def one(e):
                    for i in range(NBLK * KF):
                        tb, f = divmod(i, KF)
                        act.wait_ge(s.h_psum, 32 * e + i + 1)
                        if f == 0:
                            act.wait_ge(s.o_psum, PAR_O + 16 * e + 4 * (tb - 1))
                        run(hT[:, tb % 2, f, :], PS[:, i % 4, :], func,
                            bias=b1[:, e, f:f + 1]).then_inc(s.h_done, 1)

                for e in range(count):
                    one(e)

            act.wait_ge(load, 16 * 11)
            act.wait_ge(ctx_turned, 1)
            run(ctxT[:, :, :], PS[:, 7, 0:D].rearrange("p (k c) -> p k c", k=KD), ACT.Copy).then_inc(ctx_ready, 1)
            for a in range(2):
                run(ctxT2[:, :, :, a, :], PS[:, 7, 0:D].rearrange("p (k b c) -> p k b c", k=KD, b=B), ACT.Copy)\
                    .then_inc(ctx_ready, 1)
            act.wait_ge(const, 1)
            evacuate_norm(0)
            cross(0)
            evacuate_norm(1, G1, B1)
            self_attention()
            evacuate_norm(2, G2, B2)
            act.wait_ge(load2, 16 * 13)
            route(0)
            experts(0, E0R)
            evacuate_norm(3)
            cross(1)
            evacuate_norm(4)
            route(1)
            experts(1, E1)

        @block.vector
        def _(dve):
            v = nc.vector

            def norm(n, src, ready, before, at_least=None):
                s = LN[n]
                for t in range(NT):
                    dve.wait_ge(ready, before + (t + 1 if at_least is None else at_least))
                    v.bn_stats(stats[:, t, :], src[:, t, :]).then_inc(s.stats, 1)
                dve.wait_ge(s.stats, NT)
                for t in range(NT):
                    v.bn_aggr(mv[:, t, :], stats[:, t, :]).then_inc(s.mean_var, 1)
                dve.wait_ge(s.std, 1)
                v.reciprocal(rstd[:, :], std[:, :]).then_inc(s.rstd, 1)
                dve.wait_ge(s.rstd, 1)
                scale, steps = rstd, 1
                if n == 1:
                    v.tensor_tensor(vtmp[:, :], mv[:, :, 1], rstd[:, :], ALU.mult).then_inc(s.rstd, 1)
                    dve.wait_ge(s.rstd, 2)
                    v.tensor_tensor(vtmp[:, :], vtmp[:, :], rstd[:, :], ALU.mult).then_inc(s.rstd, 1)
                    dve.wait_ge(s.std, 2)
                    v.reciprocal(rstd2[:, :], std[:, :]).then_inc(s.rstd, 1)
                    dve.wait_ge(s.rstd, 4)
                    v.tensor_tensor(rstd2[:, :], rstd2[:, :], rstd[:, :], ALU.mult).then_inc(s.rstd, 1)
                    dve.wait_ge(s.rstd, 5)
                    scale = rstd2
                for t in range(NT):
                    if t >= 4:
                        dve.wait_ge(s.turned, t - 3)
                    v.tensor_scalar(xn[:, t % 4, :], src[:, t, :], mv[:, t, 0:1], scale[:, t:t + 1],
                                    ALU.subtract, ALU.mult).then_inc(s.normed, 1)

            def cross(n):
                s = X[n]
                bv = (BV0, BV1)[n]
                dve.wait_ge(s.k_ready, 1)
                for b in range(B):
                    for m in range(KD):
                        v.tensor_tensor(kbd[:, b, m, :].rearrange("p (h c) -> p h c", h=8),
                                        kT[:, m, b * CTX:(b + 1) * CTX].unsqueeze(1).broadcast_to([P, 8, CTX]),
                                        head_mask[:, :].unsqueeze(2).broadcast_to([P, 8, CTX]), ALU.mult)\
                            .then_inc(s.kbd_ready, 1)
                dve.wait_ge(s.v_psum, 1)
                v.tensor_tensor(vb, PS[:, 5, :].rearrange("p (b d) -> p b d", b=B),
                                rows[:, bv, :].unsqueeze(1).broadcast_to([P, B, D]), ALU.add).then_inc(s.v_biased, 1)
                dve.wait_ge(s.v_biased, 1)
                for b in range(B):
                    v.tensor_tensor(vbd[:, b, :, :], vb[:, b, :].rearrange("p (h c) -> p h c", h=8),
                                    pair_mask[:, :].unsqueeze(1).broadcast_to([P, 8, 32]), ALU.mult)\
                        .then_inc(s.vbd_ready, 1)

                def shift(t):
                    dve.wait_ge(s.s_ready, t + 1)
                    sc = PS[:, 2 * (t % 2):2 * (t % 2) + 2, :].rearrange("p m (h c) -> p (m h) c", c=CTX)
                    v.tensor_reduce(mx[:, t % 3, :], sc, AX_X, ALU.max).then_inc(s.max_ready, 1)
                    dve.wait_ge(s.max_ready, t + 1)
                    if t >= 3:
                        dve.wait_ge(s.pt_psum, t - 2)
                    v.tensor_tensor(pbuf[:, t % 3, :].rearrange("p (h c) -> p h c", h=H), sc,
                                    mx[:, t % 3, :].unsqueeze(2).broadcast_to([P, H, CTX]), ALU.subtract)\
                        .then_inc(s.s_shifted, 1)

                shift(0)
                for t in range(NT):
                    blk, sub = divmod(t, 4)
                    if t + 1 < NT:
                        shift(t + 1)
                    dve.wait_ge(s.pt_psum, t + 1)
                    if sub == 0 and blk >= 2:
                        dve.wait_ge(s.av_ready, KD * (blk - 1))
                    v.tensor_copy(pT[:, blk % 2, 4:8, sub * P:(sub + 1) * P],
                                  PS[:, 5, :].rearrange("p (h q) -> p h q", h=4)).then_inc(s.pt_dve, 1)
                    if sub < 3:
                        continue
                    for m in range(KD):
                        i = KD * blk + m
                        dve.wait_ge(s.av_ready, i + 1)
                        v.reciprocal(rden[:, m, :], PS[:, 7, :]).then_inc(s.recip_ready, 1)
                        dve.wait_ge(s.recip_ready, i + 1)
                        v.tensor_tensor(aT[:, blk % 2, m, :], PS[:, 6, :], rden[:, m, :], ALU.mult)\
                            .then_inc(s.at_ready, 1)
                    dve.wait_ge(s.x_biased, 1)
                    for c in range(2):
                        tt = 4 * blk + 2 * c
                        dve.wait_ge(s.wo_ready, 2 * blk + c + 1)
                        v.tensor_tensor(x[:, tt:tt + 2, :], x[:, tt:tt + 2, :],
                                        PS[:, 6 + c, :].rearrange("p (t d) -> p t d", t=2), ALU.add)\
                            .then_inc(s.x_done, 2)

            def self_attention():
                def rest(i):
                    w, m, blk = i // 8, i // 4 % 2, i % 4
                    dve.wait_ge(high_ready, i + 1)
                    if i >= 2:
                        dve.wait_ge(mid_ready, i - 1)
                        dve.wait_ge(low_ready, i - 1)
                    v.scalar_tensor_tensor(out=rres[:, i % 2, :], in0=PS[:, 4 + i % 4, :],
                                           scalar=cols[:, (BQS, BKS)[w], m:m + 1],
                                           in1=split[w][:, 0, m, blk * 512:(blk + 1) * 512],
                                           op0=ALU.add, op1=ALU.subtract).then_inc(rest_ready, 1)

                def low(i):
                    w, m, blk = i // 8, i // 4 % 2, i % 4
                    dve.wait_ge(mid_ready, i + 1)
                    v.tensor_tensor(split[w][:, 2, m, blk * 512:(blk + 1) * 512], rres[:, i % 2, :],
                                    split[w][:, 1, m, blk * 512:(blk + 1) * 512], ALU.subtract).then_inc(low_ready, 1)

                n = 2 * KD * NBLK
                for i in range(n):
                    rest(i)
                    if i >= 1:
                        low(i - 1)
                low(n - 1)
                dve.wait_ge(load, 16 * 11)
                for t in range(NT):
                    dve.wait_ge(vs_psum, t + 1)
                    v.tensor_tensor(vones[:, t, :, :].rearrange("p h (a c) -> p h a c", a=3)[:, :, 0::2, :],
                                    PS[:, t % 4, 0:D].rearrange("p (h a c) -> p h a c", h=8, a=2),
                                    rows[:, BVS, :].rearrange("p (h a c) -> p h a c", h=8, a=2), ALU.add)\
                        .then_inc(vs_ready, 1)

                job = 0
                for u in range(-1, NU):
                    w = u + 1
                    if w < NU:
                        for s in range(64):
                            dve.wait_ge(ring_full, job + 1)
                            v.tensor_reduce(mpart[:, s // 2, s % 2:s % 2 + 1], PS[:, 4 + job % 2, :], AX_X, ALU.max)\
                                .then_inc(ring_free, 1)
                            job += 1
                        dve.wait_ge(ring_free, job)
                        v.tensor_tensor(mrow, mpart[:, :, 0], mpart[:, :, 1], ALU.max).then_inc(max_joined, 1)
                    if u >= 0:
                        dve.wait_ge(av_done, 32 * (u + 1))
                        v.tensor_copy(oT[:, 0:512], PS[:, 6, :]).then_inc(o_copied, 1)
                    if w < NU:
                        dve.wait_ge(ring_full, job + 1)
                        if w >= 1:
                            dve.wait_ge(mrow_landed, 48 * w)
                        ps = PS[0:32, 4 + job % 2, 0:P]
                        v.tensor_scalar(msplit[0:32, 0, :], ps, -1.0, None, ALU.mult).then_inc(msplit_tmp, 1)
                        dve.wait_ge(msplit_tmp, 2 * w + 1)
                        v.scalar_tensor_tensor(out=mres[0:32, :], in0=ps, scalar=-1.0, in1=msplit[0:32, 0, :],
                                               op0=ALU.mult, op1=ALU.subtract).then_inc(ring_free, 1)
                        job += 1
                        dve.wait_ge(ring_free, job)
                        v.tensor_copy(msplit[0:32, 1, :], mres[0:32, :]).then_inc(msplit_tmp, 1)
                        dve.wait_ge(msplit_tmp, 2 * w + 2)
                        v.tensor_tensor(msplit[0:32, 2, :], mres[0:32, :], msplit[0:32, 1, :], ALU.subtract)\
                            .then_inc(msplit_ready, 1)
                    if u >= 0:
                        b, g = divmod(u, NG)
                        for half in range(2):
                            dve.wait_ge(ring_full, job + 1)
                            o = PS[:, 4 + job % 2, :].rearrange("p (c h a d) -> p c h a d", c=4, h=2, a=4)
                            r = rsum[:, half, :].rearrange("p (c h a) -> p c h a", c=4, h=2)
                            v.reciprocal(r, o[:, :, :, 1:3, 0]).then_inc(rsum_ready, 1)
                            dve.wait_ge(rsum_ready, 2 * u + half + 1)
                            t0 = b * QT + 4 * half
                            for pair in range(2):
                                c = 64 * g + 32 * pair
                                last = v.tensor_tensor(
                                    attn[:, t0:t0 + 4, c:c + 32].rearrange("p c (a d) -> p c a d", a=2),
                                    o[:, :, pair, 0::3, :], r[:, :, pair, :].unsqueeze(3).broadcast_to([P, 4, 2, DH]),
                                    ALU.mult)
                            last.then_inc(ring_free, 1)
                            job += 1
                assert job == JOBS
                for t in range(NT):
                    v.tensor_scalar(x2[:, t, :], x[:, t, :], mv[:, t, 0:1], rstd[:, t:t + 1],
                                    ALU.subtract, ALU.mult).then_inc(y_ready, 1)
                for t in range(NT):
                    if t % 4 == 0:
                        dve.wait_ge(y_biased, t // 4 + 1)
                    dve.wait_ge(so_psum, t + 1)
                    v.tensor_tensor(x2[:, t, :], x2[:, t, :], PS[:, 4 + t % 4, 0:D], ALU.add).then_inc(x2_ready, 1)

            def route_experts():
                n = [0]

                def link(ins):
                    n[0] += 1
                    ins.then_inc(r_step, 1)
                    dve.wait_ge(r_step, n[0])

                def wide(a, c=E0):
                    return a[:, 0:NT * c].rearrange("p (t e) -> p t e", t=NT)

                def over(a, c=E0):
                    return a.unsqueeze(2).broadcast_to([P, NT, c])

                dve.wait_ge(r_psum, 1)
                L = PS[:, 4, 0:NT * (E0 + 2)].rearrange("p (t e) -> p t e", t=NT)
                top = rt[0][:, 0:NT]
                link(v.tensor_reduce(top, L[:, :, 0:E0], AX_X, ALU.max))
                link(v.tensor_tensor(wide(rt[1]), L[:, :, 0:E0], over(top), ALU.subtract))
                link(v.tensor_tensor(wide(rt[5], 2), L[:, :, E0:E0 + 2],
                                     coef_b[:, :].unsqueeze(1).broadcast_to([P, NT, 2]), ALU.add))
                link(v.tensor_reduce(rt[0][:, NT:2 * NT], wide(rt[5], 2), AX_X, ALU.max))
                link(v.tensor_tensor(wide(rt[3], 2), wide(rt[5], 2), over(rt[0][:, NT:2 * NT], 2), ALU.subtract))
                link(v.tensor_scalar(rt[6], rt[1], 0.0, None, ALU.is_ge))
                link(v.tensor_tensor(wide(rt[6]), wide(rt[6]), first8[:, :].unsqueeze(1).broadcast_to([P, NT, E0]),
                                     ALU.mult))
                link(v.tensor_reduce(rt[0][:, 2 * NT:3 * NT], wide(rt[6]), AX_X, ALU.max))
                link(v.tensor_tensor(wide(rt[7]), wide(rt[6]), over(rt[0][:, 2 * NT:3 * NT]), ALU.is_equal))
                dve.wait_ge(r_exp, 2)
                link(v.tensor_reduce(rt[0][:, 3 * NT:4 * NT], wide(rt[2]), AX_X, ALU.add))
                link(v.reciprocal(rt[0][:, 4 * NT:5 * NT], rt[0][:, 3 * NT:4 * NT]))
                link(v.tensor_reduce(rt[0][:, 5 * NT:6 * NT], wide(rt[4], 2), AX_X, ALU.add))
                link(v.reciprocal(rt[0][:, 6 * NT:7 * NT], rt[0][:, 5 * NT:6 * NT]))
                link(v.tensor_tensor(wide(rt[5], 2), wide(rt[4], 2), over(rt[0][:, 6 * NT:7 * NT], 2), ALU.mult))
                link(v.tensor_tensor(rt[0][:, 7 * NT:8 * NT], rt[0][:, 4 * NT:5 * NT], wide(rt[5], 2)[:, :, 0], ALU.mult))
                link(v.tensor_copy(c0[:, :, E0], wide(rt[5], 2)[:, :, 1]))
                v.tensor_tensor(c0[:, :, 0:E0], wide(rt[7]), over(rt[0][:, 7 * NT:8 * NT]), ALU.mult)\
                    .then_inc(c_ready[0], 1)
                dve.wait_ge(c_ready[0], 1)

            def route_steps():
                n = [0]

                def link(ins):
                    n[0] += 1
                    ins.then_inc(r_step1, 1)
                    dve.wait_ge(r_step1, n[0])

                dve.wait_ge(r_psum, 2)
                link(v.tensor_scalar(rt[0][:, 0:NT], PS[:, 4, 0:NT], bu[:, 0:1], None, ALU.add))
                dve.wait_ge(r_exp1, 1)
                link(v.tensor_scalar(rt[2][:, 0:NT], rt[1][:, 0:NT], 1.0, None, ALU.add))
                link(v.reciprocal(rt[3][:, 0:NT], rt[2][:, 0:NT]))
                link(v.tensor_scalar(rt[4][:, 0:NT], rt[3][:, 0:NT], float(E1), None, ALU.mult))

                def tokens(a):
                    return a[:, 0:NT].unsqueeze(2).broadcast_to([P, NT, E1])

                def steps(a):
                    return a[:, :].unsqueeze(1).broadcast_to([P, NT, E1])

                w = rt[5][:, 0:NT * E1].rearrange("p (t e) -> p t e", t=NT)
                on = rt[6][:, 0:NT * E1].rearrange("p (t e) -> p t e", t=NT)
                link(v.tensor_tensor(w, tokens(rt[3]), steps(step_inv), ALU.mult))
                link(v.tensor_tensor(on, tokens(rt[4]), steps(step_thr), ALU.is_gt))
                v.tensor_tensor(c1[:, :, :], w, on, ALU.mult).then_inc(c_ready[1], 1)
                dve.wait_ge(c_ready[1], 1)

            def second_biases(n):
                for t in range(NT):
                    dve.wait_ge(F[n].b2_psum, t + 1)
                    v.tensor_tensor(x[:, t, :], x[:, t, :], PS[:, 4 + t % 4, 0:D], ALU.add).then_inc(F[n].b2_done, 1)
                dve.wait_ge(F[n].b2_done, NT)

            def experts(n, count):
                s = F[n]
                c = (c0, c1)[n]

                def one(e):
                    for t in range(NT):
                        dve.wait_ge(s.o_psum, PAR_O + 16 * e + t + 1)
                        dve.wait_ge(s.o_free, PAR_O - 15 + 16 * e + t)
                        v.scalar_tensor_tensor(out=x[:, t, :], in0=PS[:, 4 + t % 4, 0:D],
                                               scalar=c[:, t, bass.ds(e, 1)], in1=x[:, t, :],
                                               op0=ALU.mult, op1=ALU.add).then_inc(s.o_free, 1)

                with dve.Fori(0, count) as e:
                    one(e)

            dve.wait_ge(load, 16 * 11)
            norm(0, x, load, 16 * 11, 0)
            cross(0)
            norm(1, x, X[0].x_done, 0)
            self_attention()
            norm(2, x2, x2_ready, 0)
            dve.wait_ge(load2, 16 * 13)
            route_experts()
            dve.wait_ge(x_joined, 1)
            second_biases(0)
            experts(0, E0R)
            norm(3, x, F[0].o_free, PAR_O + NT * E0)
            cross(1)
            norm(4, x, X[1].x_done, 0)
            route_steps()
            second_biases(1)
            experts(1, E1)

        @block.gpsimd
        def _(pool):
            g = nc.gpsimd
            g.memset(eps[:, :], EPS).then_inc(const, 1)
            for n in range(2):
                g.memset(credit[:, 3 * n:3 * n + 1], 0.0).then_inc(F[n].h_done, H_FREE)
                g.memset(credit[:, 3 * n + 1:3 * n + 2], 0.0).then_inc(F[n].o_psum, PAR_O)
                g.memset(credit[:, 3 * n + 2:3 * n + 3], 0.0).then_inc(F[n].o_free, PAR_O)

            def bias(n, row):
                pool.wait_ge(LN[3 * n].normed, NT)
                pool.wait_ge(load, 16 * 11)
                g.tensor_tensor(x[:, :, :], x[:, :, :], rows[:, row, :].unsqueeze(1).broadcast_to([P, NT, D]), ALU.add)\
                    .then_inc(X[n].x_biased, 1)

            bias(0, BO0)
            pool.wait_ge(X[0].x_done, NT)
            g.memset(vones[:, :, :, 16:32], 1.0).then_inc(ones_ready, 1)
            for n in range(NSTK):
                pool.wait_ge(ones_ready, n + 1)
                g.memset(kstk[n][KS:KM, :, :], 1.0).then_inc(ones_ready, 1)
            for c in range(4):
                pool.wait_ge(y_ready, 4 * c + 4)
                g.tensor_tensor(x2[:, 4 * c:4 * c + 4, :], x2[:, 4 * c:4 * c + 4, :],
                                rows[:, BOS, :].unsqueeze(1).broadcast_to([P, 4, D]), ALU.add).then_inc(y_biased, 1)
            pool.wait_ge(x2_ready, NT)
            g.tensor_tensor(x[:, :, :], x[:, :, :], x2, ALU.add).then_inc(x_joined, 1)
            bias(1, BO1)


def lay_out(i):
    import numpy as np

    f = {k: np.ascontiguousarray(v) for k, v in i.items()}
    col = lambda a: a.reshape(KD, P).T
    p = np.arange(P)
    step = (np.arange(E1)[None, :] - p[:, None]) % E1
    cols = ["L0_xattn_bq", "L0_xattn_bk", None, None, "L1_xattn_bq", "L1_xattn_bk", "L0_ffn_ln1_g", "L0_ffn_ln1_b",
            "L0_ffn_ln2_g", "L0_ffn_ln2_b"]
    bqkv = f["L0_ffn_bqkv"]
    a = {
        "x": f["x"].reshape(T, D), "ctx": f["ctx_1024"].reshape(B * CTX, D),
        "ident": np.eye(P, dtype=np.float32),
        "head_mask": (p[:, None] // 16 == np.arange(8)[None, :]).astype(np.float32),
        "pair_mask": (p[:, None] // 64 == np.arange(32)[None, :] // 16).astype(np.float32),
        "cols": np.stack([col(f[n]) if n else col(bqkv[(k - 2) * D:(k - 1) * D]) for k, n in enumerate(cols)], axis=1),
        "rows": np.stack([f["L0_xattn_bv"], f["L0_xattn_bo"], bqkv[2 * D:], f["L0_ffn_bo"], f["L1_xattn_bv"],
                          f["L1_xattn_bo"]]),
        "Wqkv": f["L0_ffn_Wqkv"], "WoS": f["L0_ffn_Wo"],
        "w_route": np.concatenate([f["L0_ffn_gate_w"], f["L0_ffn_coef_w"]], axis=1),
        "w_u": col(f["L1_ffn_Wu"]), "coef_b": f["L0_ffn_coef_b"], "bu": f["L1_ffn_bu"],
        "b1_0": np.concatenate([f["L0_ffn_b1"], f["L0_ffn_rb1"][None]]).reshape(E0R, KF, P).transpose(2, 0, 1),
        "b1_1": f["L1_ffn_b1"].reshape(E1, KF, P).transpose(2, 0, 1),
        "b2_0": np.concatenate([f["L0_ffn_b2"], f["L0_ffn_rb2"][None]]), "b2_1": f["L1_ffn_b2"],
        "W1_0": np.concatenate([f["L0_ffn_W1"], f["L0_ffn_rW1"][None]]),
        "W2_0": np.concatenate([f["L0_ffn_W2"], f["L0_ffn_rW2"][None]]),
        "W1_1": f["L1_ffn_W1"], "W2_1": f["L1_ffn_W2"],
        "step_inv": (1.0 / (step + 1)).astype(np.float32),
        "step_thr": np.where(step == 0, -1, step).astype(np.float32),
        "first8": np.broadcast_to(E0 - np.arange(E0, dtype=np.float32), (P, E0)),
    }
    for w in "qkvo":
        a[f"W{w}0"] = f[f"L0_xattn_W{w}"]
        a[f"W{w}1"] = f[f"L1_xattn_W{w}"].T
    return {k: np.ascontiguousarray(v) for k, v in a.items()}


def kernel(**inputs):
    import concourse.bacc as _bacc
    from concourse import mybir as _mybir
    from concourse.bass_utils import run_bass_kernel_spmd as _run

    nc = _bacc.Bacc("TRN2", target_bir_lowering=False, num_devices=1)
    laid = lay_out(inputs)
    arrays = {f"in_{k}": v for k, v in laid.items()}
    aps = {k: nc.dram_tensor(f"in_{k}", v.shape, _mybir.dt.from_np(v.dtype), kind="ExternalInput").ap()
           for k, v in laid.items()}
    out = nc.dram_tensor("out_x", (T, D), F32, kind="ExternalOutput").ap()
    block_kernel(nc, aps, out)
    r = _run(nc, [arrays], core_ids=[0])
    return r.results[0]["out_x"].reshape(B, S, D)
```

```python
from collections import namedtuple
from contextlib import ExitStack

import concourse.bass as bass
from concourse import mybir

ALU = mybir.AluOpType
ACT = mybir.ActivationFunctionType
F32 = mybir.dt.float32
BF16 = mybir.dt.bfloat16
U32 = mybir.dt.uint32
AX_X = mybir.AxisListType.X

P = 128
B, S, D = 2, 1024, 256
T = B * S
NT = T // P
NBLK = T // 512
KD = D // P
H, DH = 16, 16
CTX = 64
FF = 1024
KF = FF // P
E0, E0R, E1 = 8, 9, 4
EPS = 1e-5
SCALE = 0.25
NG = H // 4
NU = B * NG
QT = S // P
NSLOT = NT + E0 - 1
LEAD = 6
NSTK = 3
ARENA = 35456
PAR_O = 20
H_FREE = 4
QPART = (0, 0, 1, 0, 2, 1)
KPART = (0, 1, 0, 2, 0, 1)
KS = 16 * len(QPART)
KM = KS + 3


LN_SEMS = ("stats", "std", "rstd", "normed", "turned", "xt_ready")
LNSems = namedtuple("LNSems", LN_SEMS)
X_SEMS = ("kv_psum", "k_ready", "kv_spread", "v_biased", "q_psum", "q_ready", "s_ready",
          "max_ready", "s_shifted", "p_ready", "pt_psum", "pt_act", "pt_dve", "av_ready", "recip_ready", "at_ready",
          "wo_ready", "x_biased", "x_done")
XSems = namedtuple("XSems", X_SEMS)
F_SEMS = ("weights0", "weights1", "h_psum", "h_done", "o_psum", "o_free", "ct_psum", "ct_ready", "b2_done")
FSems = namedtuple("FSems", F_SEMS)


def block_kernel(nc, A, out):
    ctx = ExitStack()
    with ctx:
        def sb(name, shape, dt=F32):
            return ctx.enter_context(nc.sbuf_tensor(name, shape, dt))

        def sem(name):
            return ctx.enter_context(nc.semaphore(name))

        x = sb("x", [P, NT, D])
        xT = sb("xT", [P, KD, T])
        attn = xT[:, :, :].rearrange("p k t -> p (k t)").rearrange("p (t d) -> p t d", d=D)
        ident = sb("ident", [P, P])
        head_mask = sb("head_mask", [P, 8])
        pair_mask = sb("pair_mask", [P, 32])
        w_both = sb("w_both", [P, KD * 5 * D])
        w_self_o = w_both[:, 0:KD * D].rearrange("p (k d) -> p k d", k=KD)
        w_qkv = w_both[:, KD * D:KD * 4 * D].rearrange("p (k d) -> p k d", k=KD)
        rw2 = w_both[:, 0:KF * D].rearrange("p (k d) -> p k d", k=KF)
        slot_y = w_both[:, KF * D:].rearrange("p (n d) -> p n d", n=2)
        w_route = sb("w_route", [P, KD, E0 + 2])
        w_u = sb("w_u", [P, KD, 1])
        cols = sb("cols", [P, 12, KD])
        BQ0, BK0, BQS, BKS, BQ1, BK1, G1, B1, G2, B2 = range(10)
        rows = sb("rows", [P, 6, D])
        BV0, BO0, BVS, BOS, BV1, BO1 = range(6)
        coef_b = sb("coef_b", [P, 2])
        bu = sb("bu", [P, 1])
        b1_0 = sb("b1_0", [P, E0R, KF])
        b1_1 = sb("b1_1", [P, E1, KF])
        b2_0 = sb("b2_0", [E0R, D])
        b2_1 = sb("b2_1", [E1, D])
        step_inv = sb("step_inv", [P, E1])
        step_thr = sb("step_thr", [P, E1])
        first8 = sb("first8", [P, E0])
        stats = sb("stats", [P, NT, 6])
        mv = sb("mv", [P, NT, 2])
        std = sb("std", [P, NT])
        rstd = sb("rstd", [P, NT])
        rstd2 = sb("rstd2", [P, NT])
        vtmp = sb("vtmp", [P, NT])
        eps = sb("eps", [P, 1])
        credit = sb("credit", [P, 9])
        ctxT = sb("ctxT", [P, KD, P])
        ctxT2 = sb("ctxT2", [P, KD, B, 2, CTX])
        c0 = sb("c0", [P, NT, E0R])
        c1 = sb("c1", [P, NT, E1])
        rt_all = sb("rt_all", [P, 8 * NT * E0])
        rt = [rt_all[:, n * NT * E0:(n + 1) * NT * E0] for n in range(8)]
        before = sb("before", [P, P])
        ones = sb("ones", [P, P])
        tile_edges = sb("tile_edges", [P, NT])
        slot_index = sb("slot_index", [P, NSLOT])
        grow = sb("grow", [P, 2, NT, E0])
        sizes = sb("sizes", [P, 8, E0])
        fits = sb("fits", [P, NSLOT * E0])
        eidf = sb("eidf", [P, NSLOT])
        expert_of = sb("expert_of", [P, NSLOT], U32)
        posf = sb("posf", [P, NT])
        slot_of = sb("slot_of", [P, NT], U32)
        zeros = sb("zeros", [P, D])
        slot_in = sb("slot_in", [P, 4 * D])
        slot_x = slot_in[:, 0:2 * D].rearrange("p (n d) -> p n d", n=2)
        slot_xT = slot_in[:, 2 * D:].rearrange("p (n k q) -> p n k q", n=2, k=KD)
        ctxm = slot_x[:, 0, :]
        slot_b1 = sb("slot_b1", [P, 2, KF])
        AR = sb("arena", [P, ARENA])
        off = [0]

        def at(n, dt=F32):
            v = AR[:, off[0]:off[0] + n]
            off[0] += n
            assert off[0] <= ARENA, off[0]
            return v.bitcast(dt) if dt != F32 else v

        off[0] = 0
        qT = at(KD * T).rearrange("p (k t) -> p k t", k=KD)
        kT = at(KD * P).rearrange("p (k c) -> p k c", k=KD)
        kbd = at(B * KD * 512).rearrange("p (b k c) -> p b k c", b=B, k=KD)
        vb = at(B * D).rearrange("p (b d) -> p b d", b=B)
        vbd = at(B * 8 * 32).rearrange("p (b h c) -> p b h c", b=B, h=8)
        mx = at(3 * H).rearrange("p (n h) -> p n h", n=3)
        pbuf = at(3 * 1024).rearrange("p (n c) -> p n c", n=3)
        pT = at(2 * 8 * 512).rearrange("p (n h q) -> p n h q", n=2, h=8)
        rden = at(2 * 512).rearrange("p (n q) -> p n q", n=2)
        aT = at(2 * KD * 512).rearrange("p (n k q) -> p n k q", n=2, k=KD)
        cross_end = off[0]
        WE = KD * FF
        off[0] = 14 * WE + 4 * D
        assert cross_end <= off[0]
        xn = at(4 * D).rearrange("p (n d) -> p n d", n=4)
        wq, wk, wv, wo = (at(KD * D).rearrange("p (k d) -> p k d", k=KD) for _ in range(4))
        xn_self = AR[:, ARENA - 4 * D:].rearrange("p (n d) -> p n d", n=4)
        off[0] = 0
        split = [at(3 * KD * T // 2, BF16).rearrange("p (a k t) -> p a k t", a=3, k=KD) for _ in range(2)]
        stk = [at(4 * S // 2, BF16).rearrange("p (h t) -> p h t", h=4) for _ in range(2 * NSTK)]
        qstk, kstk = stk[:NSTK], stk[NSTK:]
        vones = at(NT * H // 2 * 48).rearrange("p (t h c) -> p t h c", t=NT, c=48)
        own = at(2 * S)
        ptb = [own[:, 0:S], own[:, S:], w_both[:, KD * D:KD * D + S], w_both[:, KD * D + S:KD * D + 2 * S],
               rt_all[:, :], slot_in[:, :], at(2 * 512)]
        NPTB = len(ptb)
        oT = at(S)
        mpart = at(2 * 64).rearrange("p (n a h) -> p n a h", n=2, h=2)
        mrow = at(32)
        rres = ptb[-1].rearrange("p (n q) -> p n q", n=2)
        mres = at(P)
        msplit = at(3 * P // 2, BF16).rearrange("p (a q) -> p a q", a=3)
        rsum = at(2 * 16).rearrange("p (n a) -> p n a", n=2)
        w1_all = AR[:, 0:E0 * WE].rearrange("p (e k f) -> p e k f", e=E0, k=KD)
        w2_all = AR[:, E0 * WE:2 * E0 * WE].rearrange("p (e k d) -> p e k d", e=E0, k=KF)
        off[0] = 12 * WE
        x2 = at(NT * D).rearrange("p (t d) -> p t d", t=NT)
        aTs = at(4 * KD * P).rearrange("p (n k q) -> p n k q", n=4, k=KD)
        rhT = AR[:, 14 * WE:16 * WE].rearrange("p (n k t) -> p n k t", n=2, k=KF)
        rw1 = AR[:, 16 * WE:17 * WE].rearrange("p (k f) -> p k f", k=KD)
        slot_h = xT[:, :, :].rearrange("p k t -> p (k t)")[:, 0:2 * FF].rearrange("p (n f) -> p n f", n=2)
        slot_hT = xT[:, :, :].rearrange("p k t -> p (k t)")[:, 2 * FF:4 * FF].rearrange("p (n k q) -> p n k q", n=2, k=KF)
        gathered_y = AR[:, 0:NT * D].rearrange("p (t d) -> p t d", t=NT)
        off[0] = NT * D
        cT = at(T)
        w1 = at(2 * KD * FF).rearrange("p (n k f) -> p n k f", n=2, k=KD)
        w2 = at(2 * KF * D).rearrange("p (n k d) -> p n k d", n=2, k=KF)
        hT = at(2 * KF * 512).rearrange("p (n k t) -> p n k t", n=2, k=KF)
        assert off[0] <= 14 * WE

        def v_and_ones(t, h):
            return vones[:, t, h // 2, 16 * (h % 2):16 * (h % 2) + 32]

        PS = ctx.enter_context(nc.psum_tensor("PS", [P, 8, 512], F32))

        load = sem("load")
        load2 = sem("load2")
        wload = sem("wload")
        const = sem("const")
        ctx_turned = sem("ctx_turned")
        ctx_ready = sem("ctx_ready")
        LN = [LNSems(*[sem(f"ln{n}_{name}") for name in LN_SEMS]) for n in range(5)]
        X = [XSems(*[sem(f"x{n}_{name}") for name in X_SEMS]) for n in range(2)]
        F = [FSems(*[sem(f"f{n}_{name}") for name in F_SEMS]) for n in range(2)]
        qk_psum = sem("qk_psum")
        high_ready = sem("high_ready")
        rest_ready = sem("rest_ready")
        mid_ready = sem("mid_ready")
        low_ready = sem("low_ready")
        vs_psum = sem("vs_psum")
        vs_ready = sem("vs_ready")
        ones_ready = sem("ones_ready")
        stacked = [sem(f"stacked{n}") for n in range(NSTK)]
        ring_full = sem("ring_full")
        ring_free = sem("ring_free")
        max_joined = sem("max_joined")
        msplit_ready = sem("msplit_ready")
        msplit_tmp = sem("msplit_tmp")
        mrow_landed = sem("mrow_landed")
        st_full = sem("st_full")
        exp_done = sem("exp_done")
        av_done = sem("av_done")
        o_full = sem("o_full")
        o_copied = sem("o_copied")
        rsum_ready = sem("rsum_ready")
        y_biased = sem("y_biased")
        a_turned = sem("a_turned")
        a_ready = sem("a_ready")
        so_psum = sem("so_psum")
        y_ready = sem("y_ready")
        x2_ready = sem("x2_ready")
        x_joined = sem("x_joined")
        r_psum = sem("r_psum")
        r_step = sem("r_step")
        r_exp = sem("r_exp")
        r_step1 = sem("r_step1")
        r_exp1 = sem("r_exp1")
        c_ready = [sem("c_ready0"), sem("c_ready1")]
        out_stored = sem("out_stored")
        zeros_ready = sem("zeros_ready")
        slots_zeroed = sem("slots_zeroed")
        w_route_all = sem("w_route_all")
        rank_psum = sem("rank_psum")
        place_step = sem("place_step")
        x2_normed = sem("x2_normed")
        scattered = sem("scattered")
        slot_loaded = [sem(f"slot_loaded{n}") for n in range(2)]
        slot_turned = sem("slot_turned")
        slot_xt = sem("slot_xt")
        slot_h_psum = sem("slot_h_psum")
        slot_h_copied = sem("slot_h_copied")
        slot_ht_psum = sem("slot_ht_psum")
        slot_b1_ready = sem("slot_b1_ready")
        slot_gelu = sem("slot_gelu")
        slot_y_psum = sem("slot_y_psum")
        slot_y_copied = sem("slot_y_copied")
        slot_stored = [sem(f"slot_stored{n}") for n in range(2)]
        gathered = [sem(f"gathered{n}") for n in range(4)]
        routed_done = sem("routed_done")

        slots_in = nc.dram_tensor("slots_in", (NSLOT * P, D), F32, kind="Internal").ap()
        slots_out = nc.dram_tensor("slots_out", (NSLOT * P, D), F32, kind="Internal").ap()

        NLOAD = [0]
        LOAD2 = 16 * 16

        def ring_jobs(n):
            jobs = []
            v, at_v = divmod(n + 32 + LEAD, 32)
            if v < NU:
                jobs += [("scores", v, 2 * at_v + half) for half in range(2)]
            if at_v == 1 and v >= 1 and v <= NU:
                jobs.append(("maxima", v - 1, 0))
            u, at_u = divmod(n, 32)
            if u >= 1 and at_u in (6, 7):
                jobs.append(("output", u - 1, at_u - 6))
            return jobs

        STEPS = range(-32 - LEAD, 32 * NU + 8)
        JOBS = sum(len(ring_jobs(n)) for n in STEPS)

        def jobs_before(n):
            return sum(len(ring_jobs(i)) for i in STEPS if i < n)

        PLACED = 27
        block = ctx.enter_context(nc.Block())

        def w_of(name):
            return A[name].rearrange("(k p) f -> p k f", p=P)

        @block.sync
        def _(sp):
            def ld(dst, src):
                sp.dma_start(dst, src).then_inc(load, 16)
                NLOAD[0] += 16

            ld(x[:, :, :], A["x"].rearrange("(t p) d -> p t d", p=P))
            ld(ident[:, :], A["ident"])
            ld(ctxm[:, :], A["ctx"])
            ld(cols[:, 0:10, :], A["cols"])
            ld(rows[:, :, :], A["rows"].unsqueeze(0).broadcast_to([P, 6, D]))
            ld(head_mask[:, :], A["head_mask"])
            ld(pair_mask[:, :], A["pair_mask"])
            for tile, name in ((wq, "Wq0"), (wk, "Wk0"), (wv, "Wv0"), (wo, "Wo0")):
                ld(tile, w_of(name))
            assert NLOAD[0] == 16 * 11
            n2 = 0
            for tile, name in ((w_qkv, "Wqkv"), (w_self_o, "WoS"), (w_route[:, :, :], "w_route")):
                sp.dma_start(tile, w_of(name)).then_inc(load2, 16)
                n2 += 16
            for dst, src in ((w_u[:, :, 0], A["w_u"]), (coef_b[:, :], A["coef_b"].unsqueeze(0).broadcast_to([P, 2])),
                             (bu[:, :], A["bu"].unsqueeze(0).broadcast_to([P, 1])),
                             (b1_0[:, :, :], A["b1_0"]), (b1_1[:, :, :], A["b1_1"]),
                             (b2_0[:, :], A["b2_0"]), (b2_1[:, :], A["b2_1"]),
                             (step_inv[:, :], A["step_inv"]), (step_thr[:, :], A["step_thr"]),
                             (before[:, :], A["before"]), (tile_edges[:, :], A["tile_edges"]),
                             (slot_index[:, :], A["slot_index"]), (first8[:, :], A["first8"])):
                sp.dma_start(dst, src).then_inc(load2, 16)
                n2 += 16
            assert n2 == LOAD2
            sp.wait_ge(zeros_ready, 1)
            sp.dma_start(slots_in.rearrange("(p j) d -> p j d", j=NSLOT), zeros[:, :].unsqueeze(1).broadcast_to([P, NSLOT, D]))\
                .then_inc(slots_zeroed, 16)

            def stack_unit(u):
                b, g = divmod(u, NG)
                if u >= NSTK:
                    sp.wait_ge(st_full, 32 * (u - NSTK + 1))
                for parts, which, dst in ((QPART, 0, qstk), (KPART, 1, kstk)):
                    for i, part in enumerate(parts):
                        for j in range(4):
                            row = (g % 2) * 64 + 16 * j
                            sp.dma_start(dst[u % NSTK][16 * i:16 * i + 16, j, :],
                                         split[which][row:row + 16, part, g // 2, b * S:(b + 1) * S])\
                                .then_inc(stacked[u % NSTK], 16)

            sp.wait_ge(high_ready, 2 * KD * NBLK)
            sp.wait_ge(mid_ready, 2 * KD * NBLK)
            sp.wait_ge(low_ready, 2 * KD * NBLK)
            for u in range(NSTK - 1):
                stack_unit(u)
            for u in range(NU):
                sp.wait_ge(msplit_ready, u + 1)
                for i in range(3):
                    sp.dma_start(qstk[u % NSTK][KS + i:KS + i + 1, :, :].rearrange("p h t -> p (h t)"),
                                 msplit[0:32, i, :]).then_inc(mrow_landed, 16)
                if u + NSTK - 1 < NU:
                    stack_unit(u + NSTK - 1)

            def experts(n, a1, a2, count):
                f = F[n]

                def one(e, par):
                    sp.wait_ge(f.o_psum, PAR_O + NT * (e - 1))
                    sp.dma_start(w1[:, par, :, :], a1[bass.ds(e, 1)].rearrange("a (k p) f -> p (a k) f", p=P))\
                        .then_inc((f.weights0, f.weights1)[par], 16)
                    sp.dma_start(w2[:, par, :, :], a2[bass.ds(e, 1)].rearrange("a (k p) f -> p (a k) f", p=P))\
                        .then_inc((f.weights0, f.weights1)[par], 16)

                with sp.Fori(0, count // 2) as pair:
                    one(pair * 2, 0)
                    one(pair * 2 + 1, 1)
                if count % 2:
                    one(count - 1, 0)

            def routed_weights(e, which):
                dst, src, k = ((w1_all, A["W1_0"], KD), (w2_all, A["W2_0"], KF))[which]
                sp.dma_start(dst[:, e, :, :], src[e].rearrange("(k p) f -> p k f", p=P)).then_inc(w_route_all, 16)

            sp.wait_ge(ring_free, JOBS)
            sp.dma_start(rw1, A["W1_0"][E0].rearrange("(k p) f -> p k f", p=P)).then_inc(F[0].weights0, 16)
            for e in range(E0):
                routed_weights(e, 0)
            for e in range(4):
                routed_weights(e, 1)
            sp.wait_ge(so_psum, NT)
            sp.dma_start(rw2, A["W2_0"][E0].rearrange("(k p) f -> p k f", p=P)).then_inc(F[0].weights0, 16)
            sp.wait_ge(scattered, 16 * NT)
            routed_weights(4, 1)
            routed_weights(5, 1)

            def load_slots(j, par):
                sp.wait_ge(slot_turned, j - 1)
                sp.dma_start(slot_x[:, par, :], slots_in[bass.ds(j * P, P), :]).then_inc(slot_loaded[par], 16)

            def store_slots(j, par):
                sp.wait_ge(slot_y_copied, j + 3)
                sp.dma_start(slots_out[bass.ds(j * P, P), :], slot_y[:, par, :]).then_inc(slot_stored[par], 16)

            for j in range(2):
                sp.dma_start(slot_x[:, j, :], slots_in[j * P:(j + 1) * P, :]).then_inc(slot_loaded[j], 16)
            sp.wait_ge(F[0].o_free, PAR_O + NT)
            routed_weights(6, 1)
            routed_weights(7, 1)
            load_slots(2, 0)
            load_slots(3, 1)
            with sp.Fori(0, (NSLOT - 5) // 2) as pair:
                for par in range(2):
                    load_slots(pair * 2 + 4 + par, par)
                    store_slots(pair * 2 + par, par)
            load_slots(NSLOT - 1, (NSLOT - 1) % 2)
            for j in range(NSLOT - 5, NSLOT):
                store_slots(j, j % 2)

            sp.wait_ge(routed_done, NT)
            for tile, name in ((wq, "Wq1"), (wk, "Wk1"), (wv, "Wv1"), (wo, "Wo1")):
                sp.dma_start(tile, w_of(name)).then_inc(wload, 16)
            sp.wait_ge(X[1].x_done, NT)
            experts(1, A["W1_1"], A["W2_1"], E1)

            sp.wait_ge(F[1].o_free, PAR_O + NT * E1)
            sp.dma_start(out.rearrange("(t p) d -> p t d", p=P), x[:, :, :]).then_inc(out_stored, 16)
            sp.wait_ge(out_stored, 16)

        @block.tensor
        def _(pe):
            mm = nc.tensor.matmul

            def turn_norm(n):
                s = LN[n]
                buf = xn_self if n == 1 else xn
                for t in range(NT):
                    pe.wait_ge(s.normed, t + 1)
                    if t >= 4:
                        pe.wait_ge(s.xt_ready, t - 3)
                    for k in range(KD):
                        last = nc.tensor.transpose(PS[:, t % 4, k * P:(k + 1) * P],
                                                   buf[:, t % 4, k * P:(k + 1) * P], ident[:, :])
                    last.then_inc(s.turned, 1)

            def cross(n):
                s = X[n]
                ln = (LN[0], LN[3])[n]
                if n == 1:
                    pe.wait_ge(wload, 16 * 4)
                    pe.wait_ge(routed_done, NT)
                for m in range(KD):
                    for k in range(KD):
                        last = mm(PS[:, 4, m * P:(m + 1) * P], wk[:, k, m * P:(m + 1) * P], ctxT[:, k, :],
                                  start=(k == 0), stop=(k == KD - 1))
                last.then_inc(s.kv_psum, 1)
                for b in range(B):
                    for k in range(KD):
                        last = mm(PS[:, 5, b * D:(b + 1) * D],
                                  ctxT2[:, k, b, :, :].rearrange("p a c -> p (a c)"), wv[:, k, :],
                                  start=(k == 0), stop=(k == KD - 1))
                last.then_inc(s.kv_psum, 1)
                for m in range(KD):
                    for blk in range(NBLK):
                        i = m * NBLK + blk
                        if m == 0:
                            pe.wait_ge(ln.xt_ready, 4 * blk + 4)
                        if i >= 2:
                            pe.wait_ge(s.q_ready, i - 1)
                        for k in range(KD):
                            last = mm(PS[:, 6 + i % 2, :], wq[:, k, m * P:(m + 1) * P],
                                      xT[:, k, blk * 512:(blk + 1) * 512], start=(k == 0), stop=(k == KD - 1))
                        last.then_inc(s.q_psum, 1)
                pe.wait_ge(s.kv_spread, B * KD + B)
                pe.wait_ge(s.q_ready, KD * NBLK)

                def scores(t):
                    b = t // QT
                    if t >= 2:
                        pe.wait_ge(s.s_shifted, t - 1)
                    for m in range(KD):
                        last = mm(PS[:, 2 * (t % 2) + m, :], qT[:, m, t * P:(t + 1) * P], kbd[:, b, m, :],
                                  start=True, stop=True)
                    last.then_inc(s.s_ready, 1)

                def turn_p(t):
                    pe.wait_ge(s.p_ready, t + 1)
                    if t >= 1:
                        pe.wait_ge(s.pt_act, t)
                        pe.wait_ge(s.pt_dve, t)
                    for h in range(8):
                        last = nc.tensor.transpose(PS[:, 4 + h // 4, (h % 4) * P:(h % 4 + 1) * P],
                                                   pbuf[:, t % 3, h * P:(h + 1) * P], ident[:, :])
                    last.then_inc(s.pt_psum, 1)

                def weigh(blk):
                    b = blk // (NBLK // B)
                    pe.wait_ge(s.pt_act, 4 * blk + 4)
                    pe.wait_ge(s.pt_dve, 4 * blk + 4)
                    for m in range(KD):
                        if m:
                            pe.wait_ge(s.at_ready, KD * blk + m)
                        elif blk:
                            pe.wait_ge(s.x_done, 4 * blk)
                        for j in range(4):
                            mm(PS[32 * j:32 * j + 32, 6, :], vbd[:, b, 4 * m + j, :], pT[:, blk % 2, 4 * m + j, :],
                               start=True, stop=True)
                        for j in range(4):
                            last = mm(PS[32 * j:32 * j + 32, 7, :], pair_mask[:, :], pT[:, blk % 2, 4 * m + j, :],
                                      start=True, stop=True)
                        last.then_inc(s.av_ready, 1)
                    pe.wait_ge(s.at_ready, KD * (blk + 1))
                    for sub in range(4):
                        for m in range(KD):
                            last = mm(PS[:, 6 + sub // 2, (sub % 2) * D:(sub % 2 + 1) * D],
                                      aT[:, blk % 2, m, sub * P:(sub + 1) * P], wo[:, m, :],
                                      start=(m == 0), stop=(m == KD - 1))
                        if sub % 2:
                            last.then_inc(s.wo_ready, 1)

                scores(0)
                for t in range(NT):
                    if t + 1 < NT:
                        scores(t + 1)
                    turn_p(t)
                    if t % 4 == 3:
                        weigh(t // 4)

            def self_attention():
                pe.wait_ge(load2, LOAD2)
                pe.wait_ge(X[0].x_done, NT)
                for w in range(2):
                    for m in range(KD):
                        for blk in range(NBLK):
                            i = (w * KD + m) * NBLK + blk
                            if i < 4:
                                pe.wait_ge(LN[1].xt_ready, 4 * blk + 4)
                            if i >= 4:
                                pe.wait_ge(rest_ready, i - 3)
                            for k in range(KD):
                                last = mm(PS[:, 4 + i % 4, :], w_qkv[:, k, w * D + m * P:w * D + (m + 1) * P],
                                          xT[:, k, blk * 512:(blk + 1) * 512], start=(k == 0), stop=(k == KD - 1))
                            last.then_inc(qk_psum, 1)
                for t in range(NT):
                    if t >= 4:
                        pe.wait_ge(vs_ready, t - 3)
                    for k in range(KD):
                        last = mm(PS[:, t % 4, 0:D], xT[:, k, t * P:(t + 1) * P], w_qkv[:, k, 2 * D:3 * D],
                                  start=(k == 0), stop=(k == KD - 1))
                    last.then_inc(vs_psum, 1)
                pe.wait_ge(vs_ready, NT)
                pe.wait_ge(rest_ready, 2 * KD * NBLK)
                pe.wait_ge(ones_ready, 1 + NSTK)

                def weigh(group, half):
                    u, kt = divmod(group, QT)
                    b, g = divmod(u, NG)
                    pe.wait_ge(exp_done, 4 * group + 4)
                    if kt == 0 and u >= 1:
                        pe.wait_ge(o_copied, 2 * u)
                    for j in range(4):
                        last = mm(PS[32 * j:32 * j + 32, 6 + half, :], v_and_ones(b * QT + kt, 4 * g + j),
                                  ptb[(4 * group + j) % NPTB][:, half * 512:(half + 1) * 512],
                                  start=(kt == 0), stop=(kt == QT - 1))
                    if half:
                        last.then_inc(av_done, 1)

                def ring_job(job, kind, u, i):
                    if job >= 2:
                        pe.wait_ge(ring_free, job - 1)
                    if kind == "scores":
                        if i == 0:
                            pe.wait_ge(stacked[u % NSTK], 16 * 48 * (u // NSTK + 1))
                        j, qt, half = i // 16, i // 2 % QT, i % 2
                        last = mm(PS[:, 4 + job % 2, :], qstk[u % NSTK][0:KS, j, qt * P:(qt + 1) * P],
                                  kstk[u % NSTK][0:KS, j, half * 512:(half + 1) * 512], start=True, stop=True)
                    elif kind == "maxima":
                        pe.wait_ge(max_joined, u + 1)
                        last = nc.tensor.transpose(PS[0:32, 4 + job % 2, 0:P], mrow[:, :], ident[:, :])
                    else:
                        pe.wait_ge(o_copied, 2 * u + 2)
                        for c in range(4):
                            last = nc.tensor.transpose(PS[:, 4 + job % 2, c * P:(c + 1) * P],
                                                       oT[:, (i * 4 + c) * P:(i * 4 + c + 1) * P], ident[:, :])
                    last.then_inc(ring_full, 1)

                job = 0
                for n in STEPS:
                    u, at_u = divmod(n, 32)
                    kt, j = divmod(at_u, 4)
                    if n >= 4 and n < 32 * NU + 4 and j % 2:
                        weigh(n // 4 - 1, j // 2)
                    jobs = ring_jobs(n)
                    for half in range(2):
                        if jobs:
                            ring_job(job, *jobs.pop(0))
                            job += 1
                        if u >= 0 and u < NU:
                            if half == 0 and at_u == 0:
                                pe.wait_ge(mrow_landed, 48 * (u + 1))
                            if half == 0 and n >= 2:
                                pe.wait_ge(exp_done, n - 1)
                            last = mm(PS[:, 2 * (n % 2) + half, :], kstk[u % NSTK][0:KM, j, kt * P:(kt + 1) * P],
                                      qstk[u % NSTK][0:KM, j, half * 512:(half + 1) * 512], start=True, stop=True)
                    if u >= 0 and u < NU:
                        last.then_inc(st_full, 1)
                    for left in jobs:
                        ring_job(job, *left)
                        job += 1

                for t in range(NT + 1):
                    if t < NT:
                        if t == 0:
                            pe.wait_ge(ring_free, JOBS)
                        if t >= 4:
                            pe.wait_ge(a_ready, t - 3)
                        for k in range(KD):
                            last = nc.tensor.transpose(PS[:, t % 4, k * P:(k + 1) * P],
                                                       attn[:, t, k * P:(k + 1) * P], ident[:, :])
                        last.then_inc(a_turned, 1)
                    if t >= 1:
                        n = t - 1
                        pe.wait_ge(a_ready, n + 1)
                        if n >= 4:
                            pe.wait_ge(x2_ready, n - 3)
                        for k in range(KD):
                            last = mm(PS[:, 4 + n % 4, 0:D], aTs[:, n % 4, k, :], w_self_o[:, k, :],
                                      start=(k == 0), stop=(k == KD - 1))
                        last.then_inc(so_psum, 1)

            def route(n):
                w, width = ((w_route, E0 + 2), (w_u, 1))[n]
                ln = (LN[2], LN[4])[n]
                pe.wait_ge(ln.xt_ready, NT)
                pe.wait_ge(load2, LOAD2)
                if n == 0:
                    pe.wait_ge(x2_ready, NT)
                else:
                    pe.wait_ge(X[1].x_done, NT)
                for t in range(NT):
                    for k in range(KD):
                        last = mm(PS[:, 4, t * width:(t + 1) * width], xT[:, k, t * P:(t + 1) * P], w[:, k, :],
                                  start=(k == 0), stop=(k == KD - 1))
                last.then_inc(r_psum, 1)

            def second_biases(n):
                pe.wait_ge(c_ready[n], 1)
                if n == 0:
                    pe.wait_ge(slot_gelu, NSLOT + 1)
                    pe.wait_ge(slot_y_copied, NSLOT + 2)
                e, c = ((E0R, c0), (E1, c1))[n]
                for t in range(NT):
                    last = nc.tensor.transpose(PS[0:e, t // 4, (t % 4) * P:(t % 4 + 1) * P], c[:, t, :], ident[:, :])
                last.then_inc(F[n].ct_psum, 1)
                pe.wait_ge(F[n].ct_ready, 1)
                b2 = (b2_0, b2_1)[n]
                for t in range(NT):
                    if t >= 4:
                        pe.wait_ge(F[n].b2_done, t - 3)
                    mm(PS[:, 4 + t % 4, 0:D], cT[0:e, t * P:(t + 1) * P], b2[:, :], start=True, stop=True)\
                        .then_inc(F[n].ct_psum, 1)
                pe.wait_ge(F[n].b2_done, NT)

            def dense_expert():
                s = F[0]
                pe.wait_ge(s.weights0, 32)
                for tb in range(9):
                    if tb < 8:
                        for f in range(KF):
                            i = tb * KF + f
                            if i >= 4:
                                pe.wait_ge(s.h_done, H_FREE + i - 3)
                            for k in range(KD):
                                last = mm(PS[:, i % 4, 0:256], rw1[:, k, f * P:(f + 1) * P],
                                          xT[:, k, tb * 256:(tb + 1) * 256], start=(k == 0), stop=(k == KD - 1))
                            last.then_inc(s.h_psum, 1)
                    if tb == 1:
                        pe.wait_ge(r_step, 9)
                        pe.wait_ge(zeros_ready, 2)
                        mm(PS[:, 7, 0:P], before[:, :], rt[7], start=True, stop=True)
                        mm(PS[:, 7, P:2 * P], ones[:, :], rt[7], start=True, stop=True).then_inc(rank_psum, 1)
                    if tb >= 1:
                        tp = tb - 1
                        pe.wait_ge(s.h_done, H_FREE + KF * (tp + 1))
                        for sub in range(2):
                            i = tp * 2 + sub
                            if i >= 2:
                                pe.wait_ge(s.o_free, PAR_O + i - 1)
                            for f in range(KF):
                                last = mm(PS[:, 4 + i % 2, 0:D], rhT[:, tp % 2, f, sub * P:(sub + 1) * P], rw2[:, f, :],
                                          start=(f == 0), stop=(f == KF - 1))
                            last.then_inc(s.o_psum, 1)

            def routed_experts():

                def turn_x(j, par):
                    pe.wait_ge(slot_loaded[par], 8 * (j - par) + 16)
                    for k in range(KD):
                        last = nc.tensor.transpose(PS[:, 6 + par, k * P:(k + 1) * P],
                                                   slot_x[:, par, k * P:(k + 1) * P], ident[:, :])
                    last.then_inc(slot_turned, 1)

                def first(j, par):
                    e = nc.tensor.value_load(expert_of[0:1, bass.ds(j, 1)], min_val=0, max_val=E0 - 1)
                    pe.wait_ge(slot_xt, j + 1)
                    pe.wait_ge(slot_h_copied, j + 1)
                    for c in range(2):
                        for k in range(KD):
                            last = mm(PS[:, c, :], slot_xT[:, par, k, :],
                                      w1_all[:, bass.ds(e, 1), k, c * 512:(c + 1) * 512].rearrange("p a f -> p (a f)"),
                                      start=(k == 0), stop=(k == KD - 1))
                    last.then_inc(slot_h_psum, 1)

                def turn_h(j, par):
                    pe.wait_ge(slot_h_copied, j + 2)
                    pe.wait_ge(slot_gelu, j + 1)
                    for f in range(KF):
                        last = nc.tensor.transpose(PS[:, 2 + f // 4, (f % 4) * P:(f % 4 + 1) * P],
                                                   slot_h[:, par, f * P:(f + 1) * P], ident[:, :])
                    last.then_inc(slot_ht_psum, 1)

                def second(j, par):
                    e = nc.tensor.value_load(expert_of[0:1, bass.ds(j, 1)], min_val=0, max_val=E0 - 1)
                    pe.wait_ge(slot_gelu, j + 2)
                    pe.wait_ge(slot_y_copied, j + 1)
                    for f in range(KF):
                        last = mm(PS[:, 4 + par, 0:D], slot_hT[:, par, f, :],
                                  w2_all[:, bass.ds(e, 1), f, :].rearrange("p a d -> p (a d)"),
                                  start=(f == 0), stop=(f == KF - 1))
                    last.then_inc(slot_y_psum, 1)

                pe.wait_ge(place_step, PLACED)
                pe.wait_ge(w_route_all, 16 * 2 * E0)
                pe.wait_ge(F[0].o_free, PAR_O + NT)
                turn_x(0, 0)
                first(0, 0)
                turn_x(1, 1)
                first(1, 1)
                turn_x(2, 0)
                turn_h(0, 0)
                first(2, 0)
                turn_x(3, 1)
                turn_h(1, 1)
                second(0, 0)

                def turn(i, par, more=True):
                    first(i, par)
                    if more:
                        turn_x(i + 1, 1 - par)
                    turn_h(i - 1, 1 - par)
                    second(i - 2, par)

                with pe.Fori(0, (NSLOT - 5) // 2) as pair:
                    turn(pair * 2 + 3, 1)
                    turn(pair * 2 + 4, 0)
                turn(NSLOT - 2, 1)
                turn(NSLOT - 1, 0, more=False)
                turn_h(NSLOT - 1, 0)
                second(NSLOT - 2, 1)
                second(NSLOT - 1, 0)

            def experts(n, count):
                s = F[n]

                def one(e, par):
                    pe.wait_ge((s.weights0, s.weights1)[par], 32 + 16 * (e - par))
                    for tb in range(NBLK + 1):
                        if tb < NBLK:
                            for f in range(KF):
                                i = tb * KF + f
                                pe.wait_ge(s.h_done, 32 * e + i + 1)
                                for k in range(KD):
                                    last = mm(PS[:, i % 4, :], w1[:, par, k, f * P:(f + 1) * P],
                                              xT[:, k, tb * 512:(tb + 1) * 512], start=(k == 0), stop=(k == KD - 1))
                                last.then_inc(s.h_psum, 1)
                        if tb >= 1:
                            tp = tb - 1
                            pe.wait_ge(s.h_done, 32 * e + H_FREE + KF * (tp + 1))
                            for sub in range(4):
                                i = tp * 4 + sub
                                pe.wait_ge(s.o_free, 16 * e + PAR_O - 3 + i)
                                for f in range(KF):
                                    last = mm(PS[:, 4 + i % 4, 0:D], hT[:, tp % 2, f, sub * P:(sub + 1) * P],
                                              w2[:, par, f, :], start=(f == 0), stop=(f == KF - 1))
                                last.then_inc(s.o_psum, 1)

                with pe.Fori(0, count // 2) as pair:
                    one(pair * 2, 0)
                    one(pair * 2 + 1, 1)
                if count % 2:
                    one(count - 1, 0)

            pe.wait_ge(load, 16 * 11)
            for k in range(KD):
                last = nc.tensor.transpose(PS[:, 7, k * P:(k + 1) * P], ctxm[:, k * P:(k + 1) * P], ident[:, :])
            last.then_inc(ctx_turned, 1)
            turn_norm(0)
            pe.wait_ge(ctx_ready, 3)
            cross(0)
            turn_norm(1)
            self_attention()
            turn_norm(2)
            route(0)
            dense_expert()
            routed_experts()
            second_biases(0)
            turn_norm(3)
            cross(1)
            turn_norm(4)
            route(1)
            second_biases(1)
            experts(1, E1)

        @block.scalar
        def _(act):
            run = nc.scalar.activation

            def evacuate_norm(n, gain=None, bias=None):
                s = LN[n]
                act.wait_ge(s.stats, 2 * NT)
                run(std[:, :], mv[:, :, 1], ACT.Sqrt, bias=eps[:, :]).then_inc(s.std, 1)
                if n == 1:
                    act.wait_ge(s.rstd, 3)
                    run(std[:, :], vtmp[:, :], ACT.Sqrt, bias=eps[:, :]).then_inc(s.std, 1)
                for t in range(NT):
                    act.wait_ge(s.turned, t + 1)
                    dst, src = xT[:, :, t * P:(t + 1) * P], PS[:, t % 4, 0:D].rearrange("p (k t) -> p k t", k=KD)
                    if gain is None:
                        run(dst, src, ACT.Copy).then_inc(s.xt_ready, 1)
                    else:
                        for k in range(KD):
                            last = run(dst[:, k, :], src[:, k, :], ACT.Identity, bias=cols[:, bias, k:k + 1],
                                       scale=cols[:, gain, k:k + 1])
                        last.then_inc(s.xt_ready, 1)

            def cross(n):
                s = X[n]
                bq, bk = ((BQ0, BK0), (BQ1, BK1))[n]
                act.wait_ge(s.kv_psum, 1)
                for m in range(KD):
                    last = run(kT[:, m, :], PS[:, 4, m * P:(m + 1) * P], ACT.Identity, bias=cols[:, bk, m:m + 1])
                last.then_inc(s.k_ready, 1)
                for i in range(KD * NBLK):
                    m, blk = divmod(i, NBLK)
                    act.wait_ge(s.q_psum, i + 1)
                    run(qT[:, m, blk * 512:(blk + 1) * 512], PS[:, 6 + i % 2, :], ACT.Identity,
                        bias=cols[:, bq, m:m + 1]).then_inc(s.q_ready, 1)

                def expo(t):
                    act.wait_ge(s.s_shifted, t + 1)
                    run(pbuf[:, t % 3, :], pbuf[:, t % 3, :], ACT.Exp, scale=SCALE).then_inc(s.p_ready, 1)

                def evacuate(t):
                    blk, sub = divmod(t, 4)
                    act.wait_ge(s.pt_psum, t + 1)
                    if sub == 0 and blk >= 2:
                        act.wait_ge(s.av_ready, KD * (blk - 1))
                    run(pT[:, blk % 2, 0:4, sub * P:(sub + 1) * P],
                        PS[:, 4, :].rearrange("p (h q) -> p h q", h=4), ACT.Copy).then_inc(s.pt_act, 1)

                expo(0)
                for t in range(NT):
                    if t + 1 < NT:
                        expo(t + 1)
                    evacuate(t)

            def self_attention():
                def high(i):
                    w, m, blk = i // 8, i // 4 % 2, i % 4
                    act.wait_ge(qk_psum, i + 1)
                    run(split[w][:, 0, m, blk * 512:(blk + 1) * 512], PS[:, 4 + i % 4, :], ACT.Identity,
                        bias=cols[:, (BQS, BKS)[w], m:m + 1]).then_inc(high_ready, 1)

                def middle(i):
                    w, m, blk = i // 8, i // 4 % 2, i % 4
                    act.wait_ge(rest_ready, i + 1)
                    run(split[w][:, 1, m, blk * 512:(blk + 1) * 512], rres[:, i % 2, :], ACT.Copy)\
                        .then_inc(mid_ready, 1)

                n = 2 * KD * NBLK
                for i in range(n):
                    high(i)
                    if i >= 1:
                        middle(i - 1)
                middle(n - 1)
                for n in range(32 * NU + 5):
                    if n >= 32 and n % 32 == 4:
                        u = n // 32 - 1
                        act.wait_ge(av_done, QT * (u + 1))
                        if u >= 1:
                            act.wait_ge(ring_free, jobs_before(n - 32 + 4))
                        run(oT[:, 512:1024], PS[:, 7, :], ACT.Copy).then_inc(o_copied, 1)
                    if n < 32 * NU:
                        act.wait_ge(st_full, n + 1)
                        if n >= NPTB:
                            act.wait_ge(av_done, (n - NPTB) // 4 + 1)
                        run(ptb[n % NPTB], PS[:, 2 * (n % 2):2 * (n % 2) + 2, :].rearrange("p a q -> p (a q)"),
                            ACT.Exp, scale=SCALE).then_inc(exp_done, 1)
                for t in range(NT):
                    act.wait_ge(a_turned, t + 1)
                    if t >= 4:
                        act.wait_ge(so_psum, t - 3)
                    run(aTs[:, t % 4, :, :], PS[:, t % 4, 0:D].rearrange("p (k q) -> p k q", k=KD), ACT.Copy)\
                        .then_inc(a_ready, 1)

            def route(n):
                if n == 0:
                    act.wait_ge(r_step, 2)
                    run(rt[2], rt[1], ACT.Exp).then_inc(r_exp, 1)
                    act.wait_ge(r_step, 5)
                    run(rt[4][:, 0:2 * NT], rt[3][:, 0:2 * NT], ACT.Exp).then_inc(r_exp, 1)
                else:
                    act.wait_ge(r_step1, 1)
                    run(rt[1][:, 0:NT], rt[0][:, 0:NT], ACT.Exp, scale=-1.0).then_inc(r_exp1, 1)

            def turned_weights(n):
                e = (E0R, E1)[n]
                act.wait_ge(F[n].ct_psum, 1)
                run(cT[0:e, :], PS[0:e, 0:4, :].rearrange("p a q -> p (a q)"), ACT.Copy).then_inc(F[n].ct_ready, 1)

            def experts(n, count):
                s = F[n]
                b1 = (b1_0, b1_1)[n]
                func = (ACT.Gelu, ACT.Relu)[n]

                def one(e):
                    for i in range(NBLK * KF):
                        tb, f = divmod(i, KF)
                        act.wait_ge(s.h_psum, 32 * e + i + 1)
                        if f == 0:
                            act.wait_ge(s.o_psum, PAR_O + 16 * e + 4 * (tb - 1))
                        run(hT[:, tb % 2, f, :], PS[:, i % 4, :], func,
                            bias=b1[:, e, f:f + 1]).then_inc(s.h_done, 1)

                for e in range(count):
                    one(e)

            def dense_expert():
                s = F[0]
                for i in range(8 * KF):
                    tb, f = divmod(i, KF)
                    act.wait_ge(s.h_psum, i + 1)
                    if f == 0 and tb >= 2:
                        act.wait_ge(s.o_psum, PAR_O + 2 * (tb - 1))
                    run(rhT[:, tb % 2, f, :], PS[:, i % 4, 0:256], ACT.Gelu, bias=b1_0[:, E0, f:f + 1])\
                        .then_inc(s.h_done, 1)

            def routed_experts():
                def evacuate(j):
                    act.wait_ge(slot_turned, j + 1)
                    if j >= 2:
                        act.wait_ge(slot_h_psum, j - 1)
                    for k in range(KD):
                        last = run(slot_xT[:, j % 2, k, :], PS[:, 6 + j % 2, k * P:(k + 1) * P], ACT.Identity,
                                   bias=cols[:, B2, k:k + 1], scale=cols[:, G2, k:k + 1])
                    last.then_inc(slot_xt, 1)

                def gelu(j):
                    act.wait_ge(slot_ht_psum, j + 1)
                    act.wait_ge(slot_b1_ready, j + 1)
                    if j >= 2:
                        act.wait_ge(slot_y_psum, j - 1)
                    for f in range(KF):
                        last = run(slot_hT[:, j % 2, f, :], PS[:, 2 + f // 4, (f % 4) * P:(f % 4 + 1) * P], ACT.Gelu,
                                   bias=slot_b1[:, j % 2, f:f + 1])
                    last.then_inc(slot_gelu, 1)

                evacuate(0)
                evacuate(1)
                for i in range(1, NSLOT + 1):
                    if i + 1 < NSLOT:
                        evacuate(i + 1)
                    gelu(i - 1)

            act.wait_ge(load, 16 * 11)
            act.wait_ge(ctx_turned, 1)
            run(ctxT[:, :, :], PS[:, 7, 0:D].rearrange("p (k c) -> p k c", k=KD), ACT.Copy).then_inc(ctx_ready, 1)
            for a in range(2):
                run(ctxT2[:, :, :, a, :], PS[:, 7, 0:D].rearrange("p (k b c) -> p k b c", k=KD, b=B), ACT.Copy)\
                    .then_inc(ctx_ready, 1)
            act.wait_ge(const, 1)
            evacuate_norm(0)
            cross(0)
            evacuate_norm(1, G1, B1)
            self_attention()
            evacuate_norm(2, G2, B2)
            act.wait_ge(load2, LOAD2)
            route(0)
            dense_expert()
            routed_experts()
            turned_weights(0)
            evacuate_norm(3)
            cross(1)
            evacuate_norm(4)
            route(1)
            turned_weights(1)
            experts(1, E1)

        @block.vector
        def _(dve):
            v = nc.vector

            def norm(n, src, ready, before, at_least=None):
                s = LN[n]
                buf = xn_self if n == 1 else xn
                for t in range(NT):
                    dve.wait_ge(ready, before + (t + 1 if at_least is None else at_least))
                    v.bn_stats(stats[:, t, :], src[:, t, :]).then_inc(s.stats, 1)
                dve.wait_ge(s.stats, NT)
                for t in range(NT):
                    v.bn_aggr(mv[:, t, :], stats[:, t, :]).then_inc(s.stats, 1)
                dve.wait_ge(s.std, 1)
                v.reciprocal(rstd[:, :], std[:, :]).then_inc(s.rstd, 1)
                dve.wait_ge(s.rstd, 1)
                scale, steps = rstd, 1
                if n == 1:
                    v.tensor_tensor(vtmp[:, :], mv[:, :, 1], rstd[:, :], ALU.mult).then_inc(s.rstd, 1)
                    dve.wait_ge(s.rstd, 2)
                    v.tensor_tensor(vtmp[:, :], vtmp[:, :], rstd[:, :], ALU.mult).then_inc(s.rstd, 1)
                    dve.wait_ge(s.std, 2)
                    v.reciprocal(rstd2[:, :], std[:, :]).then_inc(s.rstd, 1)
                    dve.wait_ge(s.rstd, 4)
                    v.tensor_tensor(rstd2[:, :], rstd2[:, :], rstd[:, :], ALU.mult).then_inc(s.rstd, 1)
                    dve.wait_ge(s.rstd, 5)
                    scale = rstd2
                for t in range(NT):
                    if t >= 4:
                        dve.wait_ge(s.turned, t - 3)
                    v.tensor_scalar(buf[:, t % 4, :], src[:, t, :], mv[:, t, 0:1], scale[:, t:t + 1],
                                    ALU.subtract, ALU.mult).then_inc(s.normed, 1)

            def cross(n):
                s = X[n]
                bv = (BV0, BV1)[n]
                dve.wait_ge(s.k_ready, 1)
                for b in range(B):
                    for m in range(KD):
                        v.tensor_tensor(kbd[:, b, m, :].rearrange("p (h c) -> p h c", h=8),
                                        kT[:, m, b * CTX:(b + 1) * CTX].unsqueeze(1).broadcast_to([P, 8, CTX]),
                                        head_mask[:, :].unsqueeze(2).broadcast_to([P, 8, CTX]), ALU.mult)\
                            .then_inc(s.kv_spread, 1)
                dve.wait_ge(s.kv_psum, 2)
                v.tensor_tensor(vb, PS[:, 5, :].rearrange("p (b d) -> p b d", b=B),
                                rows[:, bv, :].unsqueeze(1).broadcast_to([P, B, D]), ALU.add).then_inc(s.v_biased, 1)
                dve.wait_ge(s.v_biased, 1)
                for b in range(B):
                    v.tensor_tensor(vbd[:, b, :, :], vb[:, b, :].rearrange("p (h c) -> p h c", h=8),
                                    pair_mask[:, :].unsqueeze(1).broadcast_to([P, 8, 32]), ALU.mult)\
                        .then_inc(s.kv_spread, 1)

                def shift(t):
                    dve.wait_ge(s.s_ready, t + 1)
                    sc = PS[:, 2 * (t % 2):2 * (t % 2) + 2, :].rearrange("p m (h c) -> p (m h) c", c=CTX)
                    v.tensor_reduce(mx[:, t % 3, :], sc, AX_X, ALU.max).then_inc(s.max_ready, 1)
                    dve.wait_ge(s.max_ready, t + 1)
                    if t >= 3:
                        dve.wait_ge(s.pt_psum, t - 2)
                    v.tensor_tensor(pbuf[:, t % 3, :].rearrange("p (h c) -> p h c", h=H), sc,
                                    mx[:, t % 3, :].unsqueeze(2).broadcast_to([P, H, CTX]), ALU.subtract)\
                        .then_inc(s.s_shifted, 1)

                shift(0)
                for t in range(NT):
                    blk, sub = divmod(t, 4)
                    if t + 1 < NT:
                        shift(t + 1)
                    dve.wait_ge(s.pt_psum, t + 1)
                    if sub == 0 and blk >= 2:
                        dve.wait_ge(s.av_ready, KD * (blk - 1))
                    v.tensor_copy(pT[:, blk % 2, 4:8, sub * P:(sub + 1) * P],
                                  PS[:, 5, :].rearrange("p (h q) -> p h q", h=4)).then_inc(s.pt_dve, 1)
                    if sub < 3:
                        continue
                    for m in range(KD):
                        i = KD * blk + m
                        dve.wait_ge(s.av_ready, i + 1)
                        v.reciprocal(rden[:, m, :], PS[:, 7, :]).then_inc(s.recip_ready, 1)
                        dve.wait_ge(s.recip_ready, i + 1)
                        v.tensor_tensor(aT[:, blk % 2, m, :], PS[:, 6, :], rden[:, m, :], ALU.mult)\
                            .then_inc(s.at_ready, 1)
                    dve.wait_ge(s.x_biased, 1)
                    for c in range(2):
                        tt = 4 * blk + 2 * c
                        dve.wait_ge(s.wo_ready, 2 * blk + c + 1)
                        v.tensor_tensor(x[:, tt:tt + 2, :], x[:, tt:tt + 2, :],
                                        PS[:, 6 + c, :].rearrange("p (t d) -> p t d", t=2), ALU.add)\
                            .then_inc(s.x_done, 2)

            def self_attention():
                def rest(i):
                    w, m, blk = i // 8, i // 4 % 2, i % 4
                    dve.wait_ge(high_ready, i + 1)
                    if i >= 2:
                        dve.wait_ge(mid_ready, i - 1)
                        dve.wait_ge(low_ready, i - 1)
                    v.scalar_tensor_tensor(out=rres[:, i % 2, :], in0=PS[:, 4 + i % 4, :],
                                           scalar=cols[:, (BQS, BKS)[w], m:m + 1],
                                           in1=split[w][:, 0, m, blk * 512:(blk + 1) * 512],
                                           op0=ALU.add, op1=ALU.subtract).then_inc(rest_ready, 1)

                def low(i):
                    w, m, blk = i // 8, i // 4 % 2, i % 4
                    dve.wait_ge(mid_ready, i + 1)
                    v.tensor_tensor(split[w][:, 2, m, blk * 512:(blk + 1) * 512], rres[:, i % 2, :],
                                    split[w][:, 1, m, blk * 512:(blk + 1) * 512], ALU.subtract).then_inc(low_ready, 1)

                n = 2 * KD * NBLK
                for i in range(n):
                    rest(i)
                    if i >= 1:
                        low(i - 1)
                low(n - 1)
                dve.wait_ge(load, 16 * 11)
                for t in range(NT):
                    dve.wait_ge(vs_psum, t + 1)
                    v.tensor_tensor(vones[:, t, :, :].rearrange("p h (a c) -> p h a c", a=3)[:, :, 0::2, :],
                                    PS[:, t % 4, 0:D].rearrange("p (h a c) -> p h a c", h=8, a=2),
                                    rows[:, BVS, :].rearrange("p (h a c) -> p h a c", h=8, a=2), ALU.add)\
                        .then_inc(vs_ready, 1)

                def maximum(job, u, i):
                    if i == 0 and u >= 2:
                        dve.wait_ge(max_joined, u - 1)
                    v.tensor_reduce(mpart[:, u % 2, i // 2, i % 2:i % 2 + 1], PS[:, 4 + job % 2, :], AX_X, ALU.max)\
                        .then_inc(ring_free, 1)
                    if i == 63:
                        dve.wait_ge(ring_free, job + 1)
                        v.tensor_tensor(mrow, mpart[:, u % 2, :, 0], mpart[:, u % 2, :, 1], ALU.max)\
                            .then_inc(max_joined, 1)

                def split_maxima(job, u):
                    if u >= 1:
                        dve.wait_ge(mrow_landed, 48 * u)
                    ps = PS[0:32, 4 + job % 2, 0:P]
                    v.tensor_scalar(msplit[0:32, 0, :], ps, -1.0, None, ALU.mult).then_inc(msplit_tmp, 1)
                    dve.wait_ge(msplit_tmp, 2 * u + 1)
                    v.scalar_tensor_tensor(out=mres[0:32, :], in0=ps, scalar=-1.0, in1=msplit[0:32, 0, :],
                                           op0=ALU.mult, op1=ALU.subtract).then_inc(ring_free, 1)
                    dve.wait_ge(ring_free, job + 1)
                    v.tensor_copy(msplit[0:32, 1, :], mres[0:32, :]).then_inc(msplit_tmp, 1)
                    dve.wait_ge(msplit_tmp, 2 * u + 2)
                    v.tensor_tensor(msplit[0:32, 2, :], mres[0:32, :], msplit[0:32, 1, :], ALU.subtract)\
                        .then_inc(msplit_ready, 1)

                def output(job, u, half):
                    b, g = divmod(u, NG)
                    o = PS[:, 4 + job % 2, :].rearrange("p (c h a d) -> p c h a d", c=4, h=2, a=4)
                    r = rsum[:, half, :].rearrange("p (c h a) -> p c h a", c=4, h=2)
                    v.reciprocal(r, o[:, :, :, 1:3, 0]).then_inc(rsum_ready, 1)
                    dve.wait_ge(rsum_ready, 2 * u + half + 1)
                    t0 = b * QT + 4 * half
                    for pair in range(2):
                        c = 64 * g + 32 * pair
                        last = v.tensor_tensor(
                            attn[:, t0:t0 + 4, c:c + 32].rearrange("p c (a d) -> p c a d", a=2),
                            o[:, :, pair, 0::3, :], r[:, :, pair, :].unsqueeze(3).broadcast_to([P, 4, 2, DH]),
                            ALU.mult)
                    last.then_inc(ring_free, 1)

                job = 0
                for n in STEPS:
                    if n >= 32 and n % 32 == 4:
                        dve.wait_ge(av_done, QT * (n // 32))
                        v.tensor_copy(oT[:, 0:512], PS[:, 6, :]).then_inc(o_copied, 1)
                    for kind, u, i in ring_jobs(n):
                        dve.wait_ge(ring_full, job + 1)
                        if kind == "scores":
                            maximum(job, u, i)
                        elif kind == "maxima":
                            split_maxima(job, u)
                        else:
                            output(job, u, i)
                        job += 1
                assert job == JOBS
                for t in range(NT):
                    v.tensor_scalar(x2[:, t, :], x[:, t, :], mv[:, t, 0:1], rstd[:, t:t + 1],
                                    ALU.subtract, ALU.mult).then_inc(y_ready, 1)
                for t in range(NT):
                    if t % 4 == 0:
                        dve.wait_ge(y_biased, t // 4 + 1)
                    dve.wait_ge(so_psum, t + 1)
                    v.tensor_tensor(x2[:, t, :], x2[:, t, :], PS[:, 4 + t % 4, 0:D], ALU.add).then_inc(x2_ready, 1)

            def route_experts():
                n = [0]

                def link(ins):
                    n[0] += 1
                    ins.then_inc(r_step, 1)
                    dve.wait_ge(r_step, n[0])

                def wide(a, c=E0):
                    return a[:, 0:NT * c].rearrange("p (t e) -> p t e", t=NT)

                def over(a, c=E0):
                    return a.unsqueeze(2).broadcast_to([P, NT, c])

                dve.wait_ge(r_psum, 1)
                L = PS[:, 4, 0:NT * (E0 + 2)].rearrange("p (t e) -> p t e", t=NT)
                top = rt[0][:, 0:NT]
                link(v.tensor_reduce(top, L[:, :, 0:E0], AX_X, ALU.max))
                link(v.tensor_tensor(wide(rt[1]), L[:, :, 0:E0], over(top), ALU.subtract))
                link(v.tensor_tensor(wide(rt[5], 2), L[:, :, E0:E0 + 2],
                                     coef_b[:, :].unsqueeze(1).broadcast_to([P, NT, 2]), ALU.add))
                link(v.tensor_reduce(rt[0][:, NT:2 * NT], wide(rt[5], 2), AX_X, ALU.max))
                link(v.tensor_tensor(wide(rt[3], 2), wide(rt[5], 2), over(rt[0][:, NT:2 * NT], 2), ALU.subtract))
                link(v.tensor_scalar(rt[6], rt[1], 0.0, None, ALU.is_ge))
                link(v.tensor_tensor(wide(rt[6]), wide(rt[6]), first8[:, :].unsqueeze(1).broadcast_to([P, NT, E0]),
                                     ALU.mult))
                link(v.tensor_reduce(rt[0][:, 2 * NT:3 * NT], wide(rt[6]), AX_X, ALU.max))
                link(v.tensor_tensor(wide(rt[7]), wide(rt[6]), over(rt[0][:, 2 * NT:3 * NT]), ALU.is_equal))
                dve.wait_ge(r_exp, 2)
                link(v.tensor_reduce(rt[0][:, 3 * NT:4 * NT], wide(rt[2]), AX_X, ALU.add))
                link(v.reciprocal(rt[0][:, 4 * NT:5 * NT], rt[0][:, 3 * NT:4 * NT]))
                link(v.tensor_reduce(rt[0][:, 5 * NT:6 * NT], wide(rt[4], 2), AX_X, ALU.add))
                link(v.reciprocal(rt[0][:, 6 * NT:7 * NT], rt[0][:, 5 * NT:6 * NT]))
                link(v.tensor_tensor(wide(rt[5], 2), wide(rt[4], 2), over(rt[0][:, 6 * NT:7 * NT], 2), ALU.mult))
                link(v.tensor_tensor(rt[0][:, 7 * NT:8 * NT], rt[0][:, 4 * NT:5 * NT], wide(rt[5], 2)[:, :, 0], ALU.mult))
                link(v.tensor_copy(c0[:, :, E0], wide(rt[5], 2)[:, :, 1]))
                v.tensor_tensor(c0[:, :, 0:E0], wide(rt[7]), over(rt[0][:, 7 * NT:8 * NT]), ALU.mult)\
                    .then_inc(c_ready[0], 1)
                dve.wait_ge(c_ready[0], 1)

            def route_steps():
                n = [0]

                def link(ins):
                    n[0] += 1
                    ins.then_inc(r_step1, 1)
                    dve.wait_ge(r_step1, n[0])

                dve.wait_ge(r_psum, 2)
                link(v.tensor_scalar(rt[0][:, 0:NT], PS[:, 4, 0:NT], bu[:, 0:1], None, ALU.add))
                dve.wait_ge(r_exp1, 1)
                link(v.tensor_scalar(rt[2][:, 0:NT], rt[1][:, 0:NT], 1.0, None, ALU.add))
                link(v.reciprocal(rt[3][:, 0:NT], rt[2][:, 0:NT]))
                link(v.tensor_scalar(rt[4][:, 0:NT], rt[3][:, 0:NT], float(E1), None, ALU.mult))

                def tokens(a):
                    return a[:, 0:NT].unsqueeze(2).broadcast_to([P, NT, E1])

                def steps(a):
                    return a[:, :].unsqueeze(1).broadcast_to([P, NT, E1])

                w = rt[5][:, 0:NT * E1].rearrange("p (t e) -> p t e", t=NT)
                on = rt[6][:, 0:NT * E1].rearrange("p (t e) -> p t e", t=NT)
                link(v.tensor_tensor(w, tokens(rt[3]), steps(step_inv), ALU.mult))
                link(v.tensor_tensor(on, tokens(rt[4]), steps(step_thr), ALU.is_gt))
                v.tensor_tensor(c1[:, :, :], w, on, ALU.mult).then_inc(c_ready[1], 1)
                dve.wait_ge(c_ready[1], 1)

            def place_tokens():
                n = [0]

                def link(ins):
                    n[0] += 1
                    ins.then_inc(place_step, 1)
                    dve.wait_ge(place_step, n[0])

                def by_tile(a):
                    return a.rearrange("p (t e) -> p t e", t=NT)

                dve.wait_ge(rank_psum, 1)
                rank, total, hot = by_tile(PS[:, 7, 0:P]), by_tile(PS[:, 7, P:2 * P]), by_tile(rt[7])
                link(v.tensor_copy(grow[:, 0], total))
                a = 0
                for far in (1, 2, 4, 8):
                    link(v.tensor_tensor(grow[:, 1 - a, far:, :], grow[:, a, far:, :], grow[:, a, :NT - far, :], ALU.add))
                    link(v.tensor_copy(grow[:, 1 - a, :far, :], grow[:, a, :far, :]))
                    a = 1 - a
                link(v.tensor_tensor(grow[:, 1], grow[:, 0], total, ALU.subtract))
                count = grow[:, 0, NT - 1, :]
                need = fits[:, 0:E0 * NT].rearrange("p (e i) -> p e i", e=E0)
                link(v.tensor_tensor(need, count.unsqueeze(2).broadcast_to([P, E0, NT]),
                                     tile_edges[:, :].unsqueeze(1).broadcast_to([P, E0, NT]), ALU.is_gt))
                link(v.tensor_reduce(sizes[:, 0, :], need, AX_X, ALU.add))
                for m, far in enumerate((1, 2, 4)):
                    link(v.tensor_tensor(sizes[:, m + 1, far:], sizes[:, m, far:], sizes[:, m, :E0 - far], ALU.add))
                    link(v.tensor_copy(sizes[:, m + 1, :far], sizes[:, m, :far]))
                ends = sizes[:, 3, :]
                link(v.tensor_tensor(sizes[:, 4, :], ends, sizes[:, 0, :], ALU.subtract))
                link(v.scalar_tensor_tensor(out=grow[:, 0], in0=sizes[:, 4, :].unsqueeze(1).broadcast_to([P, NT, E0]),
                                            scalar=float(P), in1=grow[:, 1], op0=ALU.mult, op1=ALU.add))
                link(v.tensor_tensor(grow[:, 1], grow[:, 0], rank, ALU.add))
                link(v.tensor_tensor(grow[:, 0], grow[:, 1], hot, ALU.mult))
                link(v.tensor_reduce(posf[:, :], grow[:, 0], AX_X, ALU.add))
                over = fits[:, :].rearrange("p (j e) -> p j e", j=NSLOT)
                link(v.tensor_tensor(over, ends.unsqueeze(1).broadcast_to([P, NSLOT, E0]),
                                     slot_index[:, :].unsqueeze(2).broadcast_to([P, NSLOT, E0]), ALU.is_le))
                link(v.tensor_reduce(eidf[:, :], over, AX_X, ALU.add))
                link(v.tensor_scalar(expert_of[:, :], eidf[:, :], float(E0 - 1), None, ALU.min))
                link(v.tensor_copy(slot_of[:, :], posf[:, :]))
                assert n[0] == PLACED, n[0]

            def dense_combine():
                s = F[0]
                for t in range(NT):
                    dve.wait_ge(s.o_psum, PAR_O + t + 1)
                    v.scalar_tensor_tensor(out=x[:, t, :], in0=PS[:, 4 + t % 2, 0:D], scalar=c0[:, t, E0:E0 + 1],
                                           in1=x[:, t, :], op0=ALU.mult, op1=ALU.add).then_inc(s.o_free, 1)
                dve.wait_ge(s.o_free, PAR_O + NT)

            def routed_experts():
                def hidden(j, par):
                    if not isinstance(j, int) or j >= 2:
                        dve.wait_ge(slot_ht_psum, j - 1)
                        dve.wait_ge(slot_gelu, j)
                    e = nc.vector.value_load(expert_of[0:1, bass.ds(j, 1)], min_val=0, max_val=E0 - 1)
                    v.tensor_copy(slot_b1[:, par, :], b1_0[:, bass.ds(e, 1), :].rearrange("p a f -> p (a f)"))\
                        .then_inc(slot_b1_ready, 1)
                    dve.wait_ge(slot_h_psum, j + 1)
                    v.tensor_copy(slot_h[:, par, :], PS[:, 0:2, :].rearrange("p a f -> p (a f)"))\
                        .then_inc(slot_h_copied, 1)

                def output(j, par):
                    if not isinstance(j, int) or j >= 2:
                        dve.wait_ge(slot_stored[par], 8 * (j - par))
                    dve.wait_ge(slot_y_psum, j + 1)
                    v.tensor_copy(slot_y[:, par, :], PS[:, 4 + par, 0:D]).then_inc(slot_y_copied, 1)

                hidden(0, 0)
                hidden(1, 1)
                hidden(2, 0)
                output(0, 0)
                hidden(3, 1)
                output(1, 1)
                with dve.Fori(0, (NSLOT - 5) // 2) as pair:
                    hidden(pair * 2 + 4, 0)
                    output(pair * 2 + 2, 0)
                    hidden(pair * 2 + 5, 1)
                    output(pair * 2 + 3, 1)
                hidden(NSLOT - 1, 0)
                for j in range(NSLOT - 3, NSLOT):
                    output(j, j % 2)

            def routed_combine():
                for t in range(NT):
                    dve.wait_ge(gathered[t // 4], 64)
                    v.scalar_tensor_tensor(out=x[:, t, :], in0=gathered_y[:, t, :],
                                           scalar=rt[0][:, 7 * NT + t:7 * NT + t + 1], in1=x[:, t, :],
                                           op0=ALU.mult, op1=ALU.add).then_inc(routed_done, 1)

            def second_biases(n):
                for t in range(NT):
                    dve.wait_ge(F[n].ct_psum, t + 2)
                    v.tensor_tensor(x[:, t, :], x[:, t, :], PS[:, 4 + t % 4, 0:D], ALU.add).then_inc(F[n].b2_done, 1)
                dve.wait_ge(F[n].b2_done, NT)

            def experts(n, count):
                s = F[n]
                c = (c0, c1)[n]

                def one(e):
                    for t in range(NT):
                        dve.wait_ge(s.o_psum, PAR_O + 16 * e + t + 1)
                        dve.wait_ge(s.o_free, PAR_O - 15 + 16 * e + t)
                        v.scalar_tensor_tensor(out=x[:, t, :], in0=PS[:, 4 + t % 4, 0:D],
                                               scalar=c[:, t, bass.ds(e, 1)], in1=x[:, t, :],
                                               op0=ALU.mult, op1=ALU.add).then_inc(s.o_free, 1)

                with dve.Fori(0, count) as e:
                    one(e)

            dve.wait_ge(load, 16 * 11)
            norm(0, x, load, 16 * 11, 0)
            cross(0)
            norm(1, x, X[0].x_done, 0)
            self_attention()
            norm(2, x2, x2_ready, 0)
            dve.wait_ge(load2, LOAD2)
            route_experts()
            dve.wait_ge(x_joined, 1)
            for t in range(NT):
                v.tensor_scalar(x2[:, t, :], x2[:, t, :], mv[:, t, 0:1], rstd[:, t:t + 1],
                                ALU.subtract, ALU.mult).then_inc(x2_normed, 1)
            place_tokens()
            dense_combine()
            routed_experts()
            second_biases(0)
            routed_combine()
            norm(3, x, routed_done, 0)
            cross(1)
            norm(4, x, X[1].x_done, 0)
            route_steps()
            second_biases(1)
            experts(1, E1)

        @block.gpsimd
        def _(pool):
            g = nc.gpsimd
            g.memset(eps[:, :], EPS).then_inc(const, 1)
            pool.wait_ge(const, 1)
            g.memset(zeros[:, :], 0.0).then_inc(zeros_ready, 1)
            pool.wait_ge(zeros_ready, 1)
            g.memset(ones[:, :], 1.0).then_inc(zeros_ready, 1)
            g.memset(credit[:, 6:7], 0.0).then_inc(slot_h_copied, 1)
            g.memset(credit[:, 7:8], 0.0).then_inc(slot_gelu, 1)
            g.memset(credit[:, 8:9], 0.0).then_inc(slot_y_copied, 2)
            for n in range(2):
                g.memset(credit[:, 3 * n:3 * n + 1], 0.0).then_inc(F[n].h_done, H_FREE)
                g.memset(credit[:, 3 * n + 1:3 * n + 2], 0.0).then_inc(F[n].o_psum, PAR_O)
                g.memset(credit[:, 3 * n + 2:3 * n + 3], 0.0).then_inc(F[n].o_free, PAR_O)

            def bias(n, row):
                pool.wait_ge(LN[3 * n].normed, NT)
                pool.wait_ge(load, 16 * 11)
                g.tensor_tensor(x[:, :, :], x[:, :, :], rows[:, row, :].unsqueeze(1).broadcast_to([P, NT, D]), ALU.add)\
                    .then_inc(X[n].x_biased, 1)

            bias(0, BO0)
            pool.wait_ge(X[0].x_done, NT)
            g.memset(vones[:, :, :, 16:32], 1.0).then_inc(ones_ready, 1)
            for n in range(NSTK):
                pool.wait_ge(ones_ready, n + 1)
                g.memset(kstk[n][KS:KM, :, :], 1.0).then_inc(ones_ready, 1)
            for c in range(4):
                pool.wait_ge(y_ready, 4 * c + 4)
                g.tensor_tensor(x2[:, 4 * c:4 * c + 4, :], x2[:, 4 * c:4 * c + 4, :],
                                rows[:, BOS, :].unsqueeze(1).broadcast_to([P, 4, D]), ALU.add).then_inc(y_biased, 1)
            pool.wait_ge(x2_ready, NT)
            g.tensor_tensor(x[:, :, :], x[:, :, :], x2, ALU.add).then_inc(x_joined, 1)
            pool.wait_ge(slots_zeroed, 16)
            pool.wait_ge(x2_normed, NT)
            pool.wait_ge(place_step, PLACED)
            for t in range(NT):
                g.indirect_dma_start(slots_in, bass.IndirectOffsetOnAxis(ap=slot_of[:, t:t + 1], axis=0),
                                     x2[:, t, :], None).then_inc(scattered, 16)
            pool.wait_ge(slot_y_psum, NSLOT)
            pool.wait_ge(slot_stored[0], 16 * (NSLOT + 1) // 2)
            pool.wait_ge(slot_stored[1], 16 * (NSLOT // 2))
            for t in range(NT):
                g.indirect_dma_start(gathered_y[:, t, :], None, slots_out,
                                     bass.IndirectOffsetOnAxis(ap=slot_of[:, t:t + 1], axis=0))\
                    .then_inc(gathered[t // 4], 16)
            bias(1, BO1)


def lay_out(i):
    import numpy as np

    f = {k: np.ascontiguousarray(v) for k, v in i.items()}
    col = lambda a: a.reshape(KD, P).T
    p = np.arange(P)
    step = (np.arange(E1)[None, :] - p[:, None]) % E1
    cols = ["L0_xattn_bq", "L0_xattn_bk", None, None, "L1_xattn_bq", "L1_xattn_bk", "L0_ffn_ln1_g", "L0_ffn_ln1_b",
            "L0_ffn_ln2_g", "L0_ffn_ln2_b"]
    bqkv = f["L0_ffn_bqkv"]
    a = {
        "x": f["x"].reshape(T, D), "ctx": f["ctx_1024"].reshape(B * CTX, D),
        "ident": np.eye(P, dtype=np.float32),
        "head_mask": (p[:, None] // 16 == np.arange(8)[None, :]).astype(np.float32),
        "pair_mask": (p[:, None] // 64 == np.arange(32)[None, :] // 16).astype(np.float32),
        "cols": np.stack([col(f[n]) if n else col(bqkv[(k - 2) * D:(k - 1) * D]) for k, n in enumerate(cols)], axis=1),
        "rows": np.stack([f["L0_xattn_bv"], f["L0_xattn_bo"], bqkv[2 * D:], f["L0_ffn_bo"], f["L1_xattn_bv"],
                          f["L1_xattn_bo"]]),
        "Wqkv": f["L0_ffn_Wqkv"], "WoS": f["L0_ffn_Wo"],
        "w_route": np.concatenate([f["L0_ffn_gate_w"], f["L0_ffn_coef_w"]], axis=1),
        "w_u": col(f["L1_ffn_Wu"]), "coef_b": f["L0_ffn_coef_b"], "bu": f["L1_ffn_bu"],
        "b1_0": np.concatenate([f["L0_ffn_b1"], f["L0_ffn_rb1"][None]]).reshape(E0R, KF, P).transpose(2, 0, 1),
        "b1_1": f["L1_ffn_b1"].reshape(E1, KF, P).transpose(2, 0, 1),
        "b2_0": np.concatenate([f["L0_ffn_b2"], f["L0_ffn_rb2"][None]]), "b2_1": f["L1_ffn_b2"],
        "W1_0": np.concatenate([f["L0_ffn_W1"], f["L0_ffn_rW1"][None]]),
        "W2_0": np.concatenate([f["L0_ffn_W2"], f["L0_ffn_rW2"][None]]),
        "W1_1": f["L1_ffn_W1"], "W2_1": f["L1_ffn_W2"],
        "step_inv": (1.0 / (step + 1)).astype(np.float32),
        "step_thr": np.where(step == 0, -1, step).astype(np.float32),
        "before": (p[:, None] < p[None, :]).astype(np.float32),
        "tile_edges": np.broadcast_to(P * np.arange(NT, dtype=np.float32), (P, NT)),
        "slot_index": np.broadcast_to(np.arange(NSLOT, dtype=np.float32), (P, NSLOT)),
        "first8": np.broadcast_to(E0 - np.arange(E0, dtype=np.float32), (P, E0)),
    }
    for w in "qkvo":
        a[f"W{w}0"] = f[f"L0_xattn_W{w}"]
        a[f"W{w}1"] = f[f"L1_xattn_W{w}"].T
    return {k: np.ascontiguousarray(v) for k, v in a.items()}


def kernel(**inputs):
    import concourse.bacc as _bacc
    from concourse import mybir as _mybir
    from concourse.bass_utils import run_bass_kernel_spmd as _run

    nc = _bacc.Bacc("TRN2", target_bir_lowering=False, num_devices=1)
    laid = lay_out(inputs)
    arrays = {f"in_{k}": v for k, v in laid.items()}
    aps = {k: nc.dram_tensor(f"in_{k}", v.shape, _mybir.dt.from_np(v.dtype), kind="ExternalInput").ap()
           for k, v in laid.items()}
    out = nc.dram_tensor("out_x", (T, D), F32, kind="ExternalOutput").ap()
    block_kernel(nc, aps, out)
    r = _run(nc, [arrays], core_ids=[0])
    return r.results[0]["out_x"].reshape(B, S, D)
```

```python
from collections import namedtuple
from contextlib import ExitStack

import concourse.bass as bass
from concourse import mybir

ALU = mybir.AluOpType
ACT = mybir.ActivationFunctionType
F32 = mybir.dt.float32
BF16 = mybir.dt.bfloat16
U32 = mybir.dt.uint32
F32R = mybir.dt.float32r
AX_X = mybir.AxisListType.X

P = 128
B, S, D = 2, 1024, 256
T = B * S
NT = T // P
NBLK = T // 512
KD = D // P
H, DH = 16, 16
CTX = 64
FF = 1024
KF = FF // P
E0, E0R, E1 = 8, 9, 4
EPS = 1e-5
SCALE = 0.25
NG = H // 4
NU = B * NG
QT = S // P
NSLOT = NT + E0 - 1
RING = 3
LEAD = 6
NSTK = 3
ARENA = 35456
PAR_O = 20
H_FREE = 4
QPART = (0, 0, 1, 0, 2, 1)
KPART = (0, 1, 0, 2, 0, 1)
KS = 16 * len(QPART)
STACK_DMAS = 2 * len(QPART)
KM = KS + 3


LN_SEMS = ("stats", "std", "rstd", "normed", "turned", "xt_ready")
LNSems = namedtuple("LNSems", LN_SEMS)
X_SEMS = ("kv_psum", "k_ready", "kv_spread", "v_biased", "q_psum", "q_ready", "s_ready",
          "max_ready", "s_shifted", "p_ready", "pt_psum", "pt_copied", "av_ready", "recip_ready", "at_ready",
          "wo_ready", "x_biased", "x_done")
XSems = namedtuple("XSems", X_SEMS)
NRING = 4
NRAW = 2
PIECES = 8
F_SEMS = ("weights0", "weights1", "h_psum", "h_done", "o_psum", "o_free", "ct_psum", "ct_ready", "b2_done")
FSems = namedtuple("FSems", F_SEMS)


def block_kernel(nc, A, out):
    ctx = ExitStack()
    with ctx:
        def sb(name, shape, dt=F32):
            return ctx.enter_context(nc.sbuf_tensor(name, shape, dt))

        def sem(name):
            return ctx.enter_context(nc.semaphore(name))

        x = sb("x", [P, NT, D])
        xT = sb("xT", [P, KD, T])
        attn = xT[:, :, :].rearrange("p k t -> p (k t)").rearrange("p (t d) -> p t d", d=D)
        ident = sb("ident", [P, P])
        head_mask = sb("head_mask", [P, 8])
        pair_mask = sb("pair_mask", [P, 32])
        w_both = sb("w_both", [P, KD * 5 * D])
        w_self_o = w_both[:, 0:KD * D].rearrange("p (k d) -> p k d", k=KD)
        w_qkv = w_both[:, KD * D:KD * 4 * D].rearrange("p (k d) -> p k d", k=KD)
        rw2 = w_both[:, 0:KF * D].rearrange("p (k d) -> p k d", k=KF)
        slot_y = w_both[:, KF * D:].rearrange("p (n d) -> p n d", n=2)
        w_route = sb("w_route", [P, KD, E0 + 2])
        w_u = sb("w_u", [P, KD, 1])
        cols = sb("cols", [P, 12, KD])
        BQ0, BK0, BQS, BKS, BQ1, BK1, G1, B1, G2, B2 = range(10)
        rows = sb("rows", [P, 6, D])
        BV0, BO0, BVS, BOS, BV1, BO1 = range(6)
        coef_b = sb("coef_b", [P, 2])
        bu = sb("bu", [P, 1])
        b1_0 = sb("b1_0", [P, E0R, KF])
        b1_1 = sb("b1_1", [P, E1, KF])
        b2_0 = sb("b2_0", [E0R, D])
        b2_1 = sb("b2_1", [E1, D])
        step_inv = sb("step_inv", [P, E1])
        step_thr = sb("step_thr", [P, E1])
        first8 = sb("first8", [P, E0])
        stats = sb("stats", [P, NT, 6])
        mv = sb("mv", [P, NT, 2])
        std = sb("std", [P, NT])
        rstd = sb("rstd", [P, NT])
        rstd2 = sb("rstd2", [P, NT])
        vtmp = sb("vtmp", [P, NT])
        eps = sb("eps", [P, 1])
        credit = sb("credit", [P, 9])
        ctxT = sb("ctxT", [P, KD, P])
        ctxT2 = sb("ctxT2", [P, KD, B, 2, CTX])
        c0 = sb("c0", [P, NT, E0R])
        c1 = sb("c1", [P, NT, E1])
        rt_all = sb("rt_all", [P, 8 * NT * E0])
        rt = [rt_all[:, n * NT * E0:(n + 1) * NT * E0] for n in range(8)]
        before = sb("before", [P, P])
        ones = sb("ones", [P, P])
        tile_edges = sb("tile_edges", [P, NT])
        slot_index = sb("slot_index", [P, NSLOT])
        grow = sb("grow", [P, 2, NT, E0])
        sizes = sb("sizes", [P, 8, E0])
        fits = sb("fits", [P, NSLOT * E0])
        eidf = sb("eidf", [P, NSLOT])
        expert_of = sb("expert_of", [P, NSLOT], U32)
        posf = sb("posf", [P, NT])
        slot_of = sb("slot_of", [P, NT], U32)
        zeros = sb("zeros", [P, D])
        slot_in = sb("slot_in", [P, 4 * D])
        slot_x = slot_in[:, 0:2 * D].rearrange("p (n d) -> p n d", n=2)
        slot_xT = slot_in[:, 2 * D:].rearrange("p (n k q) -> p n k q", n=2, k=KD)
        ctxm = slot_x[:, 0, :]
        slot_b1 = sb("slot_b1", [P, 2, KF])
        with nc.sbuf_tensor("arena", [P, ARENA], F32) as AR:
            pass
        off = [0]

        def at(n, dt=F32):
            v = AR[:, off[0]:off[0] + n]
            off[0] += n
            assert off[0] <= ARENA, off[0]
            return v.bitcast(dt) if dt != F32 else v

        off[0] = 0
        qT = at(KD * T).rearrange("p (k t) -> p k t", k=KD)
        kT = at(KD * P).rearrange("p (k c) -> p k c", k=KD)
        kbd = at(B * KD * 512).rearrange("p (b k c) -> p b k c", b=B, k=KD)
        vb = at(B * D).rearrange("p (b d) -> p b d", b=B)
        vbd = at(B * 8 * 32).rearrange("p (b h c) -> p b h c", b=B, h=8)
        mx = at(3 * H).rearrange("p (n h) -> p n h", n=3)
        pbuf = at(3 * 1024).rearrange("p (n c) -> p n c", n=3)
        pT = at(2 * 8 * 512).rearrange("p (n h q) -> p n h q", n=2, h=8)
        rden = at(2 * 512).rearrange("p (n q) -> p n q", n=2)
        aT = at(2 * KD * 512).rearrange("p (n k q) -> p n k q", n=2, k=KD)
        cross_end = off[0]
        WE = KD * FF
        top = off[0] = cross_end + 4 * WE
        assert off[0] >= 14 * WE + 4 * D
        xn = at(4 * D).rearrange("p (n d) -> p n d", n=4)
        wq, wk, wv, wo = (at(KD * D).rearrange("p (k d) -> p k d", k=KD) for _ in range(4))
        cT = at(T)
        xn_self = AR[:, ARENA - 4 * D:].rearrange("p (n d) -> p n d", n=4)
        off[0] = 0
        split = [at(3 * KD * T // 2, BF16).rearrange("p (a k t) -> p a k t", a=3, k=KD) for _ in range(2)]
        stk = [at(4 * S // 2, BF16).rearrange("p (h t) -> p h t", h=4) for _ in range(2 * NSTK)]
        qstk, kstk = stk[:NSTK], stk[NSTK:]
        vones = at(NT * H // 2 * 48).rearrange("p (t h c) -> p t h c", t=NT, c=48)
        own = at(2 * S)
        ptb = [own[:, 0:S], own[:, S:], w_both[:, KD * D:KD * D + S], w_both[:, KD * D + S:KD * D + 2 * S],
               rt_all[:, :], slot_in[:, :], at(2 * 512)]
        NPTB = len(ptb)
        oT = at(S)
        mpart = at(2 * 64).rearrange("p (n a h) -> p n a h", n=2, h=2)
        mrow = at(32)
        rres = ptb[-1].rearrange("p (n q) -> p n q", n=2)
        mres = at(P)
        msplit = at(3 * P // 2, BF16).rearrange("p (a q) -> p a q", a=3)
        rsum = at(2 * 16).rearrange("p (n a) -> p n a", n=2)
        w1_all = AR[:, 0:E0 * WE].rearrange("p (e k f) -> p e k f", e=E0, k=KD)
        w2_all = AR[:, E0 * WE:2 * E0 * WE].rearrange("p (e k d) -> p e k d", e=E0, k=KF)
        off[0] = 12 * WE
        x2 = at(NT * D).rearrange("p (t d) -> p t d", t=NT)
        aTs = at(4 * KD * P).rearrange("p (n k q) -> p n k q", n=4, k=KD)
        rhT = AR[:, 14 * WE:16 * WE].rearrange("p (n k t) -> p n k t", n=2, k=KF)
        rw1 = AR[:, 16 * WE:17 * WE].rearrange("p (k f) -> p k f", k=KD)
        slot_h = xT[:, :, :].rearrange("p k t -> p (k t)")[:, 0:2 * FF].rearrange("p (n f) -> p n f", n=2)
        slot_hT = xT[:, :, :].rearrange("p k t -> p (k t)")[:, 2 * FF:4 * FF].rearrange("p (n k q) -> p n k q", n=2, k=KF)
        gathered_y = AR[:, 0:NT * D].rearrange("p (t d) -> p t d", t=NT)
        with_parts = 2 * KD * T + 4 * WE + 2 * NRING * 512
        last1 = ctx.enter_context(nc.sbuf_tensor("last1", [P, with_parts], F32R))
        last_raw = ctx.enter_context(nc.sbuf_tensor("last_raw", [P, cross_end - with_parts], F32))
        last0 = ctx.enter_context(nc.sbuf_tensor("last0", [P, 4 * WE], F32R))
        assert cross_end + 4 * WE <= top and NRAW * 512 <= cross_end - with_parts
        x_high, x_low = (last1[:, n * KD * T:(n + 1) * KD * T].rearrange("p (k t) -> p k t", k=KD) for n in range(2))
        w_parts1 = last1[:, 2 * KD * T:2 * KD * T + 4 * WE].rearrange("p (w a c) -> p w a c", w=2, a=2)
        w_parts = (last0[:, :].rearrange("p (w a c) -> p w a c", w=2, a=2), w_parts1)
        h_high, h_low = (last1[:, 2 * KD * T + 4 * WE + n * NRING * 512:2 * KD * T + 4 * WE + (n + 1) * NRING * 512]
                         .rearrange("p (n t) -> p n t", n=NRING) for n in range(2))
        h_raw = last_raw[:, 0:NRAW * 512].rearrange("p (n t) -> p n t", n=NRAW)
        xT_words = xT[:, :, :].rearrange("p k t -> p (k t)")

        def raw_weights(e, which, half):
            n = WE // 2
            if e > 0:
                return xT_words[:, (2 * which + half) * n:(2 * which + half + 1) * n]
            return w_both[:, half * n:(half + 1) * n] if which == 0 else (rt_all, slot_in)[half][:, :]

        def v_and_ones(t, h):
            return vones[:, t, h // 2, 16 * (h % 2):16 * (h % 2) + 32]

        PS = ctx.enter_context(nc.psum_tensor("PS", [P, 8, 512], F32))

        def sum_banks(blk, m):
            return 0 if blk == NBLK - 1 and m else 6

        x_loaded = [sem(f"x_loaded{n}") for n in range(4)]
        load = sem("load")
        load2 = sem("load2")
        const = sem("const")
        ctx_turned = sem("ctx_turned")
        ctx_ready = sem("ctx_ready")
        LN = [LNSems(*[sem(f"ln{n}_{name}") for name in LN_SEMS]) for n in range(5)]
        X = [XSems(*[sem(f"x{n}_{name}") for name in X_SEMS]) for n in range(2)]
        F = [FSems(*[None if n == 0 and name == "weights1" else sem(f"f{n}_{name}") for name in F_SEMS]) for n in range(2)]
        qk_psum = sem("qk_psum")
        high_ready = sem("high_ready")
        rest_ready = sem("rest_ready")
        mid_ready = sem("mid_ready")
        low_ready = sem("low_ready")
        vs_psum = sem("vs_psum")
        vs_ready = sem("vs_ready")
        ones_ready = sem("ones_ready")
        stacked = [sem(f"stacked{n}") for n in range(NSTK)]
        parts_stored = sem("parts_stored")
        ring_full = sem("ring_full")
        ring_free = sem("ring_free")
        max_joined = sem("max_joined")
        msplit_ready = sem("msplit_ready")
        msplit_tmp = sem("msplit_tmp")
        mrow_landed = sem("mrow_landed")
        st_full = sem("st_full")
        exp_done = sem("exp_done")
        av_done = sem("av_done")
        o_full = sem("o_full")
        o_copied = sem("o_copied")
        rsum_ready = sem("rsum_ready")
        y_biased = sem("y_biased")
        a_turned = sem("a_turned")
        a_ready = sem("a_ready")
        so_psum = sem("so_psum")
        y_ready = sem("y_ready")
        x2_ready = sem("x2_ready")
        x_joined = sem("x_joined")
        r_psum = sem("r_psum")
        r_step = sem("r_step")
        r_exp = sem("r_exp")
        r_step1 = sem("r_step1")
        c_ready = sem("c_ready")
        out_stored = sem("out_stored")
        zeros_ready = sem("zeros_ready")
        slots_zeroed = sem("slots_zeroed")
        place_step = sem("place_step")
        scattered = sem("scattered")
        slot_loaded = [sem(f"slot_loaded{n}") for n in range(2)]
        slot_turned = sem("slot_turned")
        slot_xt = sem("slot_xt")
        slot_h_psum = sem("slot_h_psum")
        slot_h_copied = sem("slot_h_copied")
        slot_ht_psum = sem("slot_ht_psum")
        slot_b1_ready = sem("slot_b1_ready")
        slot_gelu = sem("slot_gelu")
        slot_y_psum = sem("slot_y_psum")
        slot_y_copied = sem("slot_y_copied")
        slot_stored = [sem(f"slot_stored{n}") for n in range(2)]
        gathered = [sem(f"gathered{n}") for n in range(4)]
        routed_done = sem("routed_done")
        x_split = sem("x_split")
        w_split = [sem(f"w_split{n}") for n in range(2)]
        h_cut = sem("h_cut")
        h_split = sem("h_split")
        h_used = sem("h_used")

        qk_parts = nc.dram_tensor("qk_parts", (2, 3, D, T), BF16, kind="Internal").ap()
        slots_in = nc.dram_tensor("slots_in", (NSLOT * P, D), F32, kind="Internal").ap()
        slots_out = nc.dram_tensor("slots_out", (NSLOT * P, D), F32, kind="Internal").ap()

        NLOAD = [0]
        LOAD2 = 16 * 16

        def ring_jobs(n):
            jobs = []
            v, at_v = divmod(n + 32 + LEAD, 32)
            if v < NU:
                jobs += [("scores", v, 2 * at_v + half) for half in range(2)]
            if at_v == 1 and v >= 1 and v <= NU:
                jobs.append(("maxima", v - 1, 0))
            u, at_u = divmod(n, 32)
            if u >= 1 and at_u in (6, 7):
                jobs.append(("output", u - 1, at_u - 6))
            return jobs

        QK_TILES = 2 * KD * NBLK

        def qk_tile(i):
            return i // 2 % 2, i // 8, 2 * (i // 4 % 2) + i % 2

        def v_tile(n):
            t, odd = divmod(n + 32 + LEAD, 2)
            return None if odd or t >= NT else t

        STEPS = range(-32 - LEAD, 32 * NU + 8)
        JOBS = sum(len(ring_jobs(n)) for n in STEPS)

        def jobs_before(n):
            return sum(len(ring_jobs(i)) for i in STEPS if i < n)

        PLACED = 27
        block = ctx.enter_context(nc.Block())

        def w_of(name):
            return A[name].rearrange("(k p) f -> p k f", p=P)

        def tiles_of(rows_of):
            return rows_of.rearrange("(t p) d -> p t d", p=P)

        def piece_of(e, par, piece):
            n = 2 * WE // PIECES
            which, c = divmod(piece * n, WE)
            half, at_half = divmod(c, WE // 2)
            return (raw_weights(e, which, half)[:, at_half:at_half + n],
                    w_parts[par][:, which, 0, c:c + n], w_parts[par][:, which, 1, c:c + n])

        @block.sync
        def _(sp):
            def ld(dst, src):
                sp.dma_start(dst, src).then_inc(load, 16)
                NLOAD[0] += 16

            for c in range(4):
                sp.dma_start(x[:, 4 * c:4 * c + 4, :], tiles_of(A["x"])[:, 4 * c:4 * c + 4, :]).then_inc(x_loaded[c], 16)
            ld(ident[:, :], A["ident"])
            ld(ctxm[:, :], A["ctx"])
            ld(cols[:, 0:10, :], A["cols"])
            ld(rows[:, :, :], A["rows"].unsqueeze(0).broadcast_to([P, 6, D]))
            ld(head_mask[:, :], A["head_mask"])
            ld(pair_mask[:, :], A["pair_mask"])
            for tile, name in ((wq, "Wq0"), (wk, "Wk0"), (wv, "Wv0"), (wo, "Wo0")):
                ld(tile, w_of(name))
            assert NLOAD[0] == 16 * 10
            n2 = 0
            for tile, name in ((w_qkv, "Wqkv"), (w_self_o, "WoS"), (w_route[:, :, :], "w_route")):
                sp.dma_start(tile, w_of(name)).then_inc(load2, 16)
                n2 += 16
            for dst, src in ((w_u[:, :, 0], A["w_u"]), (coef_b[:, :], A["coef_b"].unsqueeze(0).broadcast_to([P, 2])),
                             (bu[:, :], A["bu"].unsqueeze(0).broadcast_to([P, 1])),
                             (b1_0[:, :, :], A["b1_0"]), (b1_1[:, :, :], A["b1_1"]),
                             (b2_0[:, :], A["b2_0"]), (b2_1[:, :], A["b2_1"]),
                             (step_inv[:, :], A["step_inv"]), (step_thr[:, :], A["step_thr"]),
                             (before[:, :], A["before"]), (tile_edges[:, :], A["tile_edges"]),
                             (slot_index[:, :], A["slot_index"]), (first8[:, :], A["first8"])):
                sp.dma_start(dst, src).then_inc(load2, 16)
                n2 += 16
            assert n2 == LOAD2
            sp.wait_ge(zeros_ready, 1)
            sp.dma_start(slots_in.rearrange("(p j) d -> p j d", j=NSLOT), zeros[:, :].unsqueeze(1).broadcast_to([P, NSLOT, D]))\
                .then_inc(slots_zeroed, 16)

            def store_parts(c):
                m, b = divmod(c, B)
                tiles = 4 * c + 4
                sp.wait_ge(high_ready, tiles)
                sp.wait_ge(mid_ready, tiles)
                sp.wait_ge(low_ready, tiles)
                for which in range(2):
                    for part in range(3):
                        sp.dma_start(qk_parts[which, part, m * P:(m + 1) * P, b * S:(b + 1) * S],
                                     split[which][:, part, m, b * S:(b + 1) * S]).then_inc(parts_stored, 16)
                sp.wait_ge(parts_stored, 16 * 6 * (c + 1))

            def stack_unit(u):
                b, g = divmod(u, NG)
                if u >= NSTK:
                    sp.wait_ge(st_full, 64 * (u - NSTK + 1))
                for which, parts, dst in ((0, QPART, qstk), (1, KPART, kstk)):
                    for i, part in enumerate(parts):
                        sp.dma_start(dst[u % NSTK][16 * i:16 * (i + 1), :, :],
                                     qk_parts[which, part, g * 64:(g + 1) * 64, b * S:(b + 1) * S]
                                     .rearrange("(j r) t -> r j t", j=4)).then_inc(stacked[u % NSTK], 16)

            store_parts(0)
            for u in range(NSTK - 1):
                stack_unit(u)
            for c in range(1, KD * B):
                store_parts(c)
            for u in range(NU):
                sp.wait_ge(msplit_ready, u + 1)
                for i in range(3):
                    sp.dma_start(qstk[u % NSTK][KS + i:KS + i + 1, :, :].rearrange("p h t -> p (h t)"),
                                 msplit[0:32, i, :]).then_inc(mrow_landed, 16)
                if u + NSTK - 1 < NU:
                    stack_unit(u + NSTK - 1)

            def last_weights(e):
                for which, name in enumerate(("W1_1", "W2_1")):
                    k = (KD, KF)[which]
                    for half in range(2):
                        rows_of = A[name][e].rearrange("(k p) f -> p k f", p=P)[:, half * k // 2:(half + 1) * k // 2, :]
                        sp.dma_start(raw_weights(e, which, half).rearrange("p (k f) -> p k f", k=k // 2), rows_of)\
                            .then_inc((F[1].weights0, F[1].weights1)[e % 2], 16)

            def routed_weights(e, which, loaded=load2):
                dst, src, k = ((w1_all, A["W1_0"], KD), (w2_all, A["W2_0"], KF))[which]
                sp.dma_start(dst[:, e, :, :], src[e].rearrange("(k p) f -> p k f", p=P)).then_inc(loaded, 16)

            sp.wait_ge(ring_free, JOBS)
            sp.dma_start(rw1, A["W1_0"][E0].rearrange("(k p) f -> p k f", p=P)).then_inc(F[0].weights0, 16)
            for e in range(E0 - 2):
                routed_weights(e, 0)
            sp.wait_ge(so_psum, NT)
            sp.dma_start(rw2, A["W2_0"][E0].rearrange("(k p) f -> p k f", p=P)).then_inc(F[0].weights0, 16)
            for e in range(E0 - 2, E0):
                routed_weights(e, 0)
            for e in range(4):
                routed_weights(e, 1)
            sp.wait_ge(scattered, 16 * NT)
            routed_weights(4, 1)
            routed_weights(5, 1)

            def load_slots(j, par):
                sp.wait_ge(slot_turned, j - 1)
                sp.dma_start(slot_x[:, par, :], slots_in[bass.ds(j * P, P), :]).then_inc(slot_loaded[par], 16)

            def store_slots(j, par):
                sp.wait_ge(slot_y_copied, j + 3)
                sp.dma_start(slots_out[bass.ds(j * P, P), :], slot_y[:, par, :]).then_inc(slot_stored[par], 16)

            for j in range(2):
                sp.dma_start(slot_x[:, j, :], slots_in[j * P:(j + 1) * P, :]).then_inc(slot_loaded[j], 16)
            sp.wait_ge(F[0].o_free, PAR_O + NT)
            routed_weights(6, 1, F[0].weights0)
            routed_weights(7, 1, F[0].weights0)
            load_slots(2, 0)
            load_slots(3, 1)
            with sp.Fori(0, (NSLOT - 5) // 2) as pair:
                for par in range(2):
                    load_slots(pair * 2 + 4 + par, par)
                    store_slots(pair * 2 + par, par)
            load_slots(NSLOT - 1, (NSLOT - 1) % 2)
            for j in range(NSLOT - 5, NSLOT):
                store_slots(j, j % 2)

            sp.wait_ge(slot_y_psum, NSLOT)
            for tile, name in ((wq, "Wq1"), (wk, "Wk1"), (wv, "Wv1"), (wo, "Wo1")):
                sp.dma_start(tile, w_of(name)).then_inc(load, 16)
            sp.wait_ge(routed_done, NT)
            last_weights(0)
            sp.wait_ge(x_split, 2 * NBLK)
            sp.wait_ge(r_psum, 3)
            last_weights(1)
            for e in range(2, E1):
                sp.wait_ge(w_split[(e - 1) % 2], 2 * PIECES * ((e - 1) // 2 + 1))
                last_weights(e)

            for c in range(4):
                sp.wait_ge(F[1].o_free, PAR_O + NT * (E1 - 1) + 4 * (c + 1))
                sp.dma_start(tiles_of(out)[:, 4 * c:4 * c + 4, :], x[:, 4 * c:4 * c + 4, :]).then_inc(out_stored, 16)
            sp.wait_ge(out_stored, 16 * 4)

        @block.tensor
        def _(pe):
            mm = nc.tensor.matmul

            def turn_norm(n, router=None):
                s = LN[n]
                buf = xn_self if n == 1 else xn
                for t in range(NT + (0 if router is None else 2)):
                    if t < NT:
                        pe.wait_ge(s.normed, t + 1)
                        if t >= 4:
                            pe.wait_ge(s.xt_ready, t - 3)
                        for k in range(KD):
                            last = nc.tensor.transpose(PS[:, t % 4, k * P:(k + 1) * P],
                                                       buf[:, t % 4, k * P:(k + 1) * P], ident[:, :])
                        last.then_inc(s.turned, 1)
                    if router is not None and t >= 2:
                        w, width = ((w_route, E0 + 2), (w_u, 1))[router]
                        if t == 2:
                            pe.wait_ge(load2, LOAD2)
                            if router == 0:
                                pe.wait_ge(x2_ready, NT)
                            else:
                                pe.wait_ge(X[1].x_done, NT)
                        m = t - 2
                        pe.wait_ge(s.xt_ready, m + 1)
                        for k in range(KD):
                            last = mm(PS[:, 4, m * width:(m + 1) * width], xT[:, k, m * P:(m + 1) * P], w[:, k, :],
                                      start=(k == 0), stop=(k == KD - 1))
                if router is not None:
                    last.then_inc(r_psum, 1)

            def keys_and_values(n):
                s = X[n]
                if n == 1:
                    pe.wait_ge(load, 16 * (10 + 4))
                for m in range(KD):
                    for k in range(KD):
                        last = mm(PS[:, 4, m * P:(m + 1) * P], wk[:, k, m * P:(m + 1) * P], ctxT[:, k, :],
                                  start=(k == 0), stop=(k == KD - 1))
                last.then_inc(s.kv_psum, 1)
                for b in range(B):
                    for k in range(KD):
                        last = mm(PS[:, 5, b * D:(b + 1) * D],
                                  ctxT2[:, k, b, :, :].rearrange("p a c -> p (a c)"), wv[:, k, :],
                                  start=(k == 0), stop=(k == KD - 1))
                last.then_inc(s.kv_psum, 1)

            def cross(n):
                s = X[n]
                ln = (LN[0], LN[3])[n]

                def queries(blk):
                    pe.wait_ge(ln.xt_ready, 4 * blk + 4)
                    for m in range(KD):
                        if blk:
                            pe.wait_ge(s.q_ready, KD * (blk - 1) + m + 1)
                        for k in range(KD):
                            last = mm(PS[:, 6 + m, :], wq[:, k, m * P:(m + 1) * P],
                                      xT[:, k, blk * 512:(blk + 1) * 512], start=(k == 0), stop=(k == KD - 1))
                        last.then_inc(s.q_psum, 1)

                def scores(t):
                    b = t // QT
                    pe.wait_ge(s.q_ready, KD * (t // 4 + 1))
                    if t >= 2:
                        pe.wait_ge(s.s_shifted, t - 1)
                    for m in range(KD):
                        last = mm(PS[:, 2 * (t % 2) + m, :], qT[:, m, t * P:(t + 1) * P], kbd[:, b, m, :],
                                  start=True, stop=True)
                    last.then_inc(s.s_ready, 1)

                def turn_p(t):
                    pe.wait_ge(s.p_ready, t + 1)
                    if t >= 1:
                        pe.wait_ge(s.pt_copied, t)
                    for h in range(8):
                        last = nc.tensor.transpose(PS[:, 4 + h // 4, (h % 4) * P:(h % 4 + 1) * P],
                                                   pbuf[:, t % 3, h * P:(h + 1) * P], ident[:, :])
                    last.then_inc(s.pt_psum, 1)

                def weigh(blk, m):
                    b = blk // (NBLK // B)
                    values = sum_banks(blk, m)
                    if values == 0:
                        pe.wait_ge(s.s_shifted, NT)
                    elif m:
                        pe.wait_ge(s.at_ready, KD * blk + m)
                    else:
                        pe.wait_ge(s.pt_copied, 4 * blk + 4)
                        if blk == 0:
                            pe.wait_ge(s.q_ready, KD * NBLK)
                        else:
                            pe.wait_ge(s.x_done, 4 * blk)
                    for j in range(4):
                        mm(PS[32 * j:32 * j + 32, values, :], vbd[:, b, 4 * m + j, :], pT[:, blk % 2, 4 * m + j, :],
                           start=True, stop=True)
                    for j in range(4):
                        last = mm(PS[32 * j:32 * j + 32, values + 1, :], pair_mask[:, :], pT[:, blk % 2, 4 * m + j, :],
                                  start=True, stop=True)
                    last.then_inc(s.av_ready, 1)

                def project(blk, c):
                    pe.wait_ge(s.at_ready, KD * (blk + 1))
                    for sub in range(2 * c, 2 * c + 2):
                        for m in range(KD):
                            last = mm(PS[:, 6 + c, (sub % 2) * D:(sub % 2 + 1) * D],
                                      aT[:, blk % 2, m, sub * P:(sub + 1) * P], wo[:, m, :],
                                      start=(m == 0), stop=(m == KD - 1))
                    last.then_inc(s.wo_ready, 1)

                queries(0)
                pe.wait_ge(s.kv_spread, B * KD + B)
                scores(0)
                for t in range(NT + 4):
                    blk, sub = divmod(t, 4)
                    if t + 1 < NT:
                        scores(t + 1)
                    if t < NT:
                        turn_p(t)
                    if t + 1 < NBLK:
                        queries(t + 1)
                    if blk >= 1:
                        if sub < 2:
                            weigh(blk - 1, sub)
                        else:
                            project(blk - 1, sub - 2)

            def self_attention():
                pe.wait_ge(load2, LOAD2)
                pe.wait_ge(X[0].x_done, NT)
                for i in range(QK_TILES):
                    w, m, blk = qk_tile(i)
                    if m == 0 and w == 0:
                        pe.wait_ge(LN[1].xt_ready, 4 * blk + 4)
                    if i >= 4:
                        pe.wait_ge(rest_ready, i - 3)
                    for k in range(KD):
                        last = mm(PS[:, 4 + i % 4, :], w_qkv[:, k, w * D + m * P:w * D + (m + 1) * P],
                                  xT[:, k, blk * 512:(blk + 1) * 512], start=(k == 0), stop=(k == KD - 1))
                    last.then_inc(qk_psum, 1)
                pe.wait_ge(rest_ready, QK_TILES)
                pe.wait_ge(ones_ready, 1 + NSTK)

                def values(t):
                    if t >= 3:
                        pe.wait_ge(vs_ready, t - 2)
                    for k in range(KD):
                        last = mm(PS[:, t % 3, 0:D], xT[:, k, t * P:(t + 1) * P], w_qkv[:, k, 2 * D:3 * D],
                                  start=(k == 0), stop=(k == KD - 1))
                    last.then_inc(vs_psum, 1)

                def weigh(group, half):
                    u, kt = divmod(group, QT)
                    b, g = divmod(u, NG)
                    pe.wait_ge(exp_done, 2 * (4 * group + 3) + half + 1)
                    if kt == 0 and u >= 1:
                        pe.wait_ge(o_copied, 2 * u)
                    for j in range(4):
                        last = mm(PS[32 * j:32 * j + 32, 6 + half, :], v_and_ones(b * QT + kt, 4 * g + j),
                                  ptb[(4 * group + j) % NPTB][:, half * 512:(half + 1) * 512],
                                  start=(kt == 0), stop=(kt == QT - 1))
                    if half:
                        last.then_inc(av_done, 1)

                def ring_job(job, kind, u, i):
                    if job >= 3:
                        pe.wait_ge(ring_free, job - 2)
                    if kind == "scores":
                        if i == 0:
                            pe.wait_ge(stacked[u % NSTK], 16 * STACK_DMAS * (u // NSTK + 1))
                        j, qt, half = i // 16, i // 2 % QT, i % 2
                        last = mm(PS[:, RING + job % 3, :], qstk[u % NSTK][0:KS, j, qt * P:(qt + 1) * P],
                                  kstk[u % NSTK][0:KS, j, half * 512:(half + 1) * 512], start=True, stop=True)
                    elif kind == "maxima":
                        pe.wait_ge(max_joined, u + 1)
                        last = nc.tensor.transpose(PS[0:32, RING + job % 3, 0:P], mrow[:, :], ident[:, :])
                    else:
                        pe.wait_ge(o_copied, 2 * u + 2)
                        for c in range(4):
                            last = nc.tensor.transpose(PS[:, RING + job % 3, c * P:(c + 1) * P],
                                                       oT[:, (i * 4 + c) * P:(i * 4 + c + 1) * P], ident[:, :])
                    last.then_inc(ring_full, 1)

                job = 0
                for n in STEPS:
                    u, at_u = divmod(n, 32)
                    kt, j = divmod(at_u, 4)
                    if n >= 4 and n < 32 * NU + 4 and j % 2:
                        weigh(n // 4 - 1, j // 2)
                    if n == 0:
                        pe.wait_ge(vs_ready, NT)
                    if v_tile(n) is not None:
                        values(v_tile(n))
                    jobs = ring_jobs(n)
                    for half in range(2):
                        if jobs:
                            ring_job(job, *jobs.pop(0))
                            job += 1
                        if u >= 0 and u < NU:
                            if half == 0 and at_u == 0:
                                pe.wait_ge(mrow_landed, 48 * (u + 1))
                            tile = 2 * n + half
                            if tile >= 3:
                                pe.wait_ge(exp_done, tile - 2)
                            mm(PS[:, tile % 3, :], kstk[u % NSTK][0:KM, j, kt * P:(kt + 1) * P],
                               qstk[u % NSTK][0:KM, j, half * 512:(half + 1) * 512], start=True, stop=True)\
                                .then_inc(st_full, 1)
                    for left in jobs:
                        ring_job(job, *left)
                        job += 1

                for t in range(NT + 2):
                    if t < NT:
                        if t == 0:
                            pe.wait_ge(ring_free, JOBS)
                        if t >= 4:
                            pe.wait_ge(a_ready, t - 3)
                        for k in range(KD):
                            last = nc.tensor.transpose(PS[:, t % 4, k * P:(k + 1) * P],
                                                       attn[:, t, k * P:(k + 1) * P], ident[:, :])
                        last.then_inc(a_turned, 1)
                    if t >= 2:
                        n = t - 2
                        pe.wait_ge(a_ready, n + 1)
                        if n >= 4:
                            pe.wait_ge(x2_ready, n - 3)
                        for k in range(KD):
                            last = mm(PS[:, 4 + n % 4, 0:D], aTs[:, n % 4, k, :], w_self_o[:, k, :],
                                      start=(k == 0), stop=(k == KD - 1))
                        last.then_inc(so_psum, 1)

            def second_biases(n):
                pe.wait_ge(c_ready, n + 1)
                if n == 0:
                    pe.wait_ge(slot_gelu, NSLOT + 1)
                    pe.wait_ge(slot_y_copied, NSLOT + 2)
                else:
                    pe.wait_ge(F[1].h_done, H_FREE + (E1 - 2) * NBLK * KF)
                    pe.wait_ge(F[1].o_free, PAR_O + (E1 - 2) * NT)
                e, c = ((E0R, c0), (E1, c1))[n]
                for t in range(NT):
                    last = nc.tensor.transpose(PS[0:e, t // 4, (t % 4) * P:(t % 4 + 1) * P], c[:, t, :], ident[:, :])
                last.then_inc(F[n].ct_psum, 1)
                pe.wait_ge(F[n].ct_ready, 1)
                b2 = (b2_0, b2_1)[n]
                for t in range(NT):
                    if t >= 4:
                        pe.wait_ge(F[n].b2_done, t - 3)
                    mm(PS[:, 4 + t % 4, 0:D], cT[0:e, t * P:(t + 1) * P], b2[:, :], start=True, stop=True)\
                        .then_inc(F[n].ct_psum, 1)
                pe.wait_ge(F[n].b2_done, NT)

            def dense_expert():
                s = F[0]
                pe.wait_ge(s.weights0, 32)
                for tb in range(9):
                    if tb < 8:
                        for f in range(KF):
                            i = tb * KF + f
                            if i >= 4:
                                pe.wait_ge(s.h_done, H_FREE + i - 3)
                            for k in range(KD):
                                last = mm(PS[:, i % 4, 0:256], rw1[:, k, f * P:(f + 1) * P],
                                          xT[:, k, tb * 256:(tb + 1) * 256], start=(k == 0), stop=(k == KD - 1))
                            last.then_inc(s.h_psum, 1)
                    if tb == 1:
                        pe.wait_ge(r_step, 9)
                        pe.wait_ge(zeros_ready, 2)
                        mm(PS[:, 7, 0:P], before[:, :], rt[7], start=True, stop=True)
                        mm(PS[:, 7, P:2 * P], ones[:, :], rt[7], start=True, stop=True).then_inc(r_psum, 1)
                    if tb >= 1:
                        tp = tb - 1
                        pe.wait_ge(s.h_done, H_FREE + KF * (tp + 1))
                        for sub in range(2):
                            i = tp * 2 + sub
                            if i >= 2:
                                pe.wait_ge(s.o_free, PAR_O + i - 1)
                            for f in range(KF):
                                last = mm(PS[:, 4 + i % 2, 0:D], rhT[:, tp % 2, f, sub * P:(sub + 1) * P], rw2[:, f, :],
                                          start=(f == 0), stop=(f == KF - 1))
                            last.then_inc(s.o_psum, 1)

            def routed_experts():

                def turn_x(j, par):
                    pe.wait_ge(slot_loaded[par], 8 * (j - par) + 16)
                    for k in range(KD):
                        last = nc.tensor.transpose(PS[:, 6 + par, k * P:(k + 1) * P],
                                                   slot_x[:, par, k * P:(k + 1) * P], ident[:, :])
                    last.then_inc(slot_turned, 1)

                def first(j, par):
                    e = nc.tensor.value_load(expert_of[0:1, bass.ds(j, 1)], min_val=0, max_val=E0 - 1)
                    pe.wait_ge(slot_xt, j + 1)
                    pe.wait_ge(slot_h_copied, j + 1)
                    for c in range(2):
                        for k in range(KD):
                            last = mm(PS[:, c, :], slot_xT[:, par, k, :],
                                      w1_all[:, bass.ds(e, 1), k, c * 512:(c + 1) * 512].rearrange("p a f -> p (a f)"),
                                      start=(k == 0), stop=(k == KD - 1))
                    last.then_inc(slot_h_psum, 1)

                def turn_h(j, par):
                    pe.wait_ge(slot_h_copied, j + 2)
                    pe.wait_ge(slot_gelu, j + 1)
                    for f in range(KF):
                        last = nc.tensor.transpose(PS[:, 2 + f // 4, (f % 4) * P:(f % 4 + 1) * P],
                                                   slot_h[:, par, f * P:(f + 1) * P], ident[:, :])
                    last.then_inc(slot_ht_psum, 1)

                def second(j, par):
                    e = nc.tensor.value_load(expert_of[0:1, bass.ds(j, 1)], min_val=0, max_val=E0 - 1)
                    pe.wait_ge(slot_gelu, j + 2)
                    pe.wait_ge(slot_y_copied, j + 1)
                    for f in range(KF):
                        last = mm(PS[:, 4 + par, 0:D], slot_hT[:, par, f, :],
                                  w2_all[:, bass.ds(e, 1), f, :].rearrange("p a d -> p (a d)"),
                                  start=(f == 0), stop=(f == KF - 1))
                    last.then_inc(slot_y_psum, 1)

                pe.wait_ge(place_step, PLACED)
                pe.wait_ge(load2, LOAD2 + 16 * (2 * E0 - 2))
                pe.wait_ge(F[0].o_free, PAR_O + NT)
                turn_x(0, 0)
                first(0, 0)
                turn_x(1, 1)
                first(1, 1)
                turn_x(2, 0)
                turn_h(0, 0)
                first(2, 0)
                turn_x(3, 1)
                turn_h(1, 1)
                pe.wait_ge(F[0].weights0, 16 * (2 + 2))
                second(0, 0)

                def turn(i, par, more=True):
                    first(i, par)
                    if more:
                        turn_x(i + 1, 1 - par)
                    turn_h(i - 1, 1 - par)
                    second(i - 2, par)

                with pe.Fori(0, (NSLOT - 5) // 2) as pair:
                    turn(pair * 2 + 3, 1)
                    turn(pair * 2 + 4, 0)
                turn(NSLOT - 2, 1)
                turn(NSLOT - 1, 0, more=False)
                turn_h(NSLOT - 1, 0)
                second(NSLOT - 2, 1)
                second(NSLOT - 1, 0)

            def last_experts():
                s = F[1]

                def parts(dst, a, b, start, stop):
                    mm(dst, a[0], b[0], start=start, stop=False)
                    mm(dst, a[0], b[1], start=False, stop=False)
                    return mm(dst, a[1], b[0], start=False, stop=stop)

                def first(e, par, i):
                    tb, f = divmod(i, KF)
                    pe.wait_ge(s.h_done, 32 * e + i + 1)
                    pe.wait_ge(x_split, 2 * (tb + 1))
                    for k in range(KD):
                        c, t = k * FF + f * P, tb * 512
                        last = parts(PS[:, i % 4, :],
                                     [w_parts[par][:, 0, a, c:c + P] for a in range(2)],
                                     [xs[:, k, t:t + 512] for xs in (x_high, x_low)],
                                     k == 0, k == KD - 1)
                    last.then_inc(s.h_psum, 1)

                def second(e, par, i):
                    tb, f = divmod(i, KF)
                    pe.wait_ge(h_split, 32 * e + i + 1)
                    for sub in range(4):
                        if f == 0:
                            pe.wait_ge(s.o_free, 16 * e + PAR_O - 3 + 4 * tb + sub)
                        last = parts(PS[:, 4 + sub, 0:D],
                                     [h[:, i % NRING, sub * P:(sub + 1) * P] for h in (h_high, h_low)],
                                     [w_parts[par][:, 1, a, f * D:(f + 1) * D] for a in range(2)],
                                     f == 0, f == KF - 1)
                        if f == KF - 1:
                            last.then_inc(s.o_psum, 1)
                    if f < KF - 1:
                        last.then_inc(h_used, 1)

                def one(e, par):
                    pe.wait_ge(w_split[par], PIECES * (e - par) + 2 * PIECES)
                    for i in range(NBLK * KF + 2):
                        if i < NBLK * KF:
                            first(e, par, i)
                        if i >= 2:
                            second(e, par, i - 2)

                with pe.Fori(0, E1 // 2 - 1) as pair:
                    one(pair * 2, 0)
                    one(pair * 2 + 1, 1)
                second_biases(1)
                one(E1 - 2, 0)
                one(E1 - 1, 1)

            pe.wait_ge(load, 16 * 10)
            for k in range(KD):
                last = nc.tensor.transpose(PS[:, 7, k * P:(k + 1) * P], ctxm[:, k * P:(k + 1) * P], ident[:, :])
            last.then_inc(ctx_turned, 1)
            pe.wait_ge(ctx_ready, 3)
            keys_and_values(0)
            turn_norm(0)
            cross(0)
            turn_norm(1)
            self_attention()
            turn_norm(2, router=0)
            dense_expert()
            routed_experts()
            second_biases(0)
            keys_and_values(1)
            turn_norm(3)
            cross(1)
            turn_norm(4, router=1)
            last_experts()

        @block.scalar
        def _(act):
            run = nc.scalar.activation

            def evacuate_norm(n, gain=None, bias=None):
                s = LN[n]
                act.wait_ge(s.stats, 2 * NT)
                run(std[:, :], mv[:, :, 1], ACT.Sqrt, bias=eps[:, :]).then_inc(s.std, 1)
                if n == 1:
                    act.wait_ge(s.rstd, 3)
                    run(std[:, :], vtmp[:, :], ACT.Sqrt, bias=eps[:, :]).then_inc(s.std, 1)
                for t in range(NT):
                    act.wait_ge(s.turned, t + 1)
                    dst, src = xT[:, :, t * P:(t + 1) * P], PS[:, t % 4, 0:D].rearrange("p (k t) -> p k t", k=KD)
                    if gain is None:
                        run(dst, src, ACT.Copy).then_inc(s.xt_ready, 1)
                    else:
                        for k in range(KD):
                            last = run(dst[:, k, :], src[:, k, :], ACT.Identity, bias=cols[:, bias, k:k + 1],
                                       scale=cols[:, gain, k:k + 1])
                        last.then_inc(s.xt_ready, 1)

            def keys(n):
                s = X[n]
                bk = (BK0, BK1)[n]
                act.wait_ge(s.kv_psum, 1)
                for m in range(KD):
                    last = run(kT[:, m, :], PS[:, 4, m * P:(m + 1) * P], ACT.Identity, bias=cols[:, bk, m:m + 1])
                last.then_inc(s.k_ready, 1)

            def cross(n):
                s = X[n]
                bq = (BQ0, BQ1)[n]
                def queries(blk):
                    for m in range(KD):
                        act.wait_ge(s.q_psum, KD * blk + m + 1)
                        run(qT[:, m, blk * 512:(blk + 1) * 512], PS[:, 6 + m, :], ACT.Identity,
                            bias=cols[:, bq, m:m + 1]).then_inc(s.q_ready, 1)

                def expo(t):
                    act.wait_ge(s.s_shifted, t + 1)
                    run(pbuf[:, t % 3, :], pbuf[:, t % 3, :], ACT.Exp, scale=SCALE).then_inc(s.p_ready, 1)

                def evacuate(t):
                    blk, sub = divmod(t, 4)
                    act.wait_ge(s.pt_psum, t + 1)
                    if sub == 0 and blk >= 2:
                        act.wait_ge(s.av_ready, KD * (blk - 1))
                    run(pT[:, blk % 2, :, sub * P:(sub + 1) * P],
                        PS[:, 4:6, :].rearrange("p a (h q) -> p (a h) q", h=4), ACT.Copy).then_inc(s.pt_copied, 1)

                queries(0)
                expo(0)
                for t in range(NT):
                    if t + 1 < NT:
                        expo(t + 1)
                    evacuate(t)
                    if t + 1 < NBLK:
                        queries(t + 1)

            def self_attention():
                def high(i):
                    w, m, blk = qk_tile(i)
                    act.wait_ge(qk_psum, i + 1)
                    run(split[w][:, 0, m, blk * 512:(blk + 1) * 512], PS[:, 4 + i % 4, :], ACT.Identity,
                        bias=cols[:, (BQS, BKS)[w], m:m + 1]).then_inc(high_ready, 1)

                def middle(i):
                    w, m, blk = qk_tile(i)
                    act.wait_ge(rest_ready, i + 1)
                    run(split[w][:, 1, m, blk * 512:(blk + 1) * 512], rres[:, i % 2, :], ACT.Copy)\
                        .then_inc(mid_ready, 1)

                n = QK_TILES
                for i in range(n):
                    high(i)
                    if i >= 1:
                        middle(i - 1)
                middle(n - 1)
                for n in range(32 * NU + 5):
                    if n >= 32 and n % 32 == 4:
                        u = n // 32 - 1
                        act.wait_ge(av_done, QT * (u + 1))
                        if u >= 1:
                            act.wait_ge(ring_free, jobs_before(n - 32 + 4))
                        run(oT[:, 512:1024], PS[:, 7, :], ACT.Copy).then_inc(o_copied, 1)
                    if n < 32 * NU:
                        if n >= NPTB:
                            act.wait_ge(av_done, (n - NPTB) // 4 + 1)
                        for half in range(2):
                            tile = 2 * n + half
                            act.wait_ge(st_full, tile + 1)
                            run(ptb[n % NPTB][:, half * 512:(half + 1) * 512], PS[:, tile % 3, :], ACT.Exp,
                                scale=SCALE).then_inc(exp_done, 1)
                for t in range(NT):
                    act.wait_ge(a_turned, t + 1)
                    if t >= 4:
                        act.wait_ge(so_psum, t - 3)
                    run(aTs[:, t % 4, :, :], PS[:, t % 4, 0:D].rearrange("p (k q) -> p k q", k=KD), ACT.Copy)\
                        .then_inc(a_ready, 1)

            def route(n):
                if n == 0:
                    act.wait_ge(r_step, 2)
                    run(rt[2], rt[1], ACT.Exp).then_inc(r_exp, 1)
                    act.wait_ge(r_step, 5)
                    run(rt[4][:, 0:2 * NT], rt[3][:, 0:2 * NT], ACT.Exp).then_inc(r_exp, 1)
                else:
                    act.wait_ge(r_step1, 1)
                    run(rt[1][:, 0:NT], rt[0][:, 0:NT], ACT.Exp, scale=-1.0).then_inc(r_exp, 1)

            def turned_weights(n):
                e = (E0R, E1)[n]
                act.wait_ge(F[n].ct_psum, 1)
                run(cT[0:e, :], PS[0:e, 0:4, :].rearrange("p a q -> p (a q)"), ACT.Copy).then_inc(F[n].ct_ready, 1)

            def last_experts():
                s = F[1]
                for i in range(E1 * NBLK * KF):
                    if i == (E1 - 2) * NBLK * KF:
                        turned_weights(1)
                    e, f = i // (NBLK * KF), i % KF
                    act.wait_ge(s.h_psum, i + 1)
                    if i >= NRAW:
                        act.wait_ge(h_split, i - NRAW + 1)
                    run(h_raw[:, i % NRAW, :], PS[:, i % 4, :], ACT.Relu, bias=b1_1[:, e, f:f + 1]).then_inc(s.h_done, 1)

            def dense_expert():
                s = F[0]
                for i in range(8 * KF):
                    tb, f = divmod(i, KF)
                    act.wait_ge(s.h_psum, i + 1)
                    if f == 0 and tb >= 2:
                        act.wait_ge(s.o_psum, PAR_O + 2 * (tb - 1))
                    run(rhT[:, tb % 2, f, :], PS[:, i % 4, 0:256], ACT.Gelu, bias=b1_0[:, E0, f:f + 1])\
                        .then_inc(s.h_done, 1)

            def routed_experts():
                def evacuate(j):
                    act.wait_ge(slot_turned, j + 1)
                    if j >= 2:
                        act.wait_ge(slot_h_psum, j - 1)
                    for k in range(KD):
                        last = run(slot_xT[:, j % 2, k, :], PS[:, 6 + j % 2, k * P:(k + 1) * P], ACT.Identity,
                                   bias=cols[:, B2, k:k + 1], scale=cols[:, G2, k:k + 1])
                    last.then_inc(slot_xt, 1)

                def gelu(j):
                    act.wait_ge(slot_ht_psum, j + 1)
                    act.wait_ge(slot_b1_ready, j + 1)
                    if j >= 2:
                        act.wait_ge(slot_y_psum, j - 1)
                    for f in range(KF):
                        last = run(slot_hT[:, j % 2, f, :], PS[:, 2 + f // 4, (f % 4) * P:(f % 4 + 1) * P], ACT.Gelu,
                                   bias=slot_b1[:, j % 2, f:f + 1])
                    last.then_inc(slot_gelu, 1)

                evacuate(0)
                evacuate(1)
                for i in range(1, NSLOT + 1):
                    if i + 1 < NSLOT:
                        evacuate(i + 1)
                    gelu(i - 1)

            act.wait_ge(load, 16 * 10)
            act.wait_ge(ctx_turned, 1)
            run(ctxT[:, :, :], PS[:, 7, 0:D].rearrange("p (k c) -> p k c", k=KD), ACT.Copy).then_inc(ctx_ready, 1)
            for a in range(2):
                run(ctxT2[:, :, :, a, :], PS[:, 7, 0:D].rearrange("p (k b c) -> p k b c", k=KD, b=B), ACT.Copy)\
                    .then_inc(ctx_ready, 1)
            act.wait_ge(const, 1)
            keys(0)
            evacuate_norm(0)
            cross(0)
            evacuate_norm(1, G1, B1)
            self_attention()
            evacuate_norm(2, G2, B2)
            act.wait_ge(load2, LOAD2)
            route(0)
            dense_expert()
            routed_experts()
            turned_weights(0)
            keys(1)
            evacuate_norm(3)
            cross(1)
            evacuate_norm(4)
            route(1)
            last_experts()

        @block.vector
        def _(dve):
            v = nc.vector

            def statistics(n, src, t):
                v.bn_stats(stats[:, t, :], src[:, t, :]).then_inc(LN[n].stats, 1)

            def split_input(tb):
                t = slice(tb * 512, (tb + 1) * 512)
                dve.wait_ge(LN[4].xt_ready, 4 * tb + 4)
                v.tensor_copy(x_high[:, :, t], xT[:, :, t]).then_inc(x_split, 1)
                dve.wait_ge(x_split, 2 * tb + 1)
                v.tensor_tensor(x_low[:, :, t], xT[:, :, t], x_high[:, :, t].bitcast(F32), ALU.subtract)\
                    .then_inc(x_split, 1)

            def norm(n, src):
                s = LN[n]
                buf = xn_self if n == 1 else xn
                dve.wait_ge(s.stats, NT)
                for t in range(NT):
                    v.bn_aggr(mv[:, t, :], stats[:, t, :]).then_inc(s.stats, 1)
                dve.wait_ge(s.std, 1)
                v.reciprocal(rstd[:, :], std[:, :]).then_inc(s.rstd, 1)
                dve.wait_ge(s.rstd, 1)
                scale = rstd
                if n == 1:
                    v.tensor_tensor(vtmp[:, :], mv[:, :, 1], rstd[:, :], ALU.mult).then_inc(s.rstd, 1)
                    dve.wait_ge(s.rstd, 2)
                    v.tensor_tensor(vtmp[:, :], vtmp[:, :], rstd[:, :], ALU.mult).then_inc(s.rstd, 1)
                    dve.wait_ge(s.std, 2)
                    v.reciprocal(rstd2[:, :], std[:, :]).then_inc(s.rstd, 1)
                    dve.wait_ge(s.rstd, 4)
                    v.tensor_tensor(rstd2[:, :], rstd2[:, :], rstd[:, :], ALU.mult).then_inc(s.rstd, 1)
                    dve.wait_ge(s.rstd, 5)
                    scale = rstd2
                for t in range(NT):
                    if t >= 4:
                        dve.wait_ge(s.turned, t - 3)
                    v.tensor_scalar(buf[:, t % 4, :], src[:, t, :], mv[:, t, 0:1], scale[:, t:t + 1],
                                    ALU.subtract, ALU.mult).then_inc(s.normed, 1)
                    if n == 4 and t % 4 == 3 and t > 4:
                        split_input(t // 4 - 1)
                if n == 4:
                    split_input(NBLK - 1)

            def cut_weights(e, par, piece):
                whole, high, low = piece_of(e, par, piece)
                v.tensor_copy(high, whole).then_inc(w_split[par], 1)

            def rest_of_weights(e, par, piece):
                whole, high, low = piece_of(e, par, piece)
                v.tensor_tensor(low, whole, high.bitcast(F32), ALU.subtract).then_inc(w_split[par], 1)

            def cross(n):
                s = X[n]
                bv = (BV0, BV1)[n]
                dve.wait_ge(s.kv_psum, 2)
                v.tensor_tensor(vb, PS[:, 5, :].rearrange("p (b d) -> p b d", b=B),
                                rows[:, bv, :].unsqueeze(1).broadcast_to([P, B, D]), ALU.add).then_inc(s.v_biased, 1)

                def shift(t):
                    dve.wait_ge(s.s_ready, t + 1)
                    sc = PS[:, 2 * (t % 2):2 * (t % 2) + 2, :].rearrange("p m (h c) -> p (m h) c", c=CTX)
                    v.tensor_reduce(mx[:, t % 3, :], sc, AX_X, ALU.max).then_inc(s.max_ready, 1)
                    dve.wait_ge(s.max_ready, t + 1)
                    if t >= 3:
                        dve.wait_ge(s.pt_psum, t - 2)
                    v.tensor_tensor(pbuf[:, t % 3, :].rearrange("p (h c) -> p h c", h=H), sc,
                                    mx[:, t % 3, :].unsqueeze(2).broadcast_to([P, H, CTX]), ALU.subtract)\
                        .then_inc(s.s_shifted, 1)

                def normalise(blk, m):
                    i = KD * blk + m
                    dve.wait_ge(s.av_ready, i + 1)
                    values = sum_banks(blk, m)
                    v.reciprocal(rden[:, m, :], PS[:, values + 1, :]).then_inc(s.recip_ready, 1)
                    dve.wait_ge(s.recip_ready, i + 1)
                    v.tensor_tensor(aT[:, blk % 2, m, :], PS[:, values, :], rden[:, m, :], ALU.mult)\
                        .then_inc(s.at_ready, 1)

                def add(blk, c):
                    tt = 4 * blk + 2 * c
                    dve.wait_ge(s.x_biased, 1)
                    dve.wait_ge(s.wo_ready, 2 * blk + c + 1)
                    v.tensor_tensor(x[:, tt:tt + 2, :], x[:, tt:tt + 2, :],
                                    PS[:, 6 + c, :].rearrange("p (t d) -> p t d", t=2), ALU.add)\
                        .then_inc(s.x_done, 2)
                    if tt:
                        two_statistics(tt - 2)

                def two_statistics(tt):
                    dve.wait_ge(s.x_done, tt + 2)
                    for t in range(tt, tt + 2):
                        statistics((1, 4)[n], x, t)

                shift(0)
                for t in range(NT + 4):
                    blk, sub = divmod(t, 4)
                    if t + 1 < NT:
                        shift(t + 1)
                    if blk >= 1:
                        if sub < 2:
                            normalise(blk - 1, sub)
                        else:
                            add(blk - 1, sub - 2)
                two_statistics(NT - 2)

            def self_attention():
                def rest(i):
                    w, m, blk = qk_tile(i)
                    dve.wait_ge(high_ready, i + 1)
                    if i >= 2:
                        dve.wait_ge(mid_ready, i - 1)
                        dve.wait_ge(low_ready, i - 1)
                    v.scalar_tensor_tensor(out=rres[:, i % 2, :], in0=PS[:, 4 + i % 4, :],
                                           scalar=cols[:, (BQS, BKS)[w], m:m + 1],
                                           in1=split[w][:, 0, m, blk * 512:(blk + 1) * 512],
                                           op0=ALU.add, op1=ALU.subtract).then_inc(rest_ready, 1)

                def low(i):
                    w, m, blk = qk_tile(i)
                    dve.wait_ge(mid_ready, i + 1)
                    v.tensor_tensor(split[w][:, 2, m, blk * 512:(blk + 1) * 512], rres[:, i % 2, :],
                                    split[w][:, 1, m, blk * 512:(blk + 1) * 512], ALU.subtract).then_inc(low_ready, 1)

                n = QK_TILES
                for i in range(n):
                    rest(i)
                    if i >= 1:
                        low(i - 1)
                low(n - 1)

                def values(t):
                    dve.wait_ge(vs_psum, t + 1)
                    v.tensor_tensor(vones[:, t, :, :].rearrange("p h (a c) -> p h a c", a=3)[:, :, 0::2, :],
                                    PS[:, t % 3, 0:D].rearrange("p (h a c) -> p h a c", h=8, a=2),
                                    rows[:, BVS, :].rearrange("p (h a c) -> p h a c", h=8, a=2), ALU.add)\
                        .then_inc(vs_ready, 1)

                def maximum(job, u, i):
                    if i == 0 and u >= 2:
                        dve.wait_ge(max_joined, u - 1)
                    v.tensor_reduce(mpart[:, u % 2, i // 2, i % 2:i % 2 + 1], PS[:, RING + job % 3, :], AX_X, ALU.max)\
                        .then_inc(ring_free, 1)
                    if i == 63:
                        dve.wait_ge(ring_free, job + 1)
                        v.tensor_tensor(mrow, mpart[:, u % 2, :, 0], mpart[:, u % 2, :, 1], ALU.max)\
                            .then_inc(max_joined, 1)

                def split_maxima(job, u):
                    if u >= 1:
                        dve.wait_ge(mrow_landed, 48 * u)
                    ps = PS[0:32, RING + job % 3, 0:P]
                    v.tensor_scalar(msplit[0:32, 0, :], ps, -1.0, None, ALU.mult).then_inc(msplit_tmp, 1)
                    dve.wait_ge(msplit_tmp, 2 * u + 1)
                    v.scalar_tensor_tensor(out=mres[0:32, :], in0=ps, scalar=-1.0, in1=msplit[0:32, 0, :],
                                           op0=ALU.mult, op1=ALU.subtract).then_inc(ring_free, 1)
                    dve.wait_ge(ring_free, job + 1)
                    v.tensor_copy(msplit[0:32, 1, :], mres[0:32, :]).then_inc(msplit_tmp, 1)
                    dve.wait_ge(msplit_tmp, 2 * u + 2)
                    v.tensor_tensor(msplit[0:32, 2, :], mres[0:32, :], msplit[0:32, 1, :], ALU.subtract)\
                        .then_inc(msplit_ready, 1)

                def output(job, u, half):
                    b, g = divmod(u, NG)
                    o = PS[:, RING + job % 3, :].rearrange("p (c h a d) -> p c h a d", c=4, h=2, a=4)
                    r = rsum[:, half, :].rearrange("p (c h a) -> p c h a", c=4, h=2)
                    v.reciprocal(r, o[:, :, :, 1:3, 0]).then_inc(rsum_ready, 1)
                    dve.wait_ge(rsum_ready, 2 * u + half + 1)
                    t0 = b * QT + 4 * half
                    for pair in range(2):
                        c = 64 * g + 32 * pair
                        last = v.tensor_tensor(
                            attn[:, t0:t0 + 4, c:c + 32].rearrange("p c (a d) -> p c a d", a=2),
                            o[:, :, pair, 0::3, :], r[:, :, pair, :].unsqueeze(3).broadcast_to([P, 4, 2, DH]),
                            ALU.mult)
                    last.then_inc(ring_free, 1)

                job = 0
                for n in STEPS:
                    if n >= 32 and n % 32 == 4:
                        dve.wait_ge(av_done, QT * (n // 32))
                        v.tensor_copy(oT[:, 0:512], PS[:, 6, :]).then_inc(o_copied, 1)
                    if v_tile(n - 1) is not None:
                        values(v_tile(n - 1))
                    for kind, u, i in ring_jobs(n):
                        dve.wait_ge(ring_full, job + 1)
                        if kind == "scores":
                            maximum(job, u, i)
                        elif kind == "maxima":
                            split_maxima(job, u)
                        else:
                            output(job, u, i)
                        job += 1
                assert job == JOBS
                for t in range(NT):
                    v.tensor_scalar(x2[:, t, :], x[:, t, :], mv[:, t, 0:1], rstd[:, t:t + 1],
                                    ALU.subtract, ALU.mult).then_inc(y_ready, 1)
                for t in range(NT):
                    if t % 4 == 0:
                        dve.wait_ge(y_biased, t // 4 + 1)
                    dve.wait_ge(so_psum, t + 1)
                    v.tensor_tensor(x2[:, t, :], x2[:, t, :], PS[:, 4 + t % 4, 0:D], ALU.add).then_inc(x2_ready, 1)
                    if t:
                        dve.wait_ge(x2_ready, t)
                        statistics(2, x2, t - 1)
                dve.wait_ge(x2_ready, NT)
                statistics(2, x2, NT - 1)

            def route_experts():
                n = [0]

                def link(ins):
                    n[0] += 1
                    ins.then_inc(r_step, 1)
                    dve.wait_ge(r_step, n[0])

                def wide(a, c=E0):
                    return a[:, 0:NT * c].rearrange("p (t e) -> p t e", t=NT)

                def over(a, c=E0):
                    return a.unsqueeze(2).broadcast_to([P, NT, c])

                dve.wait_ge(r_psum, 1)
                L = PS[:, 4, 0:NT * (E0 + 2)].rearrange("p (t e) -> p t e", t=NT)
                top = rt[0][:, 0:NT]
                link(v.tensor_reduce(top, L[:, :, 0:E0], AX_X, ALU.max))
                link(v.tensor_tensor(wide(rt[1]), L[:, :, 0:E0], over(top), ALU.subtract))
                link(v.tensor_tensor(wide(rt[5], 2), L[:, :, E0:E0 + 2],
                                     coef_b[:, :].unsqueeze(1).broadcast_to([P, NT, 2]), ALU.add))
                link(v.tensor_reduce(rt[0][:, NT:2 * NT], wide(rt[5], 2), AX_X, ALU.max))
                link(v.tensor_tensor(wide(rt[3], 2), wide(rt[5], 2), over(rt[0][:, NT:2 * NT], 2), ALU.subtract))
                link(v.tensor_scalar(rt[6], rt[1], 0.0, None, ALU.is_ge))
                link(v.tensor_tensor(wide(rt[6]), wide(rt[6]), first8[:, :].unsqueeze(1).broadcast_to([P, NT, E0]),
                                     ALU.mult))
                link(v.tensor_reduce(rt[0][:, 2 * NT:3 * NT], wide(rt[6]), AX_X, ALU.max))
                link(v.tensor_tensor(wide(rt[7]), wide(rt[6]), over(rt[0][:, 2 * NT:3 * NT]), ALU.is_equal))
                dve.wait_ge(r_exp, 2)
                link(v.tensor_reduce(rt[0][:, 3 * NT:4 * NT], wide(rt[2]), AX_X, ALU.add))
                link(v.reciprocal(rt[0][:, 4 * NT:5 * NT], rt[0][:, 3 * NT:4 * NT]))
                link(v.tensor_reduce(rt[0][:, 5 * NT:6 * NT], wide(rt[4], 2), AX_X, ALU.add))
                link(v.reciprocal(rt[0][:, 6 * NT:7 * NT], rt[0][:, 5 * NT:6 * NT]))
                link(v.tensor_tensor(wide(rt[5], 2), wide(rt[4], 2), over(rt[0][:, 6 * NT:7 * NT], 2), ALU.mult))
                link(v.tensor_tensor(rt[0][:, 7 * NT:8 * NT], rt[0][:, 4 * NT:5 * NT], wide(rt[5], 2)[:, :, 0], ALU.mult))
                link(v.tensor_copy(c0[:, :, E0], wide(rt[5], 2)[:, :, 1]))
                v.tensor_tensor(c0[:, :, 0:E0], wide(rt[7]), over(rt[0][:, 7 * NT:8 * NT]), ALU.mult)\
                    .then_inc(c_ready, 1)
                dve.wait_ge(c_ready, 1)

            def route_steps():
                n = [0]

                def link(ins):
                    n[0] += 1
                    ins.then_inc(r_step1, 1)
                    dve.wait_ge(r_step1, n[0])

                dve.wait_ge(r_psum, 3)
                link(v.tensor_scalar(rt[0][:, 0:NT], PS[:, 4, 0:NT], bu[:, 0:1], None, ALU.add))
                dve.wait_ge(r_exp, 3)
                link(v.tensor_scalar(rt[2][:, 0:NT], rt[1][:, 0:NT], 1.0, None, ALU.add))
                link(v.reciprocal(rt[3][:, 0:NT], rt[2][:, 0:NT]))
                link(v.tensor_scalar(rt[4][:, 0:NT], rt[3][:, 0:NT], float(E1), None, ALU.mult))

                def tokens(a):
                    return a[:, 0:NT].unsqueeze(2).broadcast_to([P, NT, E1])

                def steps(a):
                    return a[:, :].unsqueeze(1).broadcast_to([P, NT, E1])

                w = rt[5][:, 0:NT * E1].rearrange("p (t e) -> p t e", t=NT)
                on = rt[6][:, 0:NT * E1].rearrange("p (t e) -> p t e", t=NT)
                link(v.tensor_tensor(w, tokens(rt[3]), steps(step_inv), ALU.mult))
                link(v.tensor_tensor(on, tokens(rt[4]), steps(step_thr), ALU.is_gt))
                v.tensor_tensor(c1[:, :, :], w, on, ALU.mult).then_inc(c_ready, 1)
                dve.wait_ge(c_ready, 2)

            def place_tokens():
                n = [0]

                def link(ins):
                    n[0] += 1
                    ins.then_inc(place_step, 1)
                    dve.wait_ge(place_step, n[0])

                def by_tile(a):
                    return a.rearrange("p (t e) -> p t e", t=NT)

                dve.wait_ge(r_psum, 2)
                rank, total, hot = by_tile(PS[:, 7, 0:P]), by_tile(PS[:, 7, P:2 * P]), by_tile(rt[7])
                link(v.tensor_copy(grow[:, 0], total))
                a = 0
                for far in (1, 2, 4, 8):
                    link(v.tensor_tensor(grow[:, 1 - a, far:, :], grow[:, a, far:, :], grow[:, a, :NT - far, :], ALU.add))
                    link(v.tensor_copy(grow[:, 1 - a, :far, :], grow[:, a, :far, :]))
                    a = 1 - a
                link(v.tensor_tensor(grow[:, 1], grow[:, 0], total, ALU.subtract))
                count = grow[:, 0, NT - 1, :]
                need = fits[:, 0:E0 * NT].rearrange("p (e i) -> p e i", e=E0)
                link(v.tensor_tensor(need, count.unsqueeze(2).broadcast_to([P, E0, NT]),
                                     tile_edges[:, :].unsqueeze(1).broadcast_to([P, E0, NT]), ALU.is_gt))
                link(v.tensor_reduce(sizes[:, 0, :], need, AX_X, ALU.add))
                for m, far in enumerate((1, 2, 4)):
                    link(v.tensor_tensor(sizes[:, m + 1, far:], sizes[:, m, far:], sizes[:, m, :E0 - far], ALU.add))
                    link(v.tensor_copy(sizes[:, m + 1, :far], sizes[:, m, :far]))
                ends = sizes[:, 3, :]
                link(v.tensor_tensor(sizes[:, 4, :], ends, sizes[:, 0, :], ALU.subtract))
                link(v.scalar_tensor_tensor(out=grow[:, 0], in0=sizes[:, 4, :].unsqueeze(1).broadcast_to([P, NT, E0]),
                                            scalar=float(P), in1=grow[:, 1], op0=ALU.mult, op1=ALU.add))
                link(v.tensor_tensor(grow[:, 1], grow[:, 0], rank, ALU.add))
                link(v.tensor_tensor(grow[:, 0], grow[:, 1], hot, ALU.mult))
                link(v.tensor_reduce(posf[:, :], grow[:, 0], AX_X, ALU.add))
                over = fits[:, :].rearrange("p (j e) -> p j e", j=NSLOT)
                link(v.tensor_tensor(over, ends.unsqueeze(1).broadcast_to([P, NSLOT, E0]),
                                     slot_index[:, :].unsqueeze(2).broadcast_to([P, NSLOT, E0]), ALU.is_le))
                link(v.tensor_reduce(eidf[:, :], over, AX_X, ALU.add))
                link(v.tensor_scalar(expert_of[:, :], eidf[:, :], float(E0 - 1), None, ALU.min))
                link(v.tensor_copy(slot_of[:, :], posf[:, :]))
                assert n[0] == PLACED, n[0]

            def dense_combine():
                s = F[0]
                for t in range(NT):
                    dve.wait_ge(s.o_psum, PAR_O + t + 1)
                    v.scalar_tensor_tensor(out=x[:, t, :], in0=PS[:, 4 + t % 2, 0:D], scalar=c0[:, t, E0:E0 + 1],
                                           in1=x[:, t, :], op0=ALU.mult, op1=ALU.add).then_inc(s.o_free, 1)
                dve.wait_ge(s.o_free, PAR_O + NT)

            def routed_experts():
                def hidden(j, par):
                    if not isinstance(j, int) or j >= 2:
                        dve.wait_ge(slot_ht_psum, j - 1)
                        dve.wait_ge(slot_gelu, j)
                    e = nc.vector.value_load(expert_of[0:1, bass.ds(j, 1)], min_val=0, max_val=E0 - 1)
                    v.tensor_copy(slot_b1[:, par, :], b1_0[:, bass.ds(e, 1), :].rearrange("p a f -> p (a f)"))\
                        .then_inc(slot_b1_ready, 1)
                    dve.wait_ge(slot_h_psum, j + 1)
                    v.tensor_copy(slot_h[:, par, :], PS[:, 0:2, :].rearrange("p a f -> p (a f)"))\
                        .then_inc(slot_h_copied, 1)

                def output(j, par):
                    if not isinstance(j, int) or j >= 2:
                        dve.wait_ge(slot_stored[par], 8 * (j - par))
                    dve.wait_ge(slot_y_psum, j + 1)
                    v.tensor_copy(slot_y[:, par, :], PS[:, 4 + par, 0:D]).then_inc(slot_y_copied, 1)

                hidden(0, 0)
                hidden(1, 1)
                hidden(2, 0)
                output(0, 0)
                hidden(3, 1)
                output(1, 1)
                with dve.Fori(0, (NSLOT - 5) // 2) as pair:
                    hidden(pair * 2 + 4, 0)
                    output(pair * 2 + 2, 0)
                    hidden(pair * 2 + 5, 1)
                    output(pair * 2 + 3, 1)
                hidden(NSLOT - 1, 0)
                for j in range(NSLOT - 3, NSLOT):
                    output(j, j % 2)

            def routed_combine(c):
                dve.wait_ge(gathered[c], 64)
                for t in range(4 * c, 4 * c + 4):
                    v.scalar_tensor_tensor(out=x[:, t, :], in0=gathered_y[:, t, :],
                                           scalar=rt[0][:, 7 * NT + t:7 * NT + t + 1], in1=x[:, t, :],
                                           op0=ALU.mult, op1=ALU.add).then_inc(routed_done, 1)
                for t in range(4 * c, 4 * c + 4):
                    dve.wait_ge(routed_done, t + 1)
                    statistics(3, x, t)

            def second_biases(n, quarters=range(4)):
                for t in range(4 * quarters[0], 4 * quarters[-1] + 4):
                    dve.wait_ge(F[n].ct_psum, t + 2)
                    v.tensor_tensor(x[:, t, :], x[:, t, :], PS[:, 4 + t % 4, 0:D], ALU.add).then_inc(F[n].b2_done, 1)
                dve.wait_ge(F[n].b2_done, 4 * quarters[-1] + 4)

            def last_experts():
                s = F[1]

                def combine(e, t):
                    dve.wait_ge(s.o_psum, PAR_O + 16 * e + t + 1)
                    dve.wait_ge(s.o_free, PAR_O - 15 + 16 * e + t)
                    v.scalar_tensor_tensor(out=x[:, t, :], in0=PS[:, 4 + t % 4, 0:D],
                                           scalar=c1[:, t, bass.ds(e, 1)], in1=x[:, t, :],
                                           op0=ALU.mult, op1=ALU.add).then_inc(s.o_free, 1)

                def one(e, par, more=True):
                    for i in range(NBLK * KF):
                        if i >= KF and i % KF == 2:
                            for sub in range(4):
                                combine(e, 4 * (i // KF - 1) + sub)
                        dve.wait_ge(s.h_done, H_FREE + 32 * e + i + 1)
                        if i >= NRING:
                            block, chunk = divmod(i - NRING, KF)
                            if chunk == KF - 1:
                                dve.wait_ge(s.o_psum, PAR_O + 16 * e + 4 * (block + 1))
                            else:
                                dve.wait_ge(h_used, (KF - 1) * (NBLK * e + block) + chunk + 1)
                        v.tensor_copy(h_high[:, i % NRING, :], h_raw[:, i % NRAW, :]).then_inc(h_cut, 1)
                        piece, step = divmod(i - 12, 2)
                        if more and piece >= 0 and piece < PIECES:
                            if step == 0:
                                if piece == 0:
                                    dve.wait_ge((s.weights1, s.weights0)[par], 32 * (e - par) + (64, 128)[par])
                                cut_weights(1, 1 - par, piece)
                            else:
                                dve.wait_ge(w_split[1 - par], PIECES * (e - par + 2 * par) + 2 * piece + 1)
                                rest_of_weights(1, 1 - par, piece)
                        dve.wait_ge(h_cut, 32 * e + i + 1)
                        v.tensor_tensor(h_low[:, i % NRING, :], h_raw[:, i % NRAW, :],
                                        h_high[:, i % NRING, :].bitcast(F32), ALU.subtract).then_inc(h_split, 1)
                    for sub in range(4):
                        combine(e, NT - 4 + sub)

                with dve.Fori(0, E1 // 2 - 1) as pair:
                    one(pair * 2, 0)
                    one(pair * 2 + 1, 1)
                second_biases(1)
                one(E1 - 2, 0)
                one(E1 - 1, 1, more=False)

            for c in range(4):
                dve.wait_ge(x_loaded[c], 16)
                for t in range(4 * c, 4 * c + 4):
                    statistics(0, x, t)
            norm(0, x)
            dve.wait_ge(load, 16 * 10)
            cross(0)
            norm(1, x)
            self_attention()
            norm(2, x2)
            dve.wait_ge(load2, LOAD2)
            route_experts()
            dve.wait_ge(x_joined, 1)
            for t in range(NT):
                v.tensor_scalar(x2[:, t, :], x2[:, t, :], mv[:, t, 0:1], rstd[:, t:t + 1],
                                ALU.subtract, ALU.mult).then_inc(y_ready, 1)
            place_tokens()
            dense_combine()
            routed_experts()
            for c in range(4):
                second_biases(0, range(c, c + 1))
                routed_combine(c)
            norm(3, x)
            cross(1)
            norm(4, x)
            dve.wait_ge(w_split[0], 2 * PIECES)
            route_steps()
            last_experts()

        @block.gpsimd
        def _(pool):
            g = nc.gpsimd
            g.memset(eps[:, :], EPS).then_inc(const, 1)
            pool.wait_ge(const, 1)
            g.memset(zeros[:, :], 0.0).then_inc(zeros_ready, 1)
            pool.wait_ge(zeros_ready, 1)
            g.memset(ones[:, :], 1.0).then_inc(zeros_ready, 1)
            g.memset(credit[:, 6:7], 0.0).then_inc(slot_h_copied, 1)
            g.memset(credit[:, 7:8], 0.0).then_inc(slot_gelu, 1)
            g.memset(credit[:, 8:9], 0.0).then_inc(slot_y_copied, 2)
            for n in range(2):
                g.memset(credit[:, 3 * n:3 * n + 1], 0.0).then_inc(F[n].h_done, H_FREE)
                g.memset(credit[:, 3 * n + 1:3 * n + 2], 0.0).then_inc(F[n].o_psum, PAR_O)
                g.memset(credit[:, 3 * n + 2:3 * n + 3], 0.0).then_inc(F[n].o_free, PAR_O)

            def bias(n, row):
                pool.wait_ge(LN[3 * n].normed, NT)
                pool.wait_ge(load, 16 * 10)
                g.tensor_tensor(x[:, :, :], x[:, :, :], rows[:, row, :].unsqueeze(1).broadcast_to([P, NT, D]), ALU.add)\
                    .then_inc(X[n].x_biased, 1)

            def spread(n):
                s = X[n]
                pool.wait_ge(s.k_ready, 1)
                for b in range(B):
                    for m in range(KD):
                        g.tensor_tensor(kbd[:, b, m, :].rearrange("p (h c) -> p h c", h=8),
                                        kT[:, m, b * CTX:(b + 1) * CTX].unsqueeze(1).broadcast_to([P, 8, CTX]),
                                        head_mask[:, :].unsqueeze(2).broadcast_to([P, 8, CTX]), ALU.mult)\
                            .then_inc(s.kv_spread, 1)
                pool.wait_ge(s.v_biased, 1)
                for b in range(B):
                    g.tensor_tensor(vbd[:, b, :, :], vb[:, b, :].rearrange("p (h c) -> p h c", h=8),
                                    pair_mask[:, :].unsqueeze(1).broadcast_to([P, 8, 32]), ALU.mult)\
                        .then_inc(s.kv_spread, 1)

            pool.wait_ge(load, 16 * 10)
            spread(0)
            bias(0, BO0)
            pool.wait_ge(X[0].x_done, NT)
            g.memset(vones[:, :, :, 16:32], 1.0).then_inc(ones_ready, 1)
            for n in range(NSTK):
                pool.wait_ge(ones_ready, n + 1)
                g.memset(kstk[n][KS:KM, :, :], 1.0).then_inc(ones_ready, 1)
            for c in range(4):
                pool.wait_ge(y_ready, 4 * c + 4)
                g.tensor_tensor(x2[:, 4 * c:4 * c + 4, :], x2[:, 4 * c:4 * c + 4, :],
                                rows[:, BOS, :].unsqueeze(1).broadcast_to([P, 4, D]), ALU.add).then_inc(y_biased, 1)
            pool.wait_ge(x2_ready, NT)
            g.tensor_tensor(x[:, :, :], x[:, :, :], x2, ALU.add).then_inc(x_joined, 1)
            pool.wait_ge(slots_zeroed, 16)
            pool.wait_ge(y_ready, 2 * NT)
            pool.wait_ge(place_step, PLACED)
            for t in range(NT):
                g.indirect_dma_start(slots_in, bass.IndirectOffsetOnAxis(ap=slot_of[:, t:t + 1], axis=0),
                                     x2[:, t, :], None).then_inc(scattered, 16)
            pool.wait_ge(slot_y_psum, NSLOT)
            pool.wait_ge(slot_stored[0], 16 * (NSLOT + 1) // 2)
            pool.wait_ge(slot_stored[1], 16 * (NSLOT // 2))
            for t in range(NT):
                g.indirect_dma_start(gathered_y[:, t, :], None, slots_out,
                                     bass.IndirectOffsetOnAxis(ap=slot_of[:, t:t + 1], axis=0))\
                    .then_inc(gathered[t // 4], 16)
            spread(1)
            bias(1, BO1)
            pool.wait_ge(F[1].weights0, 64)
            for piece in range(PIECES):
                whole, high, low = piece_of(0, 0, piece)
                g.tensor_copy(high, whole).then_inc(w_split[0], 1)
            for piece in range(PIECES):
                whole, high, low = piece_of(0, 0, piece)
                pool.wait_ge(w_split[0], piece + 1)
                g.tensor_tensor(low, whole, high.bitcast(F32), ALU.subtract).then_inc(w_split[0], 1)


def lay_out(i):
    import numpy as np

    f = {k: np.ascontiguousarray(v) for k, v in i.items()}
    col = lambda a: a.reshape(KD, P).T
    p = np.arange(P)
    step = (np.arange(E1)[None, :] - p[:, None]) % E1
    cols = ["L0_xattn_bq", "L0_xattn_bk", None, None, "L1_xattn_bq", "L1_xattn_bk", "L0_ffn_ln1_g", "L0_ffn_ln1_b",
            "L0_ffn_ln2_g", "L0_ffn_ln2_b"]
    bqkv = f["L0_ffn_bqkv"]
    a = {
        "x": f["x"].reshape(T, D), "ctx": f["ctx_1024"].reshape(B * CTX, D),
        "ident": np.eye(P, dtype=np.float32),
        "head_mask": (p[:, None] // 16 == np.arange(8)[None, :]).astype(np.float32),
        "pair_mask": (p[:, None] // 64 == np.arange(32)[None, :] // 16).astype(np.float32),
        "cols": np.stack([col(f[n]) if n else col(bqkv[(k - 2) * D:(k - 1) * D]) for k, n in enumerate(cols)], axis=1),
        "rows": np.stack([f["L0_xattn_bv"], f["L0_xattn_bo"], bqkv[2 * D:], f["L0_ffn_bo"], f["L1_xattn_bv"],
                          f["L1_xattn_bo"]]),
        "Wqkv": f["L0_ffn_Wqkv"], "WoS": f["L0_ffn_Wo"],
        "w_route": np.concatenate([f["L0_ffn_gate_w"], f["L0_ffn_coef_w"]], axis=1),
        "w_u": col(f["L1_ffn_Wu"]), "coef_b": f["L0_ffn_coef_b"], "bu": f["L1_ffn_bu"],
        "b1_0": np.concatenate([f["L0_ffn_b1"], f["L0_ffn_rb1"][None]]).reshape(E0R, KF, P).transpose(2, 0, 1),
        "b1_1": f["L1_ffn_b1"].reshape(E1, KF, P).transpose(2, 0, 1),
        "b2_0": np.concatenate([f["L0_ffn_b2"], f["L0_ffn_rb2"][None]]), "b2_1": f["L1_ffn_b2"],
        "W1_0": np.concatenate([f["L0_ffn_W1"], f["L0_ffn_rW1"][None]]),
        "W2_0": np.concatenate([f["L0_ffn_W2"], f["L0_ffn_rW2"][None]]),
        "W1_1": f["L1_ffn_W1"], "W2_1": f["L1_ffn_W2"],
        "step_inv": (1.0 / (step + 1)).astype(np.float32),
        "step_thr": np.where(step == 0, -1, step).astype(np.float32),
        "before": (p[:, None] < p[None, :]).astype(np.float32),
        "tile_edges": np.broadcast_to(P * np.arange(NT, dtype=np.float32), (P, NT)),
        "slot_index": np.broadcast_to(np.arange(NSLOT, dtype=np.float32), (P, NSLOT)),
        "first8": np.broadcast_to(E0 - np.arange(E0, dtype=np.float32), (P, E0)),
    }
    for w in "qkvo":
        a[f"W{w}0"] = f[f"L0_xattn_W{w}"]
        a[f"W{w}1"] = f[f"L1_xattn_W{w}"].T
    return {k: np.ascontiguousarray(v) for k, v in a.items()}


def kernel(**inputs):
    import concourse.bacc as _bacc
    from concourse import mybir as _mybir
    from concourse.bass_utils import run_bass_kernel_spmd as _run

    nc = _bacc.Bacc("TRN2", target_bir_lowering=False, num_devices=1)
    laid = lay_out(inputs)
    arrays = {f"in_{k}": v for k, v in laid.items()}
    aps = {k: nc.dram_tensor(f"in_{k}", v.shape, _mybir.dt.from_np(v.dtype), kind="ExternalInput").ap()
           for k, v in laid.items()}
    out = nc.dram_tensor("out_x", (T, D), F32, kind="ExternalOutput").ap()
    block_kernel(nc, aps, out)
    r = _run(nc, [arrays], core_ids=[0])
    return r.results[0]["out_x"].reshape(B, S, D)
```
